# Optimizing a Trainium2 kernel written in Bass

```python
import numpy as np
import jax
import jax.numpy as jnp

def _softmax(x, axis=-1):
    return jax.nn.softmax(x, axis=axis)

def _gelu(x):
    return jax.nn.gelu(x, approximate=True)

def _silu(x):
    return jax.nn.silu(x)

def _sigmoid(x):
    return jax.nn.sigmoid(x)

def _layernorm(x, axis=-1, eps=1e-05):
    m = jnp.mean(x, axis=axis, keepdims=True)
    v = jnp.var(x, axis=axis, keepdims=True)
    return (x - m) / jnp.sqrt(v + eps)

def _scatter_add(tgt, idx, src, axis=0):
    return tgt.at[idx].add(src)

def _segment_sum(src, seg, n):
    return jax.ops.segment_sum(src, seg, n)
kernel_name = 'mk_sandwich_d2_jaxref_r8_eab23b'

def setup_inputs(seed: int=0):
    np.random.seed(seed)
    _w = jnp.asarray

    def _L0_attn_setup():
        import jax, jax.numpy as jnp
        import numpy as np
        import math
        B, T, C = (2, 256, 128)
        H, L = (16, 64)
        DH = C // H
        DHE = DH // 2
        THETA = 10000.0

        def _rope_cache(t, dim):
            inv_freq = 1.0 / THETA ** (jnp.arange(0, dim, 2, dtype=jnp.float32) / dim)
            freqs = jnp.arange(t, dtype=jnp.float32)[:, None] * inv_freq[None, :]
            emb = jnp.concatenate((freqs, freqs), axis=-1)
            return (jnp.cos(emb), jnp.sin(emb))

        def _apply_rope(x, cos, sin):
            x1 = x[..., 0::2]
            x2 = x[..., 1::2]
            rot = jnp.stack((-x2, x1), axis=-1).reshape(x.shape)
            return x * cos[None, None] + rot * sin[None, None]
        key = jax.random.key(seed)
        ks = jax.random.split(key, 10)
        s = 0.02
        return {'x': jax.random.normal(ks[0], (B, T, C), jnp.float32), 'Wq_down': jax.random.normal(ks[1], (C, H * L), jnp.float32) * s, 'Wk_down': jax.random.normal(ks[2], (C, H * L), jnp.float32) * s, 'Wv_down': jax.random.normal(ks[3], (C, H * L), jnp.float32) * s, 'Wq_up_c': jax.random.normal(ks[4], (L, DHE), jnp.float32) * s, 'Wq_up_e': jax.random.normal(ks[5], (L, DHE), jnp.float32) * s, 'Wk_up_c': jax.random.normal(ks[6], (L, DHE), jnp.float32) * s, 'Wk_up_e': jax.random.normal(ks[7], (L, DHE), jnp.float32) * s, 'Wv_up': jax.random.normal(ks[8], (L, DH), jnp.float32) * s, 'Wc': jax.random.normal(ks[9], (C, C), jnp.float32) * s}
    _L0_attn_in = _L0_attn_setup()

    def _L0_ffn_setup():
        import jax, jax.numpy as jnp
        import numpy as np
        BS, SLEN, DIM = (1, 256, 128)
        NUM_EXPERTS, TOP_K = (8, 2)
        HID = 176

        def _masked_grouped_mm(x, w, onehot):
            g = jnp.einsum('tk,gnk->tgn', x, w, preferred_element_type=jnp.float32)
            return jnp.einsum('tgn,tg->tn', g, onehot)

        def moe_forward(x, gate_w, expert_bias, w_up, w_down, shared_w_up, shared_w_down):
            bs, slen, dim = x.shape
            xf = x.reshape(-1, dim)
            scores = jax.nn.sigmoid((xf @ gate_w.T).astype(jnp.float32))
            biased = scores + expert_bias
            _, sel = jax.lax.top_k(biased, TOP_K)
            top_scores = jnp.take_along_axis(scores, sel, axis=-1)
            flat_sel = sel.reshape(-1)
            counts = jnp.bincount(flat_sel, length=NUM_EXPERTS)
            order = jnp.argsort(flat_sel, stable=True)
            scores_sorted = top_scores.reshape(-1)[order]
            token_ids = order // TOP_K
            routed_in = (xf[token_ids] * scores_sorted[:, None]).astype(x.dtype)
            seg = jnp.repeat(jnp.arange(NUM_EXPERTS), counts, total_repeat_length=flat_sel.shape[0])
            onehot = jax.nn.one_hot(seg, NUM_EXPERTS, dtype=jnp.float32)
            h = _masked_grouped_mm(routed_in.astype(jnp.bfloat16), w_up.astype(jnp.bfloat16), onehot)
            h = jnp.square(jax.nn.relu(h.astype(jnp.bfloat16)))
            routed_out = _masked_grouped_mm(h.astype(jnp.bfloat16), w_down.astype(jnp.bfloat16), onehot)
            routed_out = routed_out.astype(jnp.bfloat16).astype(x.dtype)
            hs = jnp.square(jax.nn.relu(xf @ shared_w_up.T))
            shared_out = hs @ shared_w_down.T
            combined = jnp.zeros((flat_sel.shape[0], dim), routed_out.dtype).at[order].set(routed_out)
            out = combined.reshape(-1, TOP_K, dim).sum(axis=1) + shared_out
            return out.reshape(bs, slen, dim)
        key = jax.random.key(seed)
        k = jax.random.split(key, 6)
        s = 0.02
        return {'x': jax.random.normal(k[0], (BS, SLEN, DIM), jnp.float32), 'gate_w': jax.random.normal(k[1], (NUM_EXPERTS, DIM), jnp.float32) * s, 'expert_bias': jnp.zeros((NUM_EXPERTS,), jnp.float32), 'w_up': jax.random.normal(k[2], (NUM_EXPERTS, HID, DIM), jnp.float32) * s, 'w_down': jax.random.normal(k[3], (NUM_EXPERTS, DIM, HID), jnp.float32) * s, 'shared_w_up': jax.random.normal(k[4], (HID, DIM), jnp.float32) * s, 'shared_w_down': jax.random.normal(k[5], (DIM, HID), jnp.float32) * s}
    _L0_ffn_in = _L0_ffn_setup()

    def _L1_attn_setup():
        import jax, jax.numpy as jnp
        import numpy as np
        HIDDEN = 128
        HEADS = 16
        HEAD_DIM = HIDDEN // HEADS
        key = jax.random.key(seed)
        ks = jax.random.split(key, 5)
        B, S = (1, 512)
        inputs = jax.random.normal(ks[0], (B, S, HIDDEN), dtype=jnp.float32)
        lim = float(np.sqrt(6.0 / (HIDDEN + HIDDEN)))

        def w(k):
            return jax.random.uniform(k, (HIDDEN, HIDDEN), jnp.float32, -lim, lim)
        return {'inputs': inputs, 'Wq': w(ks[1]), 'bq': jnp.zeros((HIDDEN,), jnp.float32), 'Wk': w(ks[2]), 'bk': jnp.zeros((HIDDEN,), jnp.float32), 'Wv': w(ks[3]), 'bv': jnp.zeros((HIDDEN,), jnp.float32), 'Wo': w(ks[4]), 'bo': jnp.zeros((HIDDEN,), jnp.float32)}
    _L1_attn_in = _L1_attn_setup()

    def _L1_ffn_setup():
        import math
        import jax, jax.numpy as jnp
        import numpy as np
        B, T, D = (4, 512, 128)
        H = 16
        HD = D // H
        CAP = int(512 * 0.125)
        DFF = int(D * 4 * 2 / 3)
        EPS = 1e-06

        def rmsnorm(x, g):
            return x * jax.lax.rsqrt(jnp.mean(x * x, axis=-1, keepdims=True) + EPS) * g
        key = jax.random.key(seed)
        ks = jax.random.split(key, 9)
        s = lambda k, shape: jax.random.normal(k, shape, jnp.float32) * 0.02
        return {'x': jax.random.normal(ks[0], (B, T, D), jnp.float32), 'w_router': s(ks[1], (D,)), 'W_qkv': s(ks[2], (3 * D, D)), 'W_out': s(ks[3], (D, D)), 'g1': jnp.ones((D,), jnp.float32), 'g2': jnp.ones((D,), jnp.float32), 'W1': s(ks[4], (DFF, D)), 'W2': s(ks[5], (DFF, D)), 'W3': s(ks[6], (D, DFF))}
    _L1_ffn_in = _L1_ffn_setup()
    _d = {'L0_attn_x': _L0_attn_in['x'], 'L0_attn_Wq_down': _L0_attn_in['Wq_down'], 'L0_attn_Wk_down': _L0_attn_in['Wk_down'], 'L0_attn_Wv_down': _L0_attn_in['Wv_down'], 'L0_attn_Wq_up_c': _L0_attn_in['Wq_up_c'], 'L0_attn_Wq_up_e': _L0_attn_in['Wq_up_e'], 'L0_attn_Wk_up_c': _L0_attn_in['Wk_up_c'], 'L0_attn_Wk_up_e': _L0_attn_in['Wk_up_e'], 'L0_attn_Wv_up': _L0_attn_in['Wv_up'], 'L0_attn_Wc': _L0_attn_in['Wc'], 'L0_ffn_gate_w': _L0_ffn_in['gate_w'], 'L0_ffn_expert_bias': _L0_ffn_in['expert_bias'], 'L0_ffn_w_up': _L0_ffn_in['w_up'], 'L0_ffn_w_down': _L0_ffn_in['w_down'], 'L0_ffn_shared_w_up': _L0_ffn_in['shared_w_up'], 'L0_ffn_shared_w_down': _L0_ffn_in['shared_w_down'], 'L1_attn_Wq': _L1_attn_in['Wq'], 'L1_attn_bq': _L1_attn_in['bq'], 'L1_attn_Wk': _L1_attn_in['Wk'], 'L1_attn_bk': _L1_attn_in['bk'], 'L1_attn_Wv': _L1_attn_in['Wv'], 'L1_attn_bv': _L1_attn_in['bv'], 'L1_attn_Wo': _L1_attn_in['Wo'], 'L1_attn_bo': _L1_attn_in['bo'], 'L1_ffn_w_router': _L1_ffn_in['w_router'], 'L1_ffn_W_qkv': _L1_ffn_in['W_qkv'], 'L1_ffn_W_out': _L1_ffn_in['W_out'], 'L1_ffn_g1': _L1_ffn_in['g1'], 'L1_ffn_g2': _L1_ffn_in['g2'], 'L1_ffn_W1': _L1_ffn_in['W1'], 'L1_ffn_W2': _L1_ffn_in['W2'], 'L1_ffn_W3': _L1_ffn_in['W3']}
    _x0 = _d['L0_attn_x']
    _d['L0_attn_x'] = jax.random.normal(jax.random.fold_in(jax.random.key(seed), 1), (2, 1024, 128), dtype=_x0.dtype)
    del _x0
    return _d

def reference(L0_attn_x, L0_attn_Wq_down, L0_attn_Wk_down, L0_attn_Wv_down, L0_attn_Wq_up_c, L0_attn_Wq_up_e, L0_attn_Wk_up_c, L0_attn_Wk_up_e, L0_attn_Wv_up, L0_attn_Wc, L0_ffn_gate_w, L0_ffn_expert_bias, L0_ffn_w_up, L0_ffn_w_down, L0_ffn_shared_w_up, L0_ffn_shared_w_down, L1_attn_Wq, L1_attn_bq, L1_attn_Wk, L1_attn_bk, L1_attn_Wv, L1_attn_bv, L1_attn_Wo, L1_attn_bo, L1_ffn_w_router, L1_ffn_W_qkv, L1_ffn_W_out, L1_ffn_g1, L1_ffn_g2, L1_ffn_W1, L1_ffn_W2, L1_ffn_W3):

    def _L0_attn_ref(x, Wq_down, Wk_down, Wv_down, Wq_up_c, Wq_up_e, Wk_up_c, Wk_up_e, Wv_up, Wc):
        import jax, jax.numpy as jnp
        import numpy as np
        import math
        B, T, C = (2, 256, 128)
        H, L = (16, 64)
        DH = C // H
        DHE = DH // 2
        THETA = 10000.0

        def _rope_cache(t, dim):
            inv_freq = 1.0 / THETA ** (jnp.arange(0, dim, 2, dtype=jnp.float32) / dim)
            freqs = jnp.arange(t, dtype=jnp.float32)[:, None] * inv_freq[None, :]
            emb = jnp.concatenate((freqs, freqs), axis=-1)
            return (jnp.cos(emb), jnp.sin(emb))

        def _apply_rope(x, cos, sin):
            x1 = x[..., 0::2]
            x2 = x[..., 1::2]
            rot = jnp.stack((-x2, x1), axis=-1).reshape(x.shape)
            return x * cos[None, None] + rot * sin[None, None]
        b, t, c = x.shape
        q_lat = (x @ Wq_down).reshape(b, t, H, L)
        k_lat = (x @ Wk_down).reshape(b, t, H, L)
        v_lat = (x @ Wv_down).reshape(b, t, H, L)
        q_c = jnp.einsum('bthl,ld->bhtd', q_lat, Wq_up_c)
        q_e = jnp.einsum('bthl,ld->bhtd', q_lat, Wq_up_e)
        k_c = jnp.einsum('bthl,ld->bhtd', k_lat, Wk_up_c)
        k_e = jnp.einsum('bthl,ld->bhtd', k_lat, Wk_up_e)
        v = jnp.einsum('bthl,ld->bhtd', v_lat, Wv_up)
        cos, sin = _rope_cache(t, DHE)
        q = jnp.concatenate([q_c, _apply_rope(q_e, cos, sin)], axis=-1)
        k = jnp.concatenate([k_c, _apply_rope(k_e, cos, sin)], axis=-1)
        scale = 1.0 / math.sqrt(DH)
        scores = jnp.einsum('bhqd,bhkd->bhqk', q, k) * scale
        causal = jnp.tril(jnp.ones((t, t), dtype=bool))
        scores = jnp.where(causal[None, None], scores, -jnp.inf)
        att = jax.nn.softmax(scores, axis=-1)
        y = jnp.einsum('bhqk,bhkd->bhqd', att, v)
        y = y.transpose(0, 2, 1, 3).reshape(b, t, c)
        return y @ Wc

    def _L0_ffn_ref(x, gate_w, expert_bias, w_up, w_down, shared_w_up, shared_w_down):
        import jax, jax.numpy as jnp
        import numpy as np
        BS, SLEN, DIM = (1, 256, 128)
        NUM_EXPERTS, TOP_K = (8, 2)
        HID = 176

        def _masked_grouped_mm(x, w, onehot):
            g = jnp.einsum('tk,gnk->tgn', x, w, preferred_element_type=jnp.float32)
            return jnp.einsum('tgn,tg->tn', g, onehot)

        def moe_forward(x, gate_w, expert_bias, w_up, w_down, shared_w_up, shared_w_down):
            bs, slen, dim = x.shape
            xf = x.reshape(-1, dim)
            scores = jax.nn.sigmoid((xf @ gate_w.T).astype(jnp.float32))
            biased = scores + expert_bias
            _, sel = jax.lax.top_k(biased, TOP_K)
            top_scores = jnp.take_along_axis(scores, sel, axis=-1)
            flat_sel = sel.reshape(-1)
            counts = jnp.bincount(flat_sel, length=NUM_EXPERTS)
            order = jnp.argsort(flat_sel, stable=True)
            scores_sorted = top_scores.reshape(-1)[order]
            token_ids = order // TOP_K
            routed_in = (xf[token_ids] * scores_sorted[:, None]).astype(x.dtype)
            seg = jnp.repeat(jnp.arange(NUM_EXPERTS), counts, total_repeat_length=flat_sel.shape[0])
            onehot = jax.nn.one_hot(seg, NUM_EXPERTS, dtype=jnp.float32)
            h = _masked_grouped_mm(routed_in.astype(jnp.bfloat16), w_up.astype(jnp.bfloat16), onehot)
            h = jnp.square(jax.nn.relu(h.astype(jnp.bfloat16)))
            routed_out = _masked_grouped_mm(h.astype(jnp.bfloat16), w_down.astype(jnp.bfloat16), onehot)
            routed_out = routed_out.astype(jnp.bfloat16).astype(x.dtype)
            hs = jnp.square(jax.nn.relu(xf @ shared_w_up.T))
            shared_out = hs @ shared_w_down.T
            combined = jnp.zeros((flat_sel.shape[0], dim), routed_out.dtype).at[order].set(routed_out)
            out = combined.reshape(-1, TOP_K, dim).sum(axis=1) + shared_out
            return out.reshape(bs, slen, dim)
        return moe_forward(x, gate_w, expert_bias, w_up, w_down, shared_w_up, shared_w_down)

    def _L1_attn_ref(inputs, Wq, bq, Wk, bk, Wv, bv, Wo, bo):
        import jax, jax.numpy as jnp
        import numpy as np
        HIDDEN = 128
        HEADS = 16
        HEAD_DIM = HIDDEN // HEADS
        B, S, _ = inputs.shape

        def proj(W, b):
            return (inputs @ W.T + b).reshape(B, S, HEADS, HEAD_DIM)
        q = proj(Wq, bq) / jnp.asarray(np.sqrt(HEAD_DIM), inputs.dtype)
        k = proj(Wk, bk)
        v = proj(Wv, bv)
        scores = jnp.einsum('bqhd,bkhd->bhqk', q, k)
        attn = jax.nn.softmax(scores, axis=-1)
        ctx = jnp.einsum('bhqk,bkhd->bqhd', attn, v)
        ctx = ctx.reshape(B, S, HIDDEN)
        return ctx @ Wo.T + bo

    def _L1_ffn_ref(x, w_router, W_qkv, W_out, g1, g2, W1, W2, W3):
        import math
        import jax, jax.numpy as jnp
        import numpy as np
        B, T, D = (4, 512, 128)
        H = 16
        HD = D // H
        CAP = int(512 * 0.125)
        DFF = int(D * 4 * 2 / 3)
        EPS = 1e-06

        def rmsnorm(x, g):
            return x * jax.lax.rsqrt(jnp.mean(x * x, axis=-1, keepdims=True) + EPS) * g
        Bq, Tq, Dq = x.shape
        scores = x @ w_router
        _, idx = jax.lax.top_k(scores, CAP)
        x_sel = jnp.take_along_axis(x, idx[:, :, None], axis=1)
        h = rmsnorm(x_sel, g1)
        qkv = (h @ W_qkv.T).reshape(Bq, CAP, 3, H, HD)
        q, k, v = jnp.moveaxis(qkv, 2, 0)
        att = jnp.einsum('bqhd,bkhd->bhqk', q, k) / math.sqrt(HD)
        mask = jnp.triu(jnp.ones((CAP, CAP), bool), 1)
        att = jnp.where(mask, -jnp.inf, att)
        att = jax.nn.softmax(att, axis=-1)
        o = jnp.einsum('bhqk,bkhd->bqhd', att, v).reshape(Bq, CAP, Dq)
        x_attn = o @ W_out.T
        h2 = rmsnorm(x_sel + x_attn, g2)
        x_ff = jax.nn.silu(h2 @ W1.T) * (h2 @ W2.T) @ W3.T
        x_proc = x_sel + x_attn + x_ff
        out = x.at[jnp.arange(Bq)[:, None], idx].set(x_proc)
        return out
    x = L0_attn_x
    x = x + _layernorm(_L0_attn_ref(_layernorm(x, axis=-1), L0_attn_Wq_down, L0_attn_Wk_down, L0_attn_Wv_down, L0_attn_Wq_up_c, L0_attn_Wq_up_e, L0_attn_Wk_up_c, L0_attn_Wk_up_e, L0_attn_Wv_up, L0_attn_Wc), axis=-1)
    x = x + _layernorm(_L0_ffn_ref(_layernorm(x, axis=-1), L0_ffn_gate_w, L0_ffn_expert_bias, L0_ffn_w_up, L0_ffn_w_down, L0_ffn_shared_w_up, L0_ffn_shared_w_down), axis=-1)
    x = x + _layernorm(_L1_attn_ref(_layernorm(x, axis=-1), L1_attn_Wq, L1_attn_bq, L1_attn_Wk, L1_attn_bk, L1_attn_Wv, L1_attn_bv, L1_attn_Wo, L1_attn_bo), axis=-1)
    x = x + _layernorm(_L1_ffn_ref(_layernorm(x, axis=-1), L1_ffn_w_router, L1_ffn_W_qkv, L1_ffn_W_out, L1_ffn_g1, L1_ffn_g2, L1_ffn_W1, L1_ffn_W2, L1_ffn_W3), axis=-1)
    return x

_drawn_inputs = setup_inputs


def setup_inputs(seed=0):
    import zlib

    import numpy as np

    out = dict(_drawn_inputs(seed))
    spreads = {'L0_ffn_expert_bias': (0.0, 0.1),
     'L1_attn_bq': (0.0, 0.453),
     'L1_attn_bk': (0.0, 0.8),
     'L1_attn_bv': (0.0, 0.1),
     'L1_attn_bo': (0.0, 0.1),
     'L1_ffn_g1': (1.0, 0.6),
     'L1_ffn_g2': (1.0, 0.6)}
    factors = {'L0_attn_Wq_down': 8.0,
     'L0_attn_Wk_down': 8.0,
     'L0_attn_Wq_up_c': 8.0,
     'L0_attn_Wq_up_e': 8.0,
     'L0_attn_Wk_up_c': 8.0,
     'L0_attn_Wk_up_e': 8.0,
     'L1_ffn_w_router': 8.0,
     'L1_ffn_W_qkv': 8.0,
     'L1_ffn_W_out': 8.0,
     'L1_ffn_W1': 8.0,
     'L1_ffn_W2': 8.0,
     'L1_ffn_W3': 8.0}
    for name, (base, spread) in spreads.items():
        noise = np.random.default_rng([zlib.crc32(name.encode()), seed]).standard_normal(out[name].shape)
        drawn = base * np.exp(spread * noise) if base else spread * noise
        out[name] = jnp.asarray(drawn.astype(out[name].dtype))
    for name, factor in factors.items():
        out[name] = (out[name] * factor).astype(out[name].dtype)
    return out
```

```python
from contextlib import ExitStack

import numpy as np

from concourse import mybir

F32 = mybir.dt.float32
BF16 = mybir.dt.bfloat16
ACT = mybir.ActivationFunctionType
ALU = mybir.AluOpType
AX = mybir.AxisListType

P = 128
B, T, C = 2, 1024, 128
H, DH, LAT = 16, 8, 64
TILES = B * T // P
CHUNKS = 4
TC = TILES // CHUNKS
CW = TC * P
G = 4
NG = B * H // G
KT = T // P
E, HID, HH = 8, 176, 88
TOP = 64
DFF, FC = 341, 3
SCALE = 1.0 / float(np.sqrt(DH))
LN_EPS, RMS_EPS = 1e-5, 1e-6
NEG = -1e30
Q_PARTS = (0, 0, 1, 1, 0, 2)
K_PARTS = (0, 1, 0, 1, 2, 0)
NPROD = len(Q_PARTS)
STACK = DH * NPROD
STACK_M = STACK + 3
VW = DH + 1
JOBS = KT * G


class Plan:

    def __init__(self, causal):
        self.causal = causal
        self.steps = [(qh, kt) for qh in range(2) for kt in range(4 * qh + 4 if causal else KT)]
        self.n = len(self.steps)
        self.jobs = [(qt, j) for qt in range(KT) for j in range(G)]
        job_cost = [self.keys(qt) // P for qt, _ in self.jobs]
        step_cost = [4 - self.skipped(qh, kt) // P for qh, kt in self.steps]
        self.beside, at, done = [], 0, 0.0
        for i in range(self.n):
            done += step_cost[i] * sum(job_cost) / sum(step_cost)
            upto = at
            while upto < JOBS and (sum(job_cost[:upto + 1]) <= done + 1e-6 or i == self.n - 1):
                upto += 1
            self.beside.append(list(range(at, upto)))
            at = upto
        self.half = next(i for i, (qh, _) in enumerate(self.steps) if qh == 1)
        first_max = next(i for i, b in enumerate(self.beside) if JOBS // 2 - 1 in b)
        self.small = {1: "max1", 2: "out1", self.half + 1: "out0",
                      max(self.half + 2, first_max + 2): "max0"}
        assert len(self.small) == 4 and max(self.small) < self.n

    def keys(self, qt):
        return (qt + 1) * P if self.causal else T

    def skipped(self, qh, kt):
        return max(0, kt * P - qh * 512) if self.causal else 0

    def diagonal(self, qh, kt):
        return self.causal and kt * P >= qh * 512


PLANS = (Plan(True), Plan(False))
NORMS = {("ln0", 1): 0, ("post0", 0): 1, ("post0", 1): 2, ("post1", 0): 3, ("post1", 1): 4,
         ("post2", 0): 5, ("post2", 1): 6, ("post3", 0): 7}
ADDS = {"post0": 0, "post1": 1, "post2": 2, "post3": 3}
TURNED = {"ln0": 0, "post0": 1, "post1": 2}


def norms_before(name, half, c):
    return CHUNKS * NORMS[name, half] + c


def adds_before(name, c):
    return CHUNKS * ADDS[name] + c


def turned_before(name, c):
    return CHUNKS * TURNED[name] + c


TURN = {"max1": 0, "out1": 1, "out0": 2, "max0": 3}


def turn(kind, n, first=False):
    if first:
        return {"max1": 1, "out0": 2, "max0": 3}[kind]
    return 4 * n + TURN[kind]


def periods(eng, emit, last=NG - 1):
    emit(0, 0, 0, True, False)
    with eng.Fori(0, (NG - 2) // 2) as i:
        emit(2 * i + 1, 1, i, False, False)
        emit(2 * i + 2, 0, i + 1, False, False)
    emit(NG - 1, 1, NG // 2 - 1, False, True)


def build(nc, a, out):
    ctx = ExitStack()
    with ctx:
        sems = {}

        def sb(name, shape, dt=F32):
            return ctx.enter_context(nc.sbuf_tensor(name, shape, dt))

        def sem(name):
            if name not in sems:
                sems[name] = ctx.enter_context(nc.semaphore(name))
            return sems[name]

        def dram(name, shape, dt):
            return nc.dram_tensor(name, shape, dt, kind="Internal").ap()

        X = sb("X", [P, TILES, C])
        XN = sb("XN", [P, TILES, C])
        XNT = sb("XNT", [P, TILES * P])
        TMP = sb("TMP", [P, TILES, C])
        Y = sb("Y", [P, KT, NG, G * DH])
        YB = Y[:, :, :, :].rearrange("p k n d -> p (k n d)").rearrange("p (t c) -> p t c", t=TILES)
        YT = sb("YT", [P, TILES * P])
        bn = sb("bn", [P, TILES, 6])
        mv = sb("mv", [P, TILES, 2])
        veps = sb("veps", [P, TILES])
        rstd = sb("rstd", [P, TILES])
        neg_half = sb("neg_half", [P, TILES])
        ident = sb("ident", [P, P])
        masks = sb("masks", [P, 2, P])
        ident_bf = sb("ident_bf", [P, P], BF16)
        mask_bf = sb("mask_bf", [P, 2, P], BF16)
        ones_row = sb("ones_row", [1, P])
        rope = TMP[:, :, :].rearrange("p t c -> p (t c)").rearrange("p (a t) -> p a t", a=2)
        arena = sb("arena", [P, 6144])
        down = arena[0:LAT, :].rearrange("p (s h c) -> p s h c", s=3, h=H)
        parts = arena[:, :].bitcast(BF16).rearrange("p (u k t) -> p u k t", u=4, k=3)
        ups = sb("ups", [LAT, 5, DH])
        wqk = [sb(f"wqk{i}", [C, 2, 2, H * DH]) for i in range(2)]
        wv = [sb(f"wv{i}", [C, H * DH]) for i in range(2)]
        wo = [sb(f"wo{i}", [C, C]) for i in range(2)]
        bqk = sb("bqk", [P, 2])
        bvo = sb("bvo", [1, 2, C])
        full = sb("full", [P, 2, T])
        rest = sb("rest", [P, 2, T])
        Vx = sb("Vx", [P, NG, KT, G, VW])
        SQ, TQ = (sb(n, [P, 2, G, T], BF16) for n in ("SQ", "TQ"))
        SK, TK = (sb(n, [P, 2, G // 2, T], BF16) for n in ("SK", "TK"))
        VS = sb("VS", [P, 2, KT, G, VW])
        probs = sb("probs", [P, 2, G, 512])
        nmax = sb("nmax", [P, 2, 2, 2, 8])
        nmax_rest = sb("nmax_rest", [P, 2, 2, 2, 8])
        nmax3_cols = sb("nmax3", [P, 2, 2, P], BF16)
        nmax3 = nmax3_cols[:, :, :, 0:48].rearrange("p g h (e i x) -> p g h e i x", e=2, i=3)
        zeros = sb("zeros", [P, 16])
        nmaxT = sb("nmaxT", [48, 2, 2, P], BF16)
        OS = sb("OS", [P, 2, 512])
        rden = sb("rden", [P, 2, 16])
        gateT = sb("gateT", [C, E])
        ebias = sb("ebias", [P, E])
        before8 = sb("before8", [P, E, E])
        moe_f = probs[:, :, :, :].rearrange("p a j q -> p (a j q)")[:, 0:E * (HID + 2 * C)]
        moe_b = sb("moe_b", [P, E * (HID + 2 * C)], BF16)
        wup_bf = moe_b[:, 0:E * HID].rearrange("p (e h) -> p e h", e=E)
        wdn_bf = moe_b[0:HH, E * HID:].rearrange("p (e k c) -> p e k c", e=E, k=2)
        supT = sb("supT", [C, HID])
        sdnT = sb("sdnT", [HH, 2, C])
        esc = sb("esc", [P, CHUNKS, TC, E])
        ebi = sb("ebi", [P, CHUNKS, TC, E])
        cmp = sb("cmp", [P, 2, TC * E * E])
        erank = sb("erank", [P, CHUNKS, TC, E])
        esel = sb("esel", [P, CHUNKS, TC, E])
        escT = TMP[0:E, :, :].rearrange("p t c -> p (t c)").rearrange("p (c q) -> p c q", c=CHUNKS)
        arena_bf = arena[:, :].bitcast(BF16)
        xsT = arena_bf[:, 0:2 * CW].rearrange("p (u q) -> p u q", u=2)
        eout = arena_bf[:, 2 * CW:4 * CW].rearrange("p (u q) -> p u q", u=2)
        hrelu = arena_bf[0:HH, 4 * CW:8 * CW].rearrange("p (u k q) -> p u k q", u=2, k=2)
        hsq = arena_bf[0:HH, 8 * CW:12 * CW].rearrange("p (u k q) -> p u k q", u=2, k=2)
        hs = probs[0:HH, 0, 0:2, :]
        hs2 = probs[0:HH, 1, 0:2, :]

        ps = ctx.enter_context(nc.psum_tensor("ps", [P, 8, 512], F32))

        def bank(i, n=1):
            return ps[:, i:i + n, :].rearrange("p a b -> p (a b)")

        split_d = [dram(f"split{i}", [2, B, 3, P, T], BF16) for i in range(2)]
        stack_d = [dram(f"stack{i}", [2, NG, 2, P, T], BF16) for i in range(2)]
        nmax_d = [dram(f"nmaxd{i}", [2, 2, 48, P], BF16) for i in range(2)]
        score_d = dram("score_d", [TILES, P], F32)

        FF = ffn_buffers(sb, full, rest, XNT, TMP, YT, arena)

        block = ctx.enter_context(nc.Block())

        @block.sync
        def _(sp):
            sp.dma_start(X[:, :, :], a["x"].rearrange("(t p) c -> p t c", p=P)).then_inc(sem("x_in"), 16)
            for dst, src in ((ident[:, :], a["ident"]), (masks[:, :, :], a["masks"])):
                sp.dma_start(dst, src).then_inc(sem("const_in"), 16)
            sp.dma_start(ups[:, 0, :], a["upq"]).then_inc(sem("w0_in"), 16)
            sp.dma_start(ups[:, 2, :], a["upk"]).then_inc(sem("w0_in"), 16)
            sp.dma_start(ups[:, 4, :], a["upv"]).then_inc(sem("w0_in"), 16)
            sp.dma_start(down, a["down"]).then_inc(sem("w0_in"), 16)
            sp.dma_start(rope, a["rope"]).then_inc(sem("rope_in"), 16)
            later = [(wo[0][:, :], "wo0"), (gateT[:, :], "gateT"), (ebias[:, :], "ebias"),
                     (before8[:, :, :], "before8"), 
                     (moe_f[:, 0:E * HID], "wupT"), (moe_f[0:HH, E * HID:], "wdnT"),
                     (supT[:, :], "supT"), (sdnT[:, :, :], "sdnT"),
                     (wqk[1][:, 0, 0, :], "wq1"), (wqk[1][:, 1, 0, :], "wk1"), (wv[1][:, :], "wv1"),
                     (wo[1][:, :], "wo1"), (bqk[:, :], "bqk"), (bvo[:, :, :], "bvo")]
            later += [(FF[k], k) for k in FFN_INPUTS]
            for dst, key in later:
                sp.dma_start(dst, a[key]).then_inc(sem("later_in"), 16)
            assert len(later) == LATER

            def restack(L, w):
                b, side = w // 2, w % 2
                sp.wait_ge(sem(f"split_done{L}"), w + 1)
                sp.dma_start(split_d[L][side, b].rearrange("k p t -> p k t"), parts[:, w, :, :])\
                    .then_inc(sem(f"split_out{L}{w}"), 16)

            def products(L, w):
                b, side = w // 2, w % 2
                sp.wait_ge(sem(f"split_out{L}{w}"), 16)
                rows = stack_d[L][side, NG // 2 * b:NG // 2 * (b + 1)]\
                    .rearrange("g r (e s) t -> (g r e) s t", e=2)
                for i, k in enumerate((Q_PARTS, K_PARTS)[side]):
                    sp.dma_start(rows[:, DH * i:DH * (i + 1), :],
                                 split_d[L][side, b, k].rearrange("(h d) t -> h d t", d=DH))\
                        .then_inc(sem(f"stacked{L}{b}"), 16)

            def load_first(L, n, par):
                for side, dst in ((0, SQ), (1, SK)):
                    for e in range(2):
                        heads = slice(e, G, 2) if side == 0 else slice(0, G // 2)
                        sp.dma_start(dst[64 * e:64 * e + STACK, par, heads, :],
                                     stack_d[L][side, n, :, 64 * e:64 * e + STACK, :]
                                     .rearrange("r s t -> s r t")).then_inc(sem(f"first_in{L}{par}"), 16)

            def load_second(L, n, par):
                for side, dst in ((0, TQ), (1, TK)):
                    for e in range(2):
                        heads = slice(e, G, 2) if side == 0 else slice(0, G // 2)
                        sp.dma_start(dst[64 * e:64 * e + STACK, par, heads, :],
                                     stack_d[L][side, n, :, 64 * e:64 * e + STACK, :]
                                     .rearrange("r s t -> s r t")).then_inc(sem(f"second_in{L}{par}"), 16)
                sp.dma_start(VS[:, par].rearrange("p k j v -> p (k j v)"),
                             Vx[:, n].rearrange("p k j v -> p (k j v)")).then_inc(sem(f"second_in{L}{par}"), 16)

            def place_max(L, turns, n, par, qh):
                sp.wait_ge(sem(f"small_done{L}"), turns + 1)
                sp.dma_start(nmax_d[L][par, qh], nmaxT[:, par, qh, :]).then_inc(sem(f"max_out{L}{qh}"), 16)
                sp.wait_ge(sem(f"max_out{L}{qh}"), 16 * (n + 1))
                for e in range(2):
                    sp.dma_start(TQ[64 * e + STACK:64 * e + STACK_M, par, e:G:2, 512 * qh:512 * qh + 512],
                                 nmax_d[L][par, qh, 24 * e:24 * e + 24, :]
                                 .rearrange("(i r q) t -> i r (q t)", i=3, r=2))\
                        .then_inc(sem(f"max_in{L}{qh}"), 16)

            for L, plan in enumerate(PLANS):
                if L == 0:
                    sp.wait_ge(sem("pool_const"), POOL_CONSTS)
                for b in range(B):
                    restack(L, 2 * b)
                    restack(L, 2 * b + 1)
                    products(L, 2 * b)
                    products(L, 2 * b + 1)
                    if b == 0:
                        sp.wait_ge(sem(f"stacked{L}0"), 32 * NPROD)
                        load_first(L, 0, 0)
                        sp.wait_ge(sem(f"v_done{L}"), 4)
                        load_second(L, 0, 0)
                        load_first(L, 1, 1)
                        load_second(L, 1, 1)
                sp.wait_ge(sem(f"stacked{L}1"), 32 * NPROD)
                sp.wait_ge(sem(f"v_done{L}"), 8)
                place_max(L, 0, 0, 0, 0)

                def period(n, par, first=False, more_first=True, more_second=True, last=False):
                    if more_first:
                        sp.wait_ge(sem(f"rowmax{L}"), JOBS * (n + 1))
                        load_first(L, n + 2, par)
                    if not first and more_second:
                        sp.wait_ge(sem(f"pv{L}"), plan.n * n)
                        load_second(L, n + 1, 1 - par)
                    place_max(L, turn("max1", n, first), n, par, 1)
                    if not last:
                        place_max(L, turn("max0", n, first), n + 1, 1 - par, 0)

                period(0, 0, first=True)
                with sp.Fori(0, 2) as i:
                    period(2 * i + 1, 1)
                    period(2 * i + 2, 0)
                period(5, 1)
                period(6, 0, more_first=False)
                period(7, 1, more_first=False, more_second=False, last=True)

            sp.wait_ge(sem("scoreT"), 1)
            sp.dma_start(score_d, FF["scoreT"]).then_inc(sem("score_out"), 16)
            sp.wait_ge(sem("score_out"), 16)
            sp.dma_start(FF["score_row"], score_d.rearrange("t q -> (t q)").partition_broadcast(P))\
                .then_inc(sem("score_in"), 16)
            for c in range(CHUNKS):
                sp.wait_ge(sem("x_added"), adds_before("post3", c) + 1)
                sp.dma_start(out.rearrange("(t p) c -> p t c", p=P)[:, TC * c:TC * c + TC, :],
                             X[:, TC * c:TC * c + TC, :]).then_inc(sem("stored"), 16)
            sp.wait_ge(sem("stored"), 16 * CHUNKS)

        @block.gpsimd
        def _(pool):
            n_const = 0
            for dst, v in ((neg_half[:, :], -0.5), (zeros[:, :], 0.0), (TK[:, :, :, :], 1.0), (Vx[:, :, :, :, :], 1.0),
                           (ones_row[:, :], 1.0), (FF["count"], 0.0), (nmax3_cols[:, :, :, :], 0.0),
                           (SK[:, :, :, :].bitcast(F32), 0.0), (SQ[:, :, :, :].bitcast(F32), 0.0),
                           (TQ[:, :, :, :].bitcast(F32), 0.0)):
                pool.memset(dst, v).then_inc(sem("pool_const"), 1)
                n_const += 1
            assert n_const == POOL_CONSTS
            pool.wait_ge(sem("pool_const"), POOL_CONSTS)

            def inv_std(name, c, half):
                done, k = sem("norm_rstd"), norms_before(name, half, c)
                t = slice(TC * c, TC * c + TC)
                pool.wait_ge(sem("norm_stats"), k + 1)
                pool.tensor_scalar(veps[:, t], mv[:, t, 1], LN_EPS, None, ALU.add).then_inc(done, 1)
                pool.wait_ge(done, 2 * k + 1)
                pool.tensor_tensor(rstd[:, t], veps[:, t], neg_half[:, t], ALU.pow).then_inc(done, 1)

            def residual(name, c):
                pool.wait_ge(sem("normed"), TC * (norms_before(name, 0, c) + 1))
                t = slice(TC * c, TC * c + TC)
                pool.tensor_tensor(X[:, t, :], X[:, t, :], TMP[:, t, :], ALU.add)\
                    .then_inc(sem("x_added"), 1)

            def post(name, more):
                for c in range(CHUNKS):
                    inv_std(name, c, 0)
                for c in range(CHUNKS):
                    residual(name, c)
                if more:
                    for c in range(CHUNKS):
                        inv_std(name, c, 1)

            def split(L):
                for w in range(4):
                    pool.wait_ge(sem(f"part0_{L}"), w + 1)
                    pool.tensor_tensor(rest[:, w % 2, :], full[:, w % 2, :], parts[:, w, 0, :],
                                       ALU.subtract).then_inc(sem(f"rest_{L}"), 1)

            def split_max(L):
                step = sem(f"max3_{L}")
                zero = zeros[:, :].rearrange("p (e x) -> p e x", e=2)

                def one(n, par):
                    for qh in range(2):
                        at = 8 * n + 4 * qh
                        src, left = nmax[:, par, qh], nmax_rest[:, par, qh]
                        dst = nmax3[:, par, qh]
                        pool.wait_ge(sem(f"rowmax{L}"), JOBS * n + JOBS // 2 * (qh + 1))
                        pool.tensor_tensor(dst[:, :, 0, :], src, zero, ALU.add).then_inc(step, 1)
                        pool.wait_ge(step, at + 1)
                        pool.tensor_tensor(left, src, dst[:, :, 0, :], ALU.subtract).then_inc(step, 1)
                        pool.wait_ge(step, at + 2)
                        pool.tensor_tensor(dst[:, :, 1, :], left, zero, ALU.add).then_inc(step, 1)
                        pool.wait_ge(step, at + 3)
                        pool.tensor_tensor(dst[:, :, 2, :], left, dst[:, :, 1, :], ALU.subtract)\
                            .then_inc(step, 1)

                with pool.Fori(0, NG // 2) as i:
                    one(2 * i, 0)
                    one(2 * i + 1, 1)

            for c in range(CHUNKS):
                inv_std("ln0", c, 1)
            split(0)
            split_max(0)
            post("post0", True)
            for u in range(CHUNKS * E):
                c, e = divmod(u, E)
                pool.wait_ge(sem("eout"), u + 1)
                if e:
                    pool.wait_ge(sem("eacc"), u)
                    pool.tensor_tensor(YB[:, TC * c:TC * c + TC, :], YB[:, TC * c:TC * c + TC, :],
                                       eout[:, u % 2, :].rearrange("p (t c) -> p t c", t=TC), ALU.add)\
                        .then_inc(sem("eacc"), 1)
                else:
                    pool.tensor_copy(YB[:, TC * c:TC * c + TC, :],
                                     eout[:, u % 2, :].rearrange("p (t c) -> p t c", t=TC))\
                        .then_inc(sem("eacc"), 1)
            post("post1", True)
            split(1)
            split_max(1)
            post("post2", True)
            for i in range(2):
                pool.wait_ge(sem(f"ssq{i}"), 1)
                pool.tensor_scalar(FF["small"][:, 2 * i:2 * i + 1], FF["ssq"][:, i:i + 1], 1.0 / C, RMS_EPS,
                                   ALU.mult, ALU.add).then_inc(sem(f"rms{i}"), 1)
                pool.wait_ge(sem(f"rms{i}"), 1)
                pool.tensor_tensor(FF["small"][:, 2 * i + 1:2 * i + 2], FF["small"][:, 2 * i:2 * i + 1],
                                   neg_half[:, 0:1], ALU.pow).then_inc(sem(f"rms{i}"), 1)
            post("post3", False)

        @block.scalar
        def _(act):
            act.wait_ge(sem("const_in"), 32)
            act.activation(ident_bf[:, :], ident[:, :], ACT.Copy).then_inc(sem("act_const"), 1)
            act.activation(mask_bf[:, :, :], masks[:, :, :], ACT.Copy).then_inc(sem("act_const"), 1)

            def to_xnT(name):
                for c in range(CHUNKS):
                    act.wait_ge(sem("xnT_ps"), turned_before(name, c) + 1)
                    act.activation(XNT[:, CW * c:CW * c + CW], bank(c), ACT.Copy)\
                        .then_inc(sem("xnT"), 1)

            def project(L):
                def q_or_k(w):
                    act.wait_ge(sem(f"qk_ps{L}"), w + 1)
                    if w >= 2:
                        act.wait_ge(sem(f"split_done{L}"), w - 1)
                    act.activation(full[:, w % 2, :], bank(QK_BANK[w], 2), ACT.Identity,
                                   bias=bqk[:, w % 2:w % 2 + 1]).then_inc(sem(f"qk_full{L}"), 1)

                def part(w, k):
                    act.wait_ge(sem(f"qk_full{L}" if k == 0 else f"rest_{L}"), w + 1)
                    act.activation(parts[:, w, k, :], (full, rest)[k][:, w % 2, :], ACT.Copy)\
                        .then_inc(sem(f"part{k}_{L}"), 1)

                def values(b):
                    act.wait_ge(sem(f"v_ps{L}"), b + 1)
                    v = bank(V_BANK[b], 2).rearrange("p (k g j d) -> p k g j d", k=KT, g=G, j=G)
                    for g in range(G):
                        act.activation(Vx[:, G * b + g, :, :, 0:DH], v[:, :, g], ACT.Copy)\
                            .then_inc(sem(f"v_done{L}"), 1)

                for b in range(B):
                    for w in (2 * b, 2 * b + 1):
                        if L:
                            q_or_k(w)
                        part(w, 0)
                    part(2 * b, 1)
                    part(2 * b + 1, 1)
                    values(b)

            def attend(L, plan):
                exps, pv, ev = sem(f"exp{L}"), sem(f"pv{L}"), sem(f"out_copied{L}")

                def copy_out(qh, turns, n_pv):
                    act.wait_ge(pv, n_pv)
                    act.activation(OS[:, qh, :], bank(6), ACT.Copy).then_inc(ev, 1)

                def period(n, par, rounds, first, last):
                    for s, (qh, kt) in enumerate(plan.steps):
                        c0 = plan.skipped(qh, kt)
                        for j in range(G):
                            act.wait_ge(sem(f"second_ps{L}"), (plan.n * n + s) * G + j + 1)
                            if j == 0 and not (first and s < 2):
                                act.wait_ge(pv, plan.n * n + s - 1)
                            act.activation(probs[:, s % 2, j, c0:512], ps[:, 4 + j % 2, c0:512],
                                           ACT.Exp, scale=SCALE).then_inc(exps, 1)
                        if s == 0 and not first:
                            copy_out(1, None, plan.n * n)
                        if s == plan.half:
                            copy_out(0, None, plan.n * n + plan.half)

                periods(act, period)
                copy_out(1, None, plan.n * NG)

            def copy_yT(L):
                for c in range(CHUNKS):
                    act.wait_ge(sem(f"yT_ps{L}"), c + 1)
                    act.activation(YT[:, CW * c:CW * c + CW], bank(c), ACT.Copy).then_inc(sem(f"yT{L}"), 1)

            to_xnT("ln0")
            project(0)
            act.wait_ge(sem("later_in"), 16 * LATER)
            act.activation(moe_b[:, 0:E * HID], moe_f[:, 0:E * HID], ACT.Copy).then_inc(sem("moe_bf"), 1)
            act.activation(moe_b[0:HH, E * HID:], moe_f[0:HH, E * HID:], ACT.Copy).then_inc(sem("moe_bf"), 1)
            act.wait_ge(sem("moe_bf"), 2)
            attend(0, PLANS[0])
            copy_yT(0)
            to_xnT("post0")
            for c in range(CHUNKS):
                act.wait_ge(sem("gate_ps"), c + 1)
                act.activation(esc[:, c], bank(4 + c)[:, 0:TC * E].rearrange("p (t e) -> p t e", t=TC),
                               ACT.Exp, scale=-1.0).then_inc(sem("gate_exp"), 1)
            for c in range(CHUNKS):
                act.wait_ge(sem("escT_ps"), c + 1)
                act.activation(escT[:, c, :], bank(1 + c % 2)[0:E, :], ACT.Copy).then_inc(sem("escT"), 1)
            for c in range(CHUNKS):
                act.wait_ge(sem("shared_up"), c + 1)
                if c:
                    act.wait_ge(sem("shared_sq"), c)
                act.activation(hs, ps[0:HH, 2:4, :], ACT.Relu).then_inc(sem("shared_relu"), 1)
                for e in range(E):
                    u = E * c + e
                    act.wait_ge(sem("up_ps"), u + 1)
                    if u >= 2:
                        act.wait_ge(sem("hsq"), u - 1)
                    act.activation(hrelu[:, u % 2], ps[0:HH, 2:4, :], ACT.Relu).then_inc(sem("hrelu"), 1)
            to_xnT("post1")
            project(1)
            attend(1, PLANS[1])
            copy_yT(1)
            act_ffn(act, sem, bank, ps, FF)

        @block.vector
        def _(dve):
            def moments(name, half, c, src):
                st, k = sem("norm_bn"), norms_before(name, half, c)
                for t in range(TC):
                    dve.bn_stats(bn[:, TC * c + t, :], src(c, t)).then_inc(st, 1)
                for t in range(TC):
                    dve.wait_ge(st, TC * k + t + 1)
                    ins = dve.bn_aggr(mv[:, TC * c + t, :], bn[:, TC * c + t, :])
                ins.then_inc(sem("norm_stats"), 1)

            def norm(name, half, c, src, dst):
                dve.wait_ge(sem("norm_rstd"), 2 * norms_before(name, half, c) + 2)
                for t in range(TC):
                    i = TC * c + t
                    dve.tensor_scalar(dst[:, i, :], src(c, t), mv[:, i, 0:1], rstd[:, i:i + 1],
                                      ALU.subtract, ALU.mult).then_inc(sem("normed"), 1)

            def x_tile(c, t):
                return X[:, TC * c + t, :]

            def ps_tile(c, t):
                return ps[:, 4 + c, P * t:P * t + P]

            def yb_tile(c, t):
                return YB[:, TC * c + t, :]

            def post(name, ready, src, more):
                for c in range(CHUNKS):
                    dve.wait_ge(sem(ready), c + 1)
                    moments(name, 0, c, src)
                for c in range(CHUNKS):
                    norm(name, 0, c, src, TMP)
                if more:
                    for c in range(CHUNKS):
                        dve.wait_ge(sem("x_added"), adds_before(name, c) + 1)
                        moments(name, 1, c, x_tile)
                    for c in range(CHUNKS):
                        norm(name, 1, c, x_tile, XN)

            def last_part(L, w):
                dve.wait_ge(sem(f"part1_{L}"), w + 1)
                dve.tensor_tensor(parts[:, w, 2, :], rest[:, w % 2, :], parts[:, w, 1, :], ALU.subtract)\
                    .then_inc(sem(f"split_done{L}"), 1)

            def rotate(w):
                step = sem("rotated")
                dve.wait_ge(sem("qk_ps0"), w + 1)
                if w >= 2:
                    dve.wait_ge(sem("split_done0"), w - 1)
                dve.tensor_tensor(full[:, w % 2, :], bank(QK_BANK[w], 2), rope[:, 0, :], ALU.mult)\
                    .then_inc(step, 1)
                dve.tensor_tensor(rest[:, w % 2, :], bank(QK_BANK[w] + 2, 2), rope[:, 1, :], ALU.mult)\
                    .then_inc(step, 1)
                dve.wait_ge(step, 2 * w + 2)
                dve.tensor_tensor(full[:, w % 2, :], full[:, w % 2, :], rest[:, w % 2, :], ALU.add)\
                    .then_inc(sem("qk_full0"), 1)

            def attend(L, plan):
                maxed, small = sem(f"rowmax{L}"), sem(f"small_done{L}")

                def row_max(n, par, jj):
                    qt, j = plan.jobs[jj]
                    pair, e = divmod(j, 2)
                    dve.wait_ge(sem(f"first_ps{L}"), JOBS * n + jj + 1)
                    dve.tensor_reduce(nmax[:, par, qt // 4, e, 4 * pair + qt % 4:4 * pair + qt % 4 + 1],
                                      bank(2 * e, 2)[:, 0:plan.keys(qt)], AX.X, ALU.max, negate=True)\
                        .then_inc(maxed, 1)

                def copy_max(turns, par, qh):
                    dve.wait_ge(sem(f"small_ps{L}"), turns + 1)
                    dve.tensor_copy(nmaxT[:, par, qh, :], bank(7).bitcast(BF16)[0:48, 0:P]).then_inc(small, 1)

                def normalise(turns, n, qh):
                    dve.wait_ge(sem(f"small_ps{L}"), turns + 1)
                    o = bank(7).rearrange("p (x v) -> p x v", v=32)
                    dve.reciprocal(rden[:, qh, :], o[:, :, DH]).then_inc(sem(f"rden{L}"), 1)
                    dve.wait_ge(sem(f"rden{L}"), 2 * n + qh + 1)
                    dve.tensor_tensor(Y[:, 4 * qh:4 * qh + 4, n, :].rearrange("p k (j d) -> p k j d", j=G),
                                      o[:, :, 0:DH].rearrange("p (k j) d -> p k j d", j=G),
                                      rden[:, qh, :].rearrange("p (k j) -> p k j", j=G).unsqueeze(3)
                                      .to_broadcast([P, 4, G, DH]), ALU.mult)\
                        .then_inc(small, 1)

                for jj in range(JOBS):
                    row_max(0, 0, jj)
                copy_max(0, 0, 0)

                def period(n, par, rounds, first, last):
                    for s in range(plan.n):
                        if not last:
                            for jj in plan.beside[s]:
                                row_max(n + 1, 1 - par, jj)
                        kind = plan.small.get(s)
                        if kind == "max1":
                            copy_max(turn(kind, n, first), par, 1)
                        if kind == "max0" and not last:
                            copy_max(turn(kind, n, first), 1 - par, 0)
                        if kind == "out0":
                            normalise(turn(kind, n, first), n, 0)
                        if kind == "out1" and not first:
                            normalise(turn(kind, n, first), n - 1, 1)

                periods(dve, period)
                normalise(turn("max0", NG - 1), NG - 1, 1)

            dve.wait_ge(sem("w0_in"), 64)
            for q in (0, 2):
                plain = ups[:, q, 4:8].rearrange("p (i k) -> p i k", k=2)
                turned = ups[:, q + 1, 4:8].rearrange("p (i k) -> p i k", k=2)
                dve.memset(ups[:, q + 1, 0:4], 0.0).then_inc(sem("ups_rot"), 1)
                dve.tensor_scalar(turned[:, :, 0], plain[:, :, 1], -1.0, None, ALU.mult).then_inc(sem("ups_rot"), 1)
                dve.tensor_copy(turned[:, :, 1], plain[:, :, 0]).then_inc(sem("ups_rot"), 1)
            dve.wait_ge(sem("folded_ps"), 1)
            for side in range(2):
                dve.tensor_copy(wqk[0][:, side].rearrange("p r (h d) -> p r h d", h=H),
                                bank(side)[:, 0:256].rearrange("p (h r d) -> p r h d", h=H, r=2))\
                    .then_inc(sem("folded"), 1)
            dve.tensor_copy(wv[0][:, :], bank(2)[:, 0:P]).then_inc(sem("folded"), 1)
            dve.wait_ge(sem("x_in"), 16)
            dve.wait_ge(sem("pool_const"), POOL_CONSTS)
            for c in range(CHUNKS):
                moments("ln0", 1, c, x_tile)
            for c in range(CHUNKS):
                norm("ln0", 1, c, x_tile, XN)
            dve.wait_ge(sem("rope_in"), 16)
            rotate(0)
            rotate(1)
            last_part(0, 0)
            rotate(2)
            last_part(0, 1)
            rotate(3)
            last_part(0, 2)
            last_part(0, 3)
            attend(0, PLANS[0])
            post("post0", "branch_ps0", ps_tile, True)
            for c in range(CHUNKS):
                step = sem("route")
                k = 8 * c
                sc, bi = esc[:, c], ebi[:, c]
                mine = bi.unsqueeze(3).to_broadcast([P, TC, E, E])
                theirs = bi.unsqueeze(2).to_broadcast([P, TC, E, E])
                x0 = cmp[:, 0, :].rearrange("p (t e j) -> p t e j", t=TC, e=E)
                x1 = cmp[:, 1, :].rearrange("p (t e j) -> p t e j", t=TC, e=E)
                bias = ebias[:, :].unsqueeze(1).to_broadcast([P, TC, E])
                before = before8[:, :, :].unsqueeze(1).to_broadcast([P, TC, E, E])
                dve.wait_ge(sem("gate_exp"), c + 1)
                dve.tensor_scalar(sc, sc, 1.0, None, ALU.add).then_inc(step, 1)
                dve.wait_ge(step, k + 1)
                dve.reciprocal(sc, sc).then_inc(step, 1)
                dve.wait_ge(step, k + 2)
                dve.tensor_tensor(bi, sc, bias, ALU.add).then_inc(step, 1)
                dve.wait_ge(step, k + 3)
                if c:
                    dve.wait_ge(sem("esel"), c)
                dve.tensor_tensor(x1, theirs, mine, ALU.is_equal).then_inc(step, 1)
                dve.tensor_tensor(x0, theirs, mine, ALU.is_gt).then_inc(step, 1)
                dve.wait_ge(step, k + 4)
                dve.tensor_tensor(x1, x1, before, ALU.mult).then_inc(step, 1)
                dve.wait_ge(step, k + 6)
                dve.tensor_tensor(x0, x0, x1, ALU.add).then_inc(step, 1)
                dve.wait_ge(step, k + 7)
                dve.tensor_reduce(erank[:, c], x0, AX.X, ALU.add).then_inc(step, 1)
                dve.wait_ge(step, k + 8)
                dve.tensor_scalar(esel[:, c], erank[:, c], 1.5, None, ALU.is_lt).then_inc(sem("esel"), 1)

            def scale_in(u):
                c, e = divmod(u, E)
                dve.wait_ge(sem("score_ps"), u + 1)
                if u >= 2:
                    dve.wait_ge(sem("up_ps"), u - 1)
                dve.tensor_tensor(xsT[:, u % 2, :], XNT[:, CW * c:CW * c + CW], bank(1), ALU.mult)\
                    .then_inc(sem("xsT"), 1)

            def masked_out(u):
                c, e = divmod(u, E)
                dve.wait_ge(sem("down_ps"), u + 1)
                if u >= 2:
                    dve.wait_ge(sem("eacc"), u - 1)
                dve.tensor_tensor(eout[:, u % 2, :].rearrange("p (t c) -> p t c", t=TC),
                                  bank(4 + u % 2).rearrange("p (t c) -> p t c", t=TC),
                                  esel[:, c, :, e:e + 1].to_broadcast([P, TC, C]), ALU.mult)\
                    .then_inc(sem("eout"), 1)

            def square(u):
                dve.wait_ge(sem("hrelu"), u + 1)
                if u >= 2:
                    dve.wait_ge(sem("down_ps"), u - 1)
                dve.tensor_tensor(hsq[:, u % 2], hrelu[:, u % 2], hrelu[:, u % 2], ALU.mult)\
                    .then_inc(sem("hsq"), 1)

            def add_shared(c):
                dve.wait_ge(sem("eacc"), E * c + E)
                dve.wait_ge(sem("shared_ps"), c + 1)
                dve.tensor_tensor(YB[:, TC * c:TC * c + TC, :], YB[:, TC * c:TC * c + TC, :],
                                  bank(6 + c % 2).rearrange("p (t c) -> p t c", t=TC), ALU.add)\
                    .then_inc(sem("moe_out"), 1)

            dve.wait_ge(sem("esel"), CHUNKS)
            scale_in(0)
            for u in range(CHUNKS * E):
                c, e = divmod(u, E)
                if u + 1 < CHUNKS * E:
                    scale_in(u + 1)
                if e == 0:
                    dve.wait_ge(sem("shared_relu"), c + 1)
                    if c:
                        dve.wait_ge(sem("shared_ps"), c)
                    dve.tensor_tensor(hs2, hs, hs, ALU.mult).then_inc(sem("shared_sq"), 1)
                square(u)
                if u:
                    masked_out(u - 1)
                if e == 1 and c:
                    add_shared(c - 1)
            masked_out(CHUNKS * E - 1)
            add_shared(CHUNKS - 1)
            post("post1", "moe_out", yb_tile, True)
            last_order = (0, 1, 2, 3)
            for w in last_order:
                last_part(1, w)
            attend(1, PLANS[1])
            post("post2", "branch_ps1", ps_tile, True)
            dve_ffn(dve, sem, bank, ps, FF, XN, YB)
            post("post3", "ffn_out", yb_tile, False)

        @block.tensor
        def _(pe):
            def transpose_xn(name):
                for c in range(CHUNKS):
                    pe.wait_ge(sem("normed"), TC * (norms_before(name, 1, c) + 1))
                    for t in range(TC):
                        ins = pe.transpose(ps[:, c, P * t:P * t + P], XN[:, TC * c + t, :], ident[:, :])
                    ins.then_inc(sem("xnT_ps"), 1)

            def project(L, xn):
                def q_or_k(w):
                    b, side = divmod(w, 2)
                    pe.wait_ge(sem("xnT"), turned_before(xn, 2 * b + 2))
                    if w == 2:
                        pe.wait_ge(sem(f"qk_full{L}"), 2)
                    if w == 3:
                        pe.wait_ge(sem(f"v_done{L}"), 4)
                    for r in range(2 - L):
                        for c in range(2):
                            ins = pe.matmul(ps[:, QK_BANK[w] + 2 * r + c, :], wqk[L][:, side, r, :],
                                            XNT[:, T * b + CW * c:T * b + CW * c + CW], start=True, stop=True)
                    ins.then_inc(sem(f"qk_ps{L}"), 1)

                def values(b):
                    pe.wait_ge(sem(f"qk_full{L}"), 2 * b + 1)
                    for k in range(KT):
                        o = bank(V_BANK[b], 2)[:, P * k:P * k + P]
                        ins = pe.matmul(o, XNT[:, T * b + P * k:T * b + P * k + P], wv[L][:, :],
                                        start=True, stop=not L)
                        if L:
                            ins = pe.matmul(o, ones_row[:, :], bvo[:, 0, :], start=False, stop=True)
                    ins.then_inc(sem(f"v_ps{L}"), 1)

                for b in range(B):
                    if b == 0:
                        pe.wait_ge(sem("xnT"), turned_before(xn, CHUNKS))
                    q_or_k(2 * b)
                    q_or_k(2 * b + 1)
                    values(b)

            def attend(L, plan):
                first, second, pv, small = (sem(f"{k}{L}") for k in ("first_ps", "second_ps", "pv", "small_ps"))
                exps, maxed, small_done = sem(f"exp{L}"), sem(f"rowmax{L}"), sem(f"small_done{L}")

                def first_job(n, par, rounds, jj, prologue=False):
                    qt, j = plan.jobs[jj]
                    pair, e = divmod(j, 2)
                    if jj == 0:
                        pe.wait_ge(sem(f"first_in{L}{par}"), 64 * (rounds + 1))
                    if not (prologue and jj < 2):
                        pe.wait_ge(maxed, JOBS * n + jj - 1)
                    keys = plan.keys(qt)
                    for k0 in range(0, keys, 512):
                        k1 = min(keys, k0 + 512)
                        masked = plan.causal and k1 == keys
                        ins = pe.matmul(ps[:, 2 * e + k0 // 512, 0:k1 - k0],
                                        SQ[:, par, j, P * qt:P * qt + P], SK[:, par, pair, k0:k1],
                                        start=True, stop=not masked)
                        if masked:
                            ins = pe.matmul(ps[:, 2 * e + k0 // 512, k1 - k0 - P:k1 - k0],
                                            ident_bf[:, :], mask_bf[:, 0, :], start=False, stop=True)
                    ins.then_inc(first, 1)

                def scores(n, par, rounds, s, j, begin):
                    qh, kt = plan.steps[s]
                    pair, e = divmod(j, 2)
                    c0 = plan.skipped(qh, kt)
                    if s == 0 and j == 0:
                        pe.wait_ge(sem(f"second_in{L}{par}"), 80 * (rounds + 1))
                    if kt == 0 and j == 0:
                        pe.wait_ge(sem(f"max_in{L}{qh}"), 32 * (n + 1))
                    if not (begin and s == 0 and j < 2):
                        pe.wait_ge(exps, (plan.n * n + s) * G + j - 1)
                    diagonal = plan.diagonal(qh, kt)
                    ins = pe.matmul(ps[:, 4 + e, c0:512], TK[:, par, pair, P * kt:P * kt + P],
                                    TQ[:, par, j, 512 * qh + c0:512 * qh + 512],
                                    start=True, stop=not diagonal)
                    if diagonal:
                        ins = pe.matmul(ps[:, 4 + e, c0:c0 + P], ident_bf[:, :], mask_bf[:, 1, :],
                                        start=False, stop=True)
                    ins.then_inc(second, 1)

                def times_values(n, par, s, begin):
                    qh, kt = plan.steps[s]
                    c0 = plan.skipped(qh, kt)
                    pe.wait_ge(exps, (plan.n * n + s + 1) * G)
                    if kt == 0 and not (begin and qh == 0):
                        pe.wait_ge(sem(f"out_copied{L}"), 2 * n + qh)
                    end = s == plan.n - 1 or plan.steps[s + 1][0] != qh
                    for j in range(G):
                        ins = pe.matmul(ps[32 * j:32 * j + VW, 6, c0:512], VS[:, par, kt, j, :],
                                        probs[:, s % 2, j, c0:512], start=(kt == 0), stop=end)
                    ins.then_inc(pv, 1)

                def max_rows(turns, n, par, qh, begin=False):
                    if not begin:
                        pe.wait_ge(small_done, turns)
                    pe.wait_ge(sem(f"max3_{L}"), 8 * n + 4 * qh + 4)
                    pe.transpose(bank(7).bitcast(BF16)[:, 0:P], nmax3_cols[:, par, qh, :], ident_bf[:, :])\
                        .then_inc(small, 1)

                def out_rows(turns, n, qh):
                    pe.wait_ge(small_done, turns)
                    pe.wait_ge(sem(f"out_copied{L}"), 2 * n + qh + 1)
                    for q in range(4):
                        ins = pe.transpose(ps[:, 7, P * q:P * q + P], OS[:, qh, P * q:P * q + P], ident[:, :])
                    ins.then_inc(small, 1)

                for jj in range(JOBS):
                    first_job(0, 0, 0, jj, prologue=True)
                max_rows(0, 0, 0, 0, begin=True)

                def period(n, par, rounds, begin, last):
                    for s in range(plan.n):
                        beside = [] if last else plan.beside[s]
                        for j in range(G):
                            scores(n, par, rounds, s, j, begin)
                            for jj in beside[len(beside) * j // G:len(beside) * (j + 1) // G]:
                                first_job(n + 1, 1 - par, rounds + par, jj)
                        if s:
                            times_values(n, par, s - 1, begin)
                        elif not begin:
                            times_values(n - 1, 1 - par, plan.n - 1, False)
                        kind = plan.small.get(s)
                        if kind == "max1":
                            max_rows(turn(kind, n, begin), n, par, 1)
                        if kind == "max0" and not last:
                            max_rows(turn(kind, n, begin), n + 1, 1 - par, 0)
                        if kind == "out0":
                            out_rows(turn(kind, n, begin), n, 0)
                        if kind == "out1" and not begin:
                            out_rows(turn(kind, n, begin), n - 1, 1)

                periods(pe, period)
                times_values(NG - 1, 1, plan.n - 1, False)
                out_rows(turn("max0", NG - 1), NG - 1, 1)

            def project_out(L):
                pe.wait_ge(sem(f"small_done{L}"), 4 * NG)
                for c in range(CHUNKS):
                    for t in range(TC):
                        b, k = divmod(TC * c + t, KT)
                        ins = pe.transpose(ps[:, c, P * t:P * t + P],
                                           Y[:, k, G * b:G * b + G, :].rearrange("p g d -> p (g d)"), ident[:, :])
                    ins.then_inc(sem(f"yT_ps{L}"), 1)
                for c in range(CHUNKS):
                    pe.wait_ge(sem(f"yT{L}"), c + 1)
                    for t in range(TC):
                        o = ps[:, 4 + c, P * t:P * t + P]
                        ins = pe.matmul(o, YT[:, CW * c + P * t:CW * c + P * t + P], wo[L][:, :],
                                        start=True, stop=not L)
                        if L:
                            ins = pe.matmul(o, ones_row[:, :], bvo[:, 1, :], start=False, stop=True)
                    ins.then_inc(sem(f"branch_ps{L}"), 1)

            pe.wait_ge(sem("w0_in"), 64)
            pe.wait_ge(sem("ups_rot"), 6)
            for side in range(2):
                for h in range(H):
                    pe.matmul(ps[:, side, 16 * h:16 * h + 16], down[:, side, h, :],
                              ups[:, 2 * side:2 * side + 2, :].rearrange("p r d -> p (r d)"), start=True, stop=True)
            for h in range(H):
                ins = pe.matmul(ps[:, 2, DH * h:DH * h + DH], down[:, 2, h, :], ups[:, 4, :],
                                start=True, stop=True)
            ins.then_inc(sem("folded_ps"), 1)
            pe.wait_ge(sem("const_in"), 32)
            pe.wait_ge(sem("folded"), 3)
            transpose_xn("ln0")
            project(0, "ln0")
            pe.wait_ge(sem("act_const"), 2)
            pe.wait_ge(sem("qk_full0"), 4)
            pe.wait_ge(sem("v_done0"), 8)
            attend(0, PLANS[0])
            pe.wait_ge(sem("later_in"), 16 * LATER)
            project_out(0)
            transpose_xn("post0")
            for c in range(CHUNKS):
                pe.wait_ge(sem("xnT"), turned_before("post0", CHUNKS))
                for t in range(TC):
                    i = TC * c + t
                    ins = pe.matmul(ps[:, 4 + c, E * t:E * t + E], XNT[:, P * i:P * i + P], gateT[:, :],
                                    start=True, stop=True)
                ins.then_inc(sem("gate_ps"), 1)
            for c in range(CHUNKS):
                pe.wait_ge(sem("route"), 8 * c + 2)
                if c >= 2:
                    pe.wait_ge(sem("escT"), c - 1)
                for t in range(TC):
                    ins = pe.transpose(ps[0:E, 1 + c % 2, P * t:P * t + P], esc[:, c, t, :], ident[:, :])
                ins.then_inc(sem("escT_ps"), 1)
            pe.wait_ge(sem("moe_bf"), 2)
            pe.wait_ge(sem("escT"), CHUNKS)

            def spread_score(u):
                c, e = divmod(u, E)
                if u:
                    pe.wait_ge(sem("xsT"), u)
                pe.matmul(ps[:, 1, :], ident[0:E, e:e + 1].to_broadcast([E, P]), escT[:, c, :], start=True, stop=True)\
                    .then_inc(sem("score_ps"), 1)

            def shared_up(c):
                if c:
                    pe.wait_ge(sem("hrelu"), E * c)
                for k in range(2):
                    ins = pe.matmul(ps[0:HH, 2 + k, :], supT[:, HH * k:HH * k + HH],
                                    XNT[:, CW * c:CW * c + CW], start=True, stop=True)
                ins.then_inc(sem("shared_up"), 1)

            def up(u):
                c, e = divmod(u, E)
                pe.wait_ge(sem("xsT"), u + 1)
                if e == 0:
                    pe.wait_ge(sem("shared_relu"), c + 1)
                else:
                    pe.wait_ge(sem("hrelu"), u)
                for k in range(2):
                    ins = pe.matmul(ps[0:HH, 2 + k, :], wup_bf[:, e, HH * k:HH * k + HH], xsT[:, u % 2, :],
                                    start=True, stop=True)
                ins.then_inc(sem("up_ps"), 1)

            def expert_down(u):
                c, e = divmod(u, E)
                pe.wait_ge(sem("hsq"), u + 1)
                if u >= 2:
                    pe.wait_ge(sem("eout"), u - 1)
                for t in range(TC):
                    for k in range(2):
                        ins = pe.matmul(ps[:, 4 + u % 2, P * t:P * t + P], hsq[:, u % 2, k, P * t:P * t + P],
                                        wdn_bf[:, e, k, :], start=(k == 0), stop=(k == 1))
                ins.then_inc(sem("down_ps"), 1)

            def shared_down(c):
                pe.wait_ge(sem("shared_sq"), c + 1)
                if c >= 2:
                    pe.wait_ge(sem("moe_out"), c - 1)
                for t in range(TC):
                    for k in range(2):
                        ins = pe.matmul(ps[:, 6 + c % 2, P * t:P * t + P], hs2[:, k, P * t:P * t + P],
                                        sdnT[:, k, :], start=(k == 0), stop=(k == 1))
                ins.then_inc(sem("shared_ps"), 1)

            spread_score(0)
            for u in range(CHUNKS * E):
                c, e = divmod(u, E)
                if e == 0:
                    shared_up(c)
                if u + 1 < CHUNKS * E:
                    spread_score(u + 1)
                up(u)
                if e == 0:
                    shared_down(c)
                expert_down(u)
            transpose_xn("post1")
            project(1, "post1")
            pe.wait_ge(sem("qk_full1"), 4)
            pe.wait_ge(sem("v_done1"), 8)
            attend(1, PLANS[1])
            project_out(1)
            pe_ffn(pe, sem, bank, ps, FF, XN, ident)


QK_BANK = (0, 4, 4, 0)
V_BANK = (0, 4)
POOL_CONSTS = 10
FFN_INPUTS = ("wr", "iota", "offset", "tri", "g1", "g2", "qkvT", "woutT", "w1T", "w2T", "w3T",
              "headmask", "mask2")
LATER = 14 + len(FFN_INPUTS)


def ffn_buffers(sb, full, rest, XNT, TMP, YT, arena):
    f = dict(
        wr=sb("wr", [P, C]), iota=sb("iota", [P, P]), offset=sb("offset", [P, TILES]),
        tri=sb("tri", [P, P]), g1=sb("g1", [P, C]), g2=sb("g2", [P, C]), qkvT=sb("qkvT", [C, 3 * C]),
        woutT=sb("woutT", [C, C]), w1T=sb("w1T", [C, FC * P]), w2T=sb("w2T", [C, FC * P]),
        w3T=sb("w3T", [P, FC, C]), headmask=sb("headmask", [P, H]), mask2=sb("mask2", [P, P]),
        score=sb("score", [P, TILES]), scoreT=sb("scoreT", [TILES, P]), count=sb("count", [P, TILES, 4]),
        rank=sb("rank", [P, TILES]), nsel=sb("nsel", [P, TILES]), slot=sb("slot", [P, TILES]),
        ssq=sb("ssq", [P, 2]), small=sb("small", [P, 4]),
       
        smax=sb("smax", [P, H]), sden=sb("sden", [P, H]),
       
    )
    f = {k: v[:] if len(v.shape) == 1 else v[(slice(None),) * len(v.shape)] for k, v in f.items()}
    f["score_row"] = full[:, :, :].rearrange("p a t -> p (a t)")
    for k, name in enumerate(("xs", "h", "hT", "qT", "kT", "v", "o", "oT", "x2", "xp")):
        f[name] = arena[:, P * (8 + k):P * (9 + k)]
    f["ga"], f["gb"] = arena[:, 0:FC * P], arena[:, FC * P:2 * FC * P]
    f["junk"] = rest[:, 0, :]
    f["sel"] = YT[:, :].rearrange("p (t s) -> p t s", t=TILES)
    f["selT"] = XNT[:, :]
    f["s"] = TMP[:, :, :]
    f["qm"] = YT[:, :].rearrange("p (h q) -> p h q", h=H)
    f["pT"] = rest[:, :, :].rearrange("p a t -> p (a t)").rearrange("p (h q) -> p h q", h=H)
    return f


def dve_ffn(dve, sem, bank, ps, f, XN, YB):
    step = sem("ffn_dve")
    n = [0]

    def link(ins):
        n[0] += 1
        ins.then_inc(step, 1)
        dve.wait_ge(step, n[0])

    for t in range(TILES):
        if t % TC == 0:
            dve.wait_ge(sem("normed"), TC * (norms_before("post2", 1, t // TC) + 1))
        if t:
            dve.wait_ge(sem("score"), t)
        dve.tensor_tensor_reduce(out=f["junk"][:, 0:C], in0=XN[:, t, :], in1=f["wr"], scale=1.0, scalar=0.0,
                                 op0=ALU.mult, op1=ALU.add, accum_out=f["score"][:, t:t + 1])\
            .then_inc(sem("score"), 1)
    dve.wait_ge(sem("score_in"), 16)
    dve.wait_ge(sem("score"), TILES)
    for t in range(TILES):
        b, k = divmod(t, KT)
        row = f["score_row"][:, T * b:T * b + T]
        mine = f["score"][:, t:t + 1]
        cnt = f["count"]
        own = slice(P * k, P * k + P)
        if k:
            link(dve.tensor_scalar(f["junk"][:, 0:P * k], row[:, 0:P * k], mine, None, ALU.is_ge, ALU.add,
                                   accum_out=cnt[:, t, 0:1]))
        if k < KT - 1:
            link(dve.tensor_scalar(f["junk"][:, P * k + P:T], row[:, P * k + P:T], mine, None, ALU.is_gt,
                                   ALU.add, accum_out=cnt[:, t, 1:2]))
        link(dve.tensor_scalar(f["junk"][:, own], row[:, own], mine, None, ALU.is_gt, ALU.add,
                               accum_out=cnt[:, t, 2:3]))
        link(dve.scalar_tensor_tensor(out=f["junk"][:, own], in0=row[:, own], scalar=mine, in1=f["tri"],
                                      op0=ALU.is_equal, op1=ALU.mult, accum_out=cnt[:, t, 3:4]))
    link(dve.tensor_reduce(f["rank"], f["count"], AX.X, ALU.add))
    link(dve.tensor_scalar(f["nsel"], f["rank"], TOP - 0.5, None, ALU.is_gt))
    link(dve.scalar_tensor_tensor(out=f["slot"], in0=f["nsel"], scalar=4096.0, in1=f["rank"],
                                  op0=ALU.mult, op1=ALU.add))
    link(dve.tensor_tensor(f["slot"], f["slot"], f["offset"], ALU.add))
    dve.tensor_tensor(f["sel"], f["iota"].unsqueeze(1).to_broadcast([P, TILES, P]),
                      f["slot"].unsqueeze(2).to_broadcast([P, TILES, P]), ALU.is_equal)\
        .then_inc(sem("sel"), 1)

    def rms(i, src, gain):
        dve.tensor_tensor_reduce(out=f["h"], in0=src, in1=src, scale=1.0, scalar=0.0, op0=ALU.mult,
                                 op1=ALU.add, accum_out=f["ssq"][:, i:i + 1]).then_inc(sem(f"ssq{i}"), 1)
        dve.wait_ge(sem(f"rms{i}"), 2)
        dve.scalar_tensor_tensor(out=f["h"], in0=src, scalar=f["small"][:, 2 * i + 1:2 * i + 2], in1=gain,
                                 op0=ALU.mult, op1=ALU.mult).then_inc(sem(f"rows{i}"), 1)

    dve.wait_ge(sem("xs_ps"), 1)
    link(dve.tensor_copy(f["xs"], ps[:, 0, 0:C]))
    rms(0, f["xs"], f["g1"])
    dve.wait_ge(sem("qT"), 1)
    dve.tensor_tensor(f["qm"], f["qT"].unsqueeze(1).to_broadcast([P, H, P]),
                      f["headmask"].unsqueeze(2).to_broadcast([P, H, P]), ALU.mult).then_inc(sem("qm"), 1)
    dve.wait_ge(sem("s_ps"), 1)
    link(dve.tensor_tensor(f["s"], bank(0, 4).rearrange("p (h k) -> p h k", h=H),
                           f["mask2"].unsqueeze(1).to_broadcast([P, H, P]), ALU.add))
    link(dve.tensor_reduce(f["smax"], f["s"], AX.X, ALU.max, negate=True))
    dve.tensor_tensor(f["s"], f["s"], f["smax"].unsqueeze(2).to_broadcast([P, H, P]), ALU.add)\
        .then_inc(sem("s_shifted"), 1)
    dve.wait_ge(sem("s_exp"), 1)
    link(dve.tensor_reduce(f["sden"], f["s"], AX.X, ALU.add))
    link(dve.reciprocal(f["sden"], f["sden"]))
    dve.wait_ge(sem("o_ps"), 1)
    dve.tensor_tensor(f["o"].rearrange("p (h d) -> p h d", h=H), ps[:, 0, 0:C].rearrange("p (h d) -> p h d", h=H),
                      f["sden"].unsqueeze(2).to_broadcast([P, H, DH]), ALU.mult).then_inc(sem("o"), 1)
    dve.wait_ge(sem("attn_ps"), 1)
    link(dve.tensor_tensor(f["x2"], f["xs"], ps[:, 2, 0:C], ALU.add))
    rms(1, f["x2"], f["g2"])
    dve.wait_ge(sem("ga_exp"), 1)
    link(dve.tensor_scalar(f["ga"], f["ga"], 1.0, None, ALU.add))
    link(dve.reciprocal(f["ga"], f["ga"]))
    link(dve.tensor_tensor(f["ga"], f["ga"], bank(4)[:, 0:FC * P], ALU.mult))
    dve.tensor_tensor(f["gb"], f["ga"], bank(5)[:, 0:FC * P], ALU.mult).then_inc(sem("gb"), 1)
    dve.wait_ge(sem("ff_ps"), 1)
    dve.tensor_tensor(f["xp"], f["x2"], ps[:, 6, 0:C], ALU.add).then_inc(sem("xp"), 1)
    for c in range(CHUNKS):
        dve.wait_ge(sem("back_ps"), c + 1)
        for t in range(TC):
            ins = dve.scalar_tensor_tensor(out=YB[:, TC * c + t, :], in0=XN[:, TC * c + t, :],
                                           scalar=f["nsel"][:, TC * c + t:TC * c + t + 1],
                                           in1=ps[:, c, P * t:P * t + P], op0=ALU.mult, op1=ALU.add)
            if t < TC - 1:
                link(ins)
        ins.then_inc(sem("ffn_out"), 1)


def act_ffn(act, sem, bank, ps, f):
    def copy(dst, src, wait, done, func=ACT.Copy, scale=1.0):
        act.wait_ge(sem(wait), 1)
        act.activation(dst, src, func, scale=scale).then_inc(sem(done), 1)

    copy(f["scoreT"], ps[0:TILES, 0, 0:P], "scoreT_ps", "scoreT")
    for c in range(CHUNKS):
        act.wait_ge(sem("selT_ps"), c + 1)
        act.activation(f["selT"][:, CW * c:CW * c + CW], bank(4 + c), ACT.Copy).then_inc(sem("selT"), 1)
    copy(f["hT"], ps[:, 1, 0:P], "hT_ps0", "hT0")
    copy(f["qT"], ps[:, 2, 0:P], "qkv_ps", "qT")
    copy(f["kT"], ps[:, 2, P:2 * P], "qkv_ps", "kT")
    copy(f["v"], ps[:, 2, 2 * P:3 * P], "qkv_ps", "v")
    act.wait_ge(sem("s_shifted"), 1)
    act.activation(f["s"], f["s"], ACT.Exp, scale=SCALE).then_inc(sem("s_exp"), 1)
    for c in range(4):
        act.wait_ge(sem("pT_ps"), c + 1)
        act.activation(f["pT"][:, 4 * c:4 * c + 4, :], bank(4 + c).rearrange("p (h q) -> p h q", h=4), ACT.Copy)\
            .then_inc(sem("pT"), 1)
    copy(f["oT"], ps[:, 1, 0:P], "oT_ps", "oT")
    copy(f["hT"], ps[:, 1, 0:P], "hT_ps1", "hT1")
    copy(f["ga"], bank(4)[:, 0:FC * P], "ga_ps", "ga_exp", ACT.Exp, -1.0)


def pe_ffn(pe, sem, bank, ps, f, XN, ident):
    pe.wait_ge(sem("score"), TILES)
    pe.transpose(ps[0:TILES, 0, 0:P], f["score"], ident[:, :]).then_inc(sem("scoreT_ps"), 1)
    pe.wait_ge(sem("sel"), 1)
    pe.wait_ge(sem("scoreT"), 1)
    for t in range(TILES):
        ins = pe.matmul(ps[:, 0, 0:C], f["sel"][:, t, :], XN[:, t, :], start=(t == 0), stop=(t == TILES - 1))
    ins.then_inc(sem("xs_ps"), 1)
    for c in range(CHUNKS):
        for t in range(TC):
            ins = pe.transpose(ps[:, 4 + c, P * t:P * t + P], f["sel"][:, TC * c + t, :], ident[:, :])
        ins.then_inc(sem("selT_ps"), 1)
    pe.wait_ge(sem("rows0"), 1)
    pe.transpose(ps[:, 1, 0:P], f["h"], ident[:, :]).then_inc(sem("hT_ps0"), 1)
    pe.wait_ge(sem("hT0"), 1)
    pe.matmul(ps[:, 2, 0:P], f["qkvT"][:, 0:C], f["hT"], start=True, stop=True)
    pe.matmul(ps[:, 2, P:2 * P], f["qkvT"][:, C:2 * C], f["hT"], start=True, stop=True)
    pe.matmul(ps[:, 2, 2 * P:3 * P], f["hT"], f["qkvT"][:, 2 * C:3 * C], start=True, stop=True)\
        .then_inc(sem("qkv_ps"), 1)
    pe.wait_ge(sem("qm"), 1)
    pe.wait_ge(sem("v"), 1)
    for h in range(H):
        ins = pe.matmul(bank(0, 4)[:, P * h:P * h + P], f["qm"][:, h, :], f["kT"], start=True, stop=True)
    ins.then_inc(sem("s_ps"), 1)
    pe.wait_ge(sem("s_exp"), 1)
    pe.wait_ge(sem("selT"), CHUNKS)
    for c in range(4):
        for h in range(4 * c, 4 * c + 4):
            ins = pe.transpose(ps[:, 4 + c, P * (h % 4):P * (h % 4) + P], f["s"][:, h, :], ident[:, :])
        ins.then_inc(sem("pT_ps"), 1)
    for h in range(H):
        pe.wait_ge(sem("pT"), h // 4 + 1)
        ins = pe.matmul(ps[:, 0, DH * h:DH * h + DH], f["pT"][:, h, :], f["v"][:, DH * h:DH * h + DH],
                        start=True, stop=True)
    ins.then_inc(sem("o_ps"), 1)
    pe.wait_ge(sem("o"), 1)
    pe.transpose(ps[:, 1, 0:P], f["o"], ident[:, :]).then_inc(sem("oT_ps"), 1)
    pe.wait_ge(sem("oT"), 1)
    pe.matmul(ps[:, 2, 0:C], f["oT"], f["woutT"], start=True, stop=True).then_inc(sem("attn_ps"), 1)
    pe.wait_ge(sem("rows1"), 1)
    pe.transpose(ps[:, 1, 0:P], f["h"], ident[:, :]).then_inc(sem("hT_ps1"), 1)
    pe.wait_ge(sem("hT1"), 1)
    for k in range(FC):
        pe.matmul(ps[:, 4, P * k:P * k + P], f["w1T"][:, P * k:P * k + P], f["hT"], start=True, stop=True)
    for k in range(FC):
        ins = pe.matmul(ps[:, 5, P * k:P * k + P], f["w2T"][:, P * k:P * k + P], f["hT"], start=True, stop=True)
    ins.then_inc(sem("ga_ps"), 1)
    pe.wait_ge(sem("gb"), 1)
    for k in range(FC):
        ins = pe.matmul(ps[:, 6, 0:C], f["gb"][:, P * k:P * k + P], f["w3T"][:, k, :], start=(k == 0),
                        stop=(k == FC - 1))
    ins.then_inc(sem("ff_ps"), 1)
    pe.wait_ge(sem("xp"), 1)
    for c in range(CHUNKS):
        for t in range(TC):
            ins = pe.matmul(ps[:, c, P * t:P * t + P], f["selT"][:, P * (TC * c + t):P * (TC * c + t) + P],
                            f["xp"], start=True, stop=True)
        ins.then_inc(sem("back_ps"), 1)


def layouts(i):
    def c(x):
        return np.ascontiguousarray(x)

    def rows(x):
        return c(np.broadcast_to(x, (P, x.shape[-1])))

    f4 = np.float32
    hd = np.arange(P) % DH
    inv = (1.0 / 10000.0 ** (np.arange(0, 4, 2, dtype=f4) / f4(4))).astype(f4)
    angle = (np.arange(T, dtype=f4)[:, None] * inv[None, :]).astype(f4)
    angle = np.concatenate((angle, angle), -1).astype(np.float64)
    cos, sin = np.ones((P, T), f4), np.zeros((P, T), f4)
    for p in range(P):
        if hd[p] >= 4:
            cos[p], sin[p] = np.cos(angle[:, hd[p] - 4]), np.sin(angle[:, hd[p] - 4])
    k = np.arange(P)
    after = k[None, :] > k[:, None]
    return {
        "x": c(i["L0_attn_x"].reshape(B * T, C)),
        "ident": np.eye(P, dtype=f4),
        "masks": c(np.stack([np.where(after, f4(NEG), f4(0)), np.where(after.T, f4(NEG), f4(0))], 1)),
        "upq": c(np.concatenate([i["L0_attn_Wq_up_c"], i["L0_attn_Wq_up_e"]], 1)),
        "upk": c(np.concatenate([i["L0_attn_Wk_up_c"], i["L0_attn_Wk_up_e"]], 1)),
        "upv": c(i["L0_attn_Wv_up"]),
        "down": c(np.stack([i[f"L0_attn_W{s}_down"].T.reshape(H, LAT, C).transpose(1, 0, 2) for s in "qkv"], 1)),
        "rope": c(np.stack([cos, sin], 1)),
        "wo0": c(i["L0_attn_Wc"]),
        "gateT": c(i["L0_ffn_gate_w"].T),
        "ebias": rows(i["L0_ffn_expert_bias"]),
        "before8": c(np.broadcast_to((np.arange(E)[None, :] < np.arange(E)[:, None]).astype(f4), (P, E, E))),
        "wupT": c(i["L0_ffn_w_up"].transpose(2, 0, 1).reshape(C, E * HID)),
        "wdnT": c(i["L0_ffn_w_down"].reshape(E, C, 2, HH).transpose(3, 0, 2, 1).reshape(HH, E * 2 * C)),
        "supT": c(i["L0_ffn_shared_w_up"].T),
        "sdnT": c(i["L0_ffn_shared_w_down"].reshape(C, 2, HH).transpose(2, 1, 0)),
        "wq1": c(i["L1_attn_Wq"].T), "wk1": c(i["L1_attn_Wk"].T), "wv1": c(i["L1_attn_Wv"].T),
        "wo1": c(i["L1_attn_Wo"].T),
        "bqk": c(np.stack([i["L1_attn_bq"], i["L1_attn_bk"]], 1)),
        "bvo": c(np.stack([i["L1_attn_bv"], i["L1_attn_bo"]], 0)[None]),
        "wr": rows(i["L1_ffn_w_router"]),
        "iota": c(np.broadcast_to(k.astype(f4), (P, P))),
        "offset": c(np.broadcast_to((np.arange(TILES) // KT * TOP).astype(f4), (P, TILES))),
        "tri": c((~after & (k[None, :] != k[:, None])).astype(f4)),
        "g1": rows(i["L1_ffn_g1"]), "g2": rows(i["L1_ffn_g2"]),
        "qkvT": c(i["L1_ffn_W_qkv"].T), "woutT": c(i["L1_ffn_W_out"].T),
        "w1T": c(np.pad(i["L1_ffn_W1"].T, ((0, 0), (0, FC * P - DFF)))),
        "w2T": c(np.pad(i["L1_ffn_W2"].T, ((0, 0), (0, FC * P - DFF)))),
        "w3T": c(np.pad(i["L1_ffn_W3"].T, ((0, FC * P - DFF), (0, 0))).reshape(FC, P, C).transpose(1, 0, 2)),
        "headmask": c((k[:, None] // DH == np.arange(H)[None, :]).astype(f4)),
        "mask2": c(np.where(after | (k[None, :] // TOP != k[:, None] // TOP), f4(NEG), f4(0))),
    }


def kernel(**inputs):
    import concourse.bacc as bacc
    from concourse.bass_utils import run_bass_kernel_spmd

    arrays = layouts({name: np.asarray(v) for name, v in inputs.items()})
    nc = bacc.Bacc("TRN2", target_bir_lowering=False, num_devices=1)
    a = {name: nc.dram_tensor(name + "_in", v.shape, mybir.dt.from_np(v.dtype), kind="ExternalInput").ap()
         for name, v in arrays.items()}
    out = nc.dram_tensor("out", (B * T, C), F32, kind="ExternalOutput").ap()
    build(nc, a, out)
    got = run_bass_kernel_spmd(nc, [{name + "_in": v for name, v in arrays.items()}], core_ids=[0])
    return got.results[0]["out"].reshape(B, T, C)
```

```python
from contextlib import ExitStack

import numpy as np

from concourse import mybir

F32 = mybir.dt.float32
BF16 = mybir.dt.bfloat16
ACT = mybir.ActivationFunctionType
ALU = mybir.AluOpType
AX = mybir.AxisListType

P = 128
B, T, C = 2, 1024, 128
H, DH, LAT = 16, 8, 64
TILES = B * T // P
CHUNKS = 4
TC = TILES // CHUNKS
CW = TC * P
G = 4
NG = B * H // G
KT = T // P
E, HID, HH = 8, 176, 88
TOP = 64
DFF, FC = 341, 3
SCALE = 1.0 / float(np.sqrt(DH))
LN_EPS, RMS_EPS = 1e-5, 1e-6
NEG = -1e30
Q_PARTS = (0, 0, 1, 1, 0, 2)
K_PARTS = (0, 1, 0, 1, 2, 0)
NPROD = len(Q_PARTS)
STACK = DH * NPROD
STACK_M = STACK + 3
VW = DH + 1
JOBS = KT * G


JOB_COST = 0.5


class Plan:

    def __init__(self, causal):
        self.causal = causal
        self.done_by = (1, 1, 2, 3, 4) if causal else (0, 0, 0, 0, 4)
        self.steps = [(qh, kt) for qh in range(2) for kt in range(4 * qh + 4 if causal else KT)]
        self.n = len(self.steps)
        self.jobs = [(qt, j) for qt in range(KT) for j in range(G)]
        job_cost = [self.keys(qt) // P + JOB_COST for qt, _ in self.jobs]
        step_cost = [4 - self.skipped(qh, kt) // P for qh, kt in self.steps]
        self.beside, at, done = [], 0, 0.0
        for i in range(self.n):
            done += step_cost[i] * sum(job_cost) / sum(step_cost)
            upto = at
            while upto < JOBS and (sum(job_cost[:upto + 1]) <= done + 1e-6 or i == self.n - 1):
                upto += 1
            self.beside.append(list(range(at, upto)))
            at = upto
        self.half = next(i for i, (qh, _) in enumerate(self.steps) if qh == 1)
        first_max = next(i for i, b in enumerate(self.beside) if JOBS // 2 - 1 in b)
        self.small = {1: "max1", 2: "out1", self.half + 1: "out0",
                      max(self.half + 2, first_max + 2): "max0"}
        assert len(self.small) == 4 and max(self.small) < self.n

    def keys(self, qt):
        return (qt + 1) * P if self.causal else T

    def single(self, jj):
        return self.causal and self.jobs[jj][0] < 4

    def first_bank(self, jj):
        return jj % 4 if self.single(jj) else 2 * (jj % 2)

    def maxima_before(self, jj):
        if self.single(jj):
            return (-1, -1, 0, 0)[jj] if jj < 4 else jj - 3
        if jj and self.single(jj - 1):
            return jj - 2
        if jj > 1 and self.single(jj - 2):
            return jj - 1
        return jj - 1

    def skipped(self, qh, kt):
        return max(0, kt * P - qh * 512) if self.causal else 0

    def diagonal(self, qh, kt):
        return self.causal and kt * P >= qh * 512


PLANS = (Plan(True), Plan(False))
NORMS = {("ln0", 1): 0, ("post0", 0): 1, ("post0", 1): 2, ("post1", 0): 3, ("post1", 1): 4,
         ("post2", 0): 5, ("post2", 1): 6, ("post3", 0): 7}
ADDS = {"post0": 0, "post1": 1, "post2": 2, "post3": 3}
TURNED = {"ln0": 0, "post0": 1, "post1": 2}


def norms_before(name, half, c):
    if name == "post1":
        return CHUNKS * NORMS[name, 0] + (2 * c + half if c < 2 else 2 * half + c + 2)
    return CHUNKS * NORMS[name, half] + c


def adds_before(name, c):
    return CHUNKS * ADDS[name] + c


def turned_before(name, c):
    return CHUNKS * TURNED[name] + c - (2 if name == "post1" else 0)


UNITS = [(kind, c * E + e if kind == "expert" else c) for c in range(CHUNKS)
         for kind, e in [("shared", 0)] + [("expert", e) for e in range(E)]]
for _at, _unit in ((8, ("parts", 1)), (15, ("back", 0)), (16, ("parts", 2)), (19, ("parts", 3)), (24, ("turn", 0)),
                   (27, ("back", 1)), (36, ("turn", 1)), (38, ("back", 2)), (39, ("q", 0)), (41, ("k", 1)),
                   (43, ("v", 0))):
    UNITS.insert(_at, _unit)
HALVES = [1 if _kind in ("parts", "back", "turn") else 2 for _kind, _ in UNITS]
SPREAD_BANK = (0, 4)


def unit(kind, n):
    return UNITS.index((kind, n))


def halves_before(v):
    return sum(HALVES[:v])


def through(kind, n):
    return halves_before(unit(kind, n) + 1)


def half_bank(h):
    return 1 + h % 3


def expert(v):
    return UNITS[v][1] if 0 <= v < len(UNITS) and UNITS[v][0] == "expert" else None


BESIDE_EXPERTS = {17: ("moments", 0, 0), 19: ("norm", 0, 0), 21: ("moments", 1, 0), 23: ("norm", 1, 0),
                  29: ("moments", 0, 1), 31: ("norm", 0, 1), 33: ("moments", 1, 1), 35: ("norm", 1, 1),
                  40: ("moments", 0, 2), 42: ("norm", 0, 2), 44: ("part", 0, 0), 46: ("part", 0, 1)}
ROUTE_AT = {1: 1, 2: 6, 3: 11}
ROUTE_STEPS = 9
BESIDE_FIRST = {"moments0": 0, "norm0": 0, "moments1": 0, "norm1": 0, "turn": 0, "q": 0, "k": 3, "v": 6,
                "part2": 4, "part3": 8}


def qk_full(L, w):
    if L == 0:
        return "qk_full0", w + 1
    return ("unit_read", through("qk"[w], w)) if w < 2 else ("qk_full1", w - 1)


def values_done(L, b):
    if L == 0:
        return "v_done0", 4 * b + 4
    return ("unit_read", through("v", 0)) if b == 0 else ("v_done1", 4)


def rounded_by_dve(u):
    return u % 4 == 3


TURN = {"max1": 0, "out1": 1, "out0": 2, "max0": 3}


def turn(kind, n, first=False):
    if first:
        return {"max1": 1, "out0": 2, "max0": 3}[kind]
    return 4 * n + TURN[kind]


def second_bank(j, last):
    return j if last else 4 + j % 2


def periods(eng, emit, last=NG - 1):
    emit(0, 0, 0, True, False)
    with eng.Fori(0, (NG - 2) // 2) as i:
        emit(2 * i + 1, 1, i, False, False)
        emit(2 * i + 2, 0, i + 1, False, False)
    emit(NG - 1, 1, NG // 2 - 1, False, True)


def build(nc, a, out):
    ctx = ExitStack()
    with ctx:
        sems = {}

        def sb(name, shape, dt=F32):
            return ctx.enter_context(nc.sbuf_tensor(name, shape, dt))

        def sem(name):
            if name not in sems:
                sems[name] = ctx.enter_context(nc.semaphore(name))
            return sems[name]

        def dram(name, shape, dt):
            return nc.dram_tensor(name, shape, dt, kind="Internal").ap()

        X = sb("X", [P, TILES, C])
        XN = sb("XN", [P, TILES, C])
        XNT = sb("XNT", [P, TILES * P])
        TMP = sb("TMP", [P, TILES, C])
        Y = sb("Y", [P, KT, NG, G * DH])
        YB = Y[:, :, :, :].rearrange("p k n d -> p (k n d)").rearrange("p (t c) -> p t c", t=TILES)
        YT = sb("YT", [P, TILES * P])
        bn = sb("bn", [P, TILES, 6])
        mv = sb("mv", [P, TILES, 2])
        veps = sb("veps", [P, TILES])
        rstd = sb("rstd", [P, TILES])
        neg_half = sb("neg_half", [P, TILES])
        ident = sb("ident", [P, P])
        masks = sb("masks", [P, 2, P])
        ident_bf = sb("ident_bf", [P, P], BF16)
        mask_bf = sb("mask_bf", [P, 2, P], BF16)
        ones_row = sb("ones_row", [1, P])
        rope = TMP[:, :, :].rearrange("p t c -> p (t c)").rearrange("p (a t) -> p a t", a=2)
        arena = sb("arena", [P, 6144])
        down = arena[0:LAT, :].rearrange("p (s h c) -> p s h c", s=3, h=H)
        parts = [arena[:, :].bitcast(BF16).rearrange("p (u k t) -> p u k t", u=4, k=3)[:, w ^ 2 * L]
                 for L in range(2) for w in range(4)]
        ups = sb("ups", [LAT, 5, DH])
        wqk = [sb(f"wqk{i}", [C, 2, 2, H * DH]) for i in range(2)]
        wv = [sb(f"wv{i}", [C, H * DH]) for i in range(2)]
        wo = [sb(f"wo{i}", [C, C]) for i in range(2)]
        bqk = sb("bqk", [P, 2])
        bvo = sb("bvo", [1, 2, C])
        full = sb("full", [P, 2, T])
        rest = sb("rest", [P, 2, T])
        Vx = sb("Vx", [P, NG, KT, G, VW])
        SQ, TQ = (sb(n, [P, 2, G, T], BF16) for n in ("SQ", "TQ"))
        SK, TK = (sb(n, [P, 2, G // 2, T], BF16) for n in ("SK", "TK"))
        VS = sb("VS", [P, 2, KT, G, VW])
        probs = sb("probs", [P, 2, G, 512])
        nmax = sb("nmax", [P, 2, 2, 2, 8])
        nmax_rest = sb("nmax_rest", [P, 2, 2, 2, 8])
        nmax3_cols = sb("nmax3", [P, 2, 2, P], BF16)
        nmax3 = nmax3_cols[:, :, :, 0:48].rearrange("p g h (e i x) -> p g h e i x", e=2, i=3)
        zeros = sb("zeros", [P, 16])
        nmaxT = sb("nmaxT", [48, 2, 2, P], BF16)
        OS = sb("OS", [P, 2, 512])
        rden = sb("rden", [P, 2, 16])
        gateT = sb("gateT", [C, E])
        ebias = sb("ebias", [P, E])
        before8 = sb("before8", [P, E, E])
        moe_f = probs[:, :, :, :].rearrange("p a j q -> p (a j q)")[:, 0:E * (HID + 2 * C)]
        moe_b = sb("moe_b", [P, E * (HID + 2 * C)], BF16)
        wup_bf = moe_b[:, 0:E * HID].rearrange("p (e h) -> p e h", e=E)
        wdn_bf = moe_b[0:HH, E * HID:].rearrange("p (e k c) -> p e k c", e=E, k=2)
        supT = sb("supT", [C, HID])
        sdnT = sb("sdnT", [HH, 2, C])
        esc = sb("esc", [P, TILES, E])
        ebi = sb("ebi", [P, TILES, E])
        erank = sb("erank", [P, TILES, E])
        chosen = sb("chosen", [P, TILES, E])
        pick = sb("pick", [P, E])
        pick_bf = sb("pick_bf", [P, E], BF16)
        arena_bf = arena[:, :].bitcast(BF16)
        xsT = arena_bf[:, 0:2 * CW].rearrange("p (u q) -> p u q", u=2)
        eout = arena_bf[:, 2 * CW:4 * CW].rearrange("p (u q) -> p u q", u=2)
        hrelu = arena_bf[0:HH, 4 * CW:8 * CW].rearrange("p (u k q) -> p u k q", u=2, k=2)
        hsq = arena_bf[0:HH, 8 * CW:12 * CW].rearrange("p (u k q) -> p u k q", u=2, k=2)
        cmp = arena[:, 3072:3072 + 2 * TILES * E * E].rearrange("p (x t e j) -> p x t e j", x=2, t=TILES, e=E)
        esc3_cols = arena_bf[:, 20 * CW:24 * CW].rearrange("p (t x) -> p t x", t=TILES)
        esc3 = esc3_cols[:, :, 0:3 * E].rearrange("p t (e i) -> p t e i", e=E)
        esc_rest = probs[:, 0, 2, 0:TILES * E].rearrange("p (t e) -> p t e", t=TILES)
        esc3T = YT[:, :].bitcast(BF16)[:, 0:B * T]
        hs = probs[0:HH, 0, 0:2, :]
        hs2 = probs[0:HH, 1, 0:2, :]

        ps = ctx.enter_context(nc.psum_tensor("ps", [P, 8, 512], F32))

        def bank(i, n=1):
            return ps[:, i:i + n, :].rearrange("p a b -> p (a b)")

        split_d = [dram(f"split{i}", [2, B, 3, P, T], BF16) for i in range(2)]
        stack_d = [dram(f"stack{i}", [2, NG, 2, P, T], BF16) for i in range(2)]
        nmax_d = [dram(f"nmaxd{i}", [2, 2, 48, P], BF16) for i in range(2)]

        FF = ffn_buffers(sb, full, rest, XNT, TMP, YT, arena)

        block = ctx.enter_context(nc.Block())

        @block.sync
        def _(sp):
            sp.dma_start(X[:, :, :], a["x"].rearrange("(t p) c -> p t c", p=P)).then_inc(sem("x_in"), 16)
            for dst, src in ((ident[:, :], a["ident"]), (masks[:, :, :], a["masks"])):
                sp.dma_start(dst, src).then_inc(sem("const_in"), 16)
            sp.dma_start(ups[:, 0, :], a["upq"]).then_inc(sem("w0_in"), 16)
            sp.dma_start(ups[:, 2, :], a["upk"]).then_inc(sem("w0_in"), 16)
            sp.dma_start(ups[:, 4, :], a["upv"]).then_inc(sem("w0_in"), 16)
            sp.dma_start(down, a["down"]).then_inc(sem("w0_in"), 16)
            sp.dma_start(rope, a["rope"]).then_inc(sem("rope_in"), 16)
            later = [(wo[0][:, :], "wo0"), (gateT[:, :], "gateT"), (pick[:, :], "pick"), (ebias[:, :], "ebias"),
                     (before8[:, :, :], "before8"), 
                     (moe_f[:, 0:E * HID], "wupT"), (moe_f[0:HH, E * HID:], "wdnT"),
                     (supT[:, :], "supT"), (sdnT[:, :, :], "sdnT"),
                     (wqk[1][:, 0, 0, :], "wq1"), (wqk[1][:, 1, 0, :], "wk1"), (wv[1][:, :], "wv1"),
                     (wo[1][:, :], "wo1"), (bqk[:, :], "bqk"), (bvo[:, :, :], "bvo")]
            later += [(FF[k], k) for k in FFN_INPUTS]
            for dst, key in later:
                sp.dma_start(dst, a[key]).then_inc(sem("later_in"), 16)
            assert len(later) == LATER

            def restack(L, w):
                b, side = w // 2, w % 2
                sp.wait_ge(sem(f"split_done{L}"), w + 1)
                sp.dma_start(split_d[L][side, b].rearrange("k p t -> p k t"), parts[4 * L + w])\
                    .then_inc(sem(f"split_out{L}{w}"), 16)

            def products(L, w):
                b, side = w // 2, w % 2
                sp.wait_ge(sem(f"split_out{L}{w}"), 16)
                rows = stack_d[L][side, NG // 2 * b:NG // 2 * (b + 1)]\
                    .rearrange("g r (e s) t -> (g r e) s t", e=2)
                for i, k in enumerate((Q_PARTS, K_PARTS)[side]):
                    sp.dma_start(rows[:, DH * i:DH * (i + 1), :],
                                 split_d[L][side, b, k].rearrange("(h d) t -> h d t", d=DH))\
                        .then_inc(sem(f"stacked{L}{b}"), 16)

            def load_first(L, n, par):
                for side, dst in ((0, SQ), (1, SK)):
                    for e in range(2):
                        heads = slice(e, G, 2) if side == 0 else slice(0, G // 2)
                        sp.dma_start(dst[64 * e:64 * e + STACK, par, heads, :],
                                     stack_d[L][side, n, :, 64 * e:64 * e + STACK, :]
                                     .rearrange("r s t -> s r t")).then_inc(sem(f"first_in{L}{par}"), 16)

            def load_second(L, n, par):
                for side, dst in ((0, TQ), (1, TK)):
                    for e in range(2):
                        heads = slice(e, G, 2) if side == 0 else slice(0, G // 2)
                        sp.dma_start(dst[64 * e:64 * e + STACK, par, heads, :],
                                     stack_d[L][side, n, :, 64 * e:64 * e + STACK, :]
                                     .rearrange("r s t -> s r t")).then_inc(sem(f"second_in{L}{par}"), 16)
                sp.dma_start(VS[:, par].rearrange("p k j v -> p (k j v)"),
                             Vx[:, n].rearrange("p k j v -> p (k j v)")).then_inc(sem(f"second_in{L}{par}"), 16)

            def place_max(L, turns, n, par, qh):
                sp.wait_ge(sem(f"small_done{L}"), turns + 1)
                sp.dma_start(nmax_d[L][par, qh], nmaxT[:, par, qh, :]).then_inc(sem(f"max_out{L}{qh}"), 16)
                sp.wait_ge(sem(f"max_out{L}{qh}"), 16 * (n + 1))
                for e in range(2):
                    sp.dma_start(TQ[64 * e + STACK:64 * e + STACK_M, par, e:G:2, 512 * qh:512 * qh + 512],
                                 nmax_d[L][par, qh, 24 * e:24 * e + 24, :]
                                 .rearrange("(i r q) t -> i r (q t)", i=3, r=2))\
                        .then_inc(sem(f"max_in{L}{qh}"), 16)

            for L, plan in enumerate(PLANS):
                if L == 0:
                    sp.wait_ge(sem("pool_const"), POOL_CONSTS)
                restack(L, 0)
                restack(L, 1)
                products(L, 0)
                products(L, 1)
                sp.wait_ge(sem(f"stacked{L}0"), 32 * NPROD)
                load_first(L, 0, 0)
                load_first(L, 1, 1)
                name, value = values_done(L, 0)
                sp.wait_ge(sem(name), value)
                load_second(L, 0, 0)
                load_second(L, 1, 1)
                place_max(L, 0, 0, 0, 0)
                restack(L, 2)
                restack(L, 3)
                products(L, 2)
                products(L, 3)

                def period(n, par, first=False, more_first=True, more_second=True, last=False):
                    if more_first and par == 0:
                        if not first:
                            sp.wait_ge(sem(f"stacked{L}1"), 32 * NPROD)
                            name, value = values_done(L, 1)
                            sp.wait_ge(sem(name), value)
                    if more_first:
                        sp.wait_ge(sem(f"rowmax{L}"), JOBS * (n + 1))
                        load_first(L, n + 2, par)
                    if not first and more_second:
                        sp.wait_ge(sem(f"pv{L}"), plan.n * n)
                        load_second(L, n + 1, 1 - par)
                    place_max(L, turn("max1", n, first), n, par, 1)
                    if not last:
                        place_max(L, turn("max0", n, first), n + 1, 1 - par, 0)

                period(0, 0, first=True)
                with sp.Fori(0, 2) as i:
                    period(2 * i + 1, 1)
                    period(2 * i + 2, 0)
                period(5, 1)
                period(6, 0, more_first=False)
                period(7, 1, more_first=False, more_second=False, last=True)

            for c in range(CHUNKS):
                sp.wait_ge(sem("x_added"), adds_before("post3", c) + 1)
                sp.dma_start(out.rearrange("(t p) c -> p t c", p=P)[:, TC * c:TC * c + TC, :],
                             X[:, TC * c:TC * c + TC, :]).then_inc(sem("stored"), 16)
            sp.wait_ge(sem("stored"), 16 * CHUNKS)

        @block.gpsimd
        def _(pool):
            n_const = 0
            for dst, v in ((neg_half[:, :], -0.5), (zeros[:, :], 0.0), (TK[:, :, :, :], 1.0), (Vx[:, :, :, :, :], 1.0),
                           (ones_row[:, :], 1.0), (FF["count"], 0.0), (nmax3_cols[:, :, :, :], 0.0),
                           (SK[:, :, :, :].bitcast(F32), 0.0), (SQ[:, :, :, :].bitcast(F32), 0.0),
                           (TQ[:, :, :, :].bitcast(F32), 0.0)):
                pool.memset(dst, v).then_inc(sem("pool_const"), 1)
                n_const += 1
            assert n_const == POOL_CONSTS
            pool.wait_ge(sem("pool_const"), POOL_CONSTS)

            def inv_std(name, c, half):
                done, k = sem("norm_rstd"), norms_before(name, half, c)
                t = slice(TC * c, TC * c + TC)
                pool.wait_ge(sem("norm_stats"), k + 1)
                pool.tensor_scalar(veps[:, t], mv[:, t, 1], LN_EPS, None, ALU.add).then_inc(done, 1)
                pool.wait_ge(done, 2 * k + 1)
                pool.tensor_tensor(rstd[:, t], veps[:, t], neg_half[:, t], ALU.pow).then_inc(done, 1)

            def residual(name, c):
                pool.wait_ge(sem("normed"), TC * (norms_before(name, 0, c) + 1))
                t = slice(TC * c, TC * c + TC)
                pool.tensor_tensor(X[:, t, :], X[:, t, :], TMP[:, t, :], ALU.add)\
                    .then_inc(sem("x_added"), 1)

            def post(name, more):
                for c in range(CHUNKS):
                    inv_std(name, c, 0)
                for c in range(CHUNKS):
                    residual(name, c)
                if more:
                    for c in range(CHUNKS):
                        inv_std(name, c, 1)

            def split(L, w):
                pool.wait_ge(sem(f"part0_{L}"), w + 1)
                pool.tensor_tensor(rest[:, w % 2, :], full[:, w % 2, :], parts[4 * L + w][:, 0, :],
                                   ALU.subtract).then_inc(sem(f"rest_{L}"), 1)

            def split_max(L):
                step = sem(f"max3_{L}")
                zero = zeros[:, :].rearrange("p (e x) -> p e x", e=2)

                def one(n, par):
                    for qh in range(2):
                        at = 8 * n + 4 * qh
                        src, left = nmax[:, par, qh], nmax_rest[:, par, qh]
                        dst = nmax3[:, par, qh]
                        pool.wait_ge(sem(f"rowmax{L}"), JOBS * n + JOBS // 2 * (qh + 1))
                        pool.tensor_tensor(dst[:, :, 0, :], src, zero, ALU.add).then_inc(step, 1)
                        pool.wait_ge(step, at + 1)
                        pool.tensor_tensor(left, src, dst[:, :, 0, :], ALU.subtract).then_inc(step, 1)
                        pool.wait_ge(step, at + 2)
                        pool.tensor_tensor(dst[:, :, 1, :], left, zero, ALU.add).then_inc(step, 1)
                        pool.wait_ge(step, at + 3)
                        pool.tensor_tensor(dst[:, :, 2, :], left, dst[:, :, 1, :], ALU.subtract)\
                            .then_inc(step, 1)

                with pool.Fori(0, NG // 2) as i:
                    one(2 * i, 0)
                    one(2 * i + 1, 1)

            for c in range(CHUNKS):
                inv_std("ln0", c, 1)
            for w in range(4):
                split(0, w)
            split_max(0)
            post("post0", True)
            pool.memset(esc3_cols.bitcast(F32), 0.0).then_inc(sem("score3_zero"), 1)
            pool.wait_ge(sem("score3_zero"), 1)
            def score_parts(c):
                t, n = slice(TC * c, TC * c + TC), 5 * c
                src, left = esc[:, t], esc_rest[:, t]
                no_score = zeros[:, 0:E].unsqueeze(1).to_broadcast([P, TC, E])
                step = sem("score3")
                pool.wait_ge(sem("chosen"), c + 1)
                pool.tensor_tensor(esc3[:, t, :, 0], src, no_score, ALU.add).then_inc(step, 1)
                pool.wait_ge(step, n + 1)
                pool.tensor_tensor(left, src, esc3[:, t, :, 0], ALU.subtract).then_inc(step, 1)
                pool.wait_ge(step, n + 2)
                pool.tensor_tensor(esc3[:, t, :, 1], left, no_score, ALU.add).then_inc(step, 1)
                pool.wait_ge(step, n + 3)
                pool.tensor_tensor(left, left, esc3[:, t, :, 1], ALU.subtract).then_inc(step, 1)
                pool.wait_ge(step, n + 4)
                pool.tensor_tensor(esc3[:, t, :, 2], left, no_score, ALU.add).then_inc(step, 1)

            def shared_square(c):
                pool.wait_ge(sem("unit_read"), through("shared", c))
                if c:
                    pool.wait_ge(sem("shared_ps"), c)
                pool.tensor_tensor(hs2, hs, hs, ALU.mult).then_inc(sem("shared_sq"), 1)

            score_parts(0)
            shared_square(0)
            score_parts(1)
            shared_square(1)
            score_parts(2)
            score_parts(3)
            inv_std("post1", 0, 0)
            residual("post1", 0)
            inv_std("post1", 0, 1)
            shared_square(2)
            inv_std("post1", 1, 0)
            residual("post1", 1)
            inv_std("post1", 1, 1)
            shared_square(3)
            inv_std("post1", 2, 0)
            residual("post1", 2)
            split(1, 0)
            split(1, 1)
            inv_std("post1", 3, 0)
            residual("post1", 3)
            inv_std("post1", 2, 1)
            inv_std("post1", 3, 1)
            split(1, 2)
            split(1, 3)
            split_max(1)
            post("post2", True)
            for i in range(2):
                pool.wait_ge(sem(f"ssq{i}"), 1)
                pool.tensor_scalar(FF["small"][:, 2 * i:2 * i + 1], FF["ssq"][:, i:i + 1], 1.0 / C, RMS_EPS,
                                   ALU.mult, ALU.add).then_inc(sem(f"rms{i}"), 1)
                pool.wait_ge(sem(f"rms{i}"), 1)
                pool.tensor_tensor(FF["small"][:, 2 * i + 1:2 * i + 2], FF["small"][:, 2 * i:2 * i + 1],
                                   neg_half[:, 0:1], ALU.pow).then_inc(sem(f"rms{i}"), 1)
            post("post3", False)

        @block.scalar
        def _(act):
            act.wait_ge(sem("const_in"), 32)
            act.activation(ident_bf[:, :], ident[:, :], ACT.Copy).then_inc(sem("act_const"), 1)
            act.activation(mask_bf[:, :, :], masks[:, :, :], ACT.Copy).then_inc(sem("act_const"), 1)

            def to_xnT(name, banks, chunks=range(CHUNKS)):
                for c in chunks:
                    act.wait_ge(sem("xnT_ps"), turned_before(name, c) + 1)
                    act.activation(XNT[:, CW * c:CW * c + CW], bank(banks[c]), ACT.Copy)\
                        .then_inc(sem("xnT"), 1)

            def q_or_k(w, at, ready, count, done):
                act.wait_ge(sem(ready), count)
                if w >= 2:
                    act.wait_ge(sem("split_done1"), w - 1)
                act.activation(full[:, w % 2, :], bank(at, 2), ACT.Identity,
                               bias=bqk[:, w % 2:w % 2 + 1]).then_inc(sem(done), 1)

            def part(L, w, k):
                name, value = qk_full(L, w) if k == 0 else (f"rest_{L}", w + 1)
                act.wait_ge(sem(name), value)
                act.activation(parts[4 * L + w][:, k, :], (full, rest)[k][:, w % 2, :], ACT.Copy)\
                    .then_inc(sem(f"part{k}_{L}"), 1)

            def values(L, b, at):
                v = bank(at, 2).rearrange("p (k g j d) -> p k g j d", k=KT, g=G, j=G)
                return [act.activation(Vx[:, G * b + g, :, :, 0:DH], v[:, :, g], ACT.Copy) for g in range(G)]

            def attend(L, plan):
                exps, pv, ev = sem(f"exp{L}"), sem(f"pv{L}"), sem(f"out_copied{L}")

                def copy_out(qh, turns, n_pv):
                    act.wait_ge(pv, n_pv)
                    act.activation(OS[:, qh, :], bank(6), ACT.Copy).then_inc(ev, 1)

                def period(n, par, rounds, first, last):
                    for s, (qh, kt) in enumerate(plan.steps):
                        c0 = plan.skipped(qh, kt)
                        for j in range(G):
                            act.wait_ge(sem(f"second_ps{L}"), (plan.n * n + s) * G + j + 1)
                            if j == 0 and not (first and s < 2):
                                act.wait_ge(pv, plan.n * n + s - 1)
                            act.activation(probs[:, s % 2, j, c0:512], ps[:, second_bank(j, last), c0:512],
                                           ACT.Exp, scale=SCALE).then_inc(exps, 1)
                        if s == 0 and not first:
                            copy_out(1, None, plan.n * n)
                        if s == plan.half:
                            copy_out(0, None, plan.n * n + plan.half)

                periods(act, period)
                copy_out(1, None, plan.n * NG)

            def copy_yT(L):
                for c in range(CHUNKS):
                    act.wait_ge(sem(f"yT_ps{L}"), c + 1)
                    act.activation(YT[:, CW * c:CW * c + CW], bank(c), ACT.Copy).then_inc(sem(f"yT{L}"), 1)

            to_xnT("ln0", LN0_BANK, range(2))
            part(0, 0, 0)
            part(0, 1, 0)
            part(0, 0, 1)
            part(0, 1, 1)
            act.wait_ge(sem("v_ps0"), 1)
            for ins in values(0, 0, V_BANK[0][0]):
                ins.then_inc(sem("v_done0"), 1)
            to_xnT("ln0", LN0_BANK, range(2, CHUNKS))
            part(0, 2, 0)
            part(0, 3, 0)
            part(0, 2, 1)
            part(0, 3, 1)
            act.wait_ge(sem("v_ps0"), 2)
            for ins in values(0, 1, V_BANK[0][1]):
                ins.then_inc(sem("v_done0"), 1)
            act.wait_ge(sem("later_in"), 16 * LATER)
            act.activation(moe_b[:, 0:E * HID], moe_f[:, 0:E * HID], ACT.Copy).then_inc(sem("moe_bf"), 1)
            act.activation(moe_b[0:HH, E * HID:], moe_f[0:HH, E * HID:], ACT.Copy).then_inc(sem("moe_bf"), 1)
            act.wait_ge(sem("moe_bf"), 2)
            act.activation(pick_bf[:, :], pick[:, :], ACT.Copy).then_inc(sem("moe_bf"), 1)
            attend(0, PLANS[0])
            copy_yT(0)
            def gate_exp(c):
                act.wait_ge(sem("gate_ps"), c + 1)
                act.activation(esc[:, TC * c:TC * c + TC, :].rearrange("p t e -> p (t e)"),
                               bank(4 + c)[:, 0:TC * E], ACT.Exp, scale=-1.0).then_inc(sem("gate_exp"), 1)

            for c in range(CHUNKS):
                to_xnT("post0", range(CHUNKS), [c])
                if c:
                    gate_exp(c - 1)
            gate_exp(CHUNKS - 1)

            def copy_parts(at, c):
                return act.activation(esc3T[:, CW * c:CW * c + CW], bank(at).bitcast(BF16)[:, 0:CW], ACT.Copy)

            act.wait_ge(sem("esc3T_ps"), 1)
            copy_parts(0, 0).then_inc(sem("esc3T"), 1)

            def read_unit(v):
                kind, n = UNITS[v]
                for k in range(HALVES[v]):
                    h = halves_before(v) + k
                    src = bank(half_bank(h))
                    act.wait_ge(sem("unit_ps"), h + 1)
                    if kind == "shared":
                        if n and k == 0:
                            act.wait_ge(sem("shared_sq"), n)
                        ins = act.activation(hs[:, k, :], src[0:HH, :], ACT.Relu)
                    elif kind == "expert":
                        if n >= 2 and k == 0:
                            act.wait_ge(sem("hsq"), n - 1)
                        ins = act.activation(hrelu[:, n % 2, k, :], src[0:HH, :], ACT.Relu)
                    elif kind == "parts":
                        ins = copy_parts(half_bank(h), n)
                    elif kind == "turn":
                        ins = act.activation(XNT[:, CW * n:CW * n + CW], src, ACT.Copy)
                    elif kind == "back":
                        ins = act.activation(YB[:, TC * n:TC * n + TC, :], src.rearrange("p (t c) -> p t c", t=TC),
                                             ACT.Copy)
                    elif kind == "v":
                        for g in range(G):
                            ins = act.activation(Vx[:, G * n + g, TC * k:TC * k + TC, :, 0:DH],
                                                 src.rearrange("p (k g j d) -> p k g j d", k=TC, g=G, j=G)[:, :, g],
                                                 ACT.Copy)
                    else:
                        ins = act.activation(full[:, n, CW * k:CW * k + CW], src, ACT.Identity,
                                             bias=bqk[:, n:n + 1])
                    ins.then_inc(sem("unit_read"), 1)

            def round_out(u):
                act.wait_ge(sem("down_ps"), u + 1)
                if u >= 2:
                    act.wait_ge(sem("eacc"), u - 1)
                act.activation(eout[:, u % 2, :], bank(5 + u % 2), ACT.Copy).then_inc(sem("eout_act"), 1)

            for i in range(len(UNITS) + 6):
                if i < len(UNITS):
                    read_unit(i)
                if i in (unit("q", 0), unit("k", 1)):
                    part(1, UNITS[i][1], 0)
                if i == unit("k", 1) + 1:
                    part(1, 0, 1)
                if i == unit("k", 1) + 3:
                    part(1, 1, 1)
                u = expert(i - 3)
                if u is not None and not rounded_by_dve(u):
                    round_out(u)
                u = expert(i - 5)
                if u is not None and u % E == E - 1:
                    c = u // E
                    act.wait_ge(sem("eacc"), u + 1)
                    act.activation(OS[:, c % 2, :], bank(7), ACT.Copy).then_inc(sem("moe_sum"), 1)
            to_xnT("post1", TURN_BANK, range(2, CHUNKS))
            q_or_k(2, QK_BANK[1][2], "qk_ps1", 1, "qk_full1")
            part(1, 2, 0)
            q_or_k(3, QK_BANK[1][3], "qk_ps1", 2, "qk_full1")
            part(1, 3, 0)
            part(1, 2, 1)
            act.wait_ge(sem("v_ps1"), 1)
            for ins in values(1, 1, V_BANK[1][1]):
                ins.then_inc(sem("v_done1"), 1)
            part(1, 3, 1)
            attend(1, PLANS[1])
            copy_yT(1)
            act_ffn(act, sem, bank, ps, FF)

        @block.vector
        def _(dve):
            def moments(name, half, c, src):
                st, k = sem("norm_bn"), norms_before(name, half, c)
                for t in range(TC):
                    dve.bn_stats(bn[:, TC * c + t, :], src(c, t)).then_inc(st, 1)
                for t in range(TC):
                    dve.wait_ge(st, TC * k + t + 1)
                    ins = dve.bn_aggr(mv[:, TC * c + t, :], bn[:, TC * c + t, :])
                ins.then_inc(sem("norm_stats"), 1)

            def norm(name, half, c, src, dst):
                dve.wait_ge(sem("norm_rstd"), 2 * norms_before(name, half, c) + 2)
                for t in range(TC):
                    i = TC * c + t
                    dve.tensor_scalar(dst[:, i, :], src(c, t), mv[:, i, 0:1], rstd[:, i:i + 1],
                                      ALU.subtract, ALU.mult).then_inc(sem("normed"), 1)

            def x_tile(c, t):
                return X[:, TC * c + t, :]

            def ps_tile(c, t):
                return ps[:, 4 + c, P * t:P * t + P]

            def yb_tile(c, t):
                return YB[:, TC * c + t, :]

            def post(name, ready, src, more):
                for c in range(CHUNKS):
                    dve.wait_ge(sem(ready), c + 1)
                    moments(name, 0, c, src)
                for c in range(CHUNKS):
                    norm(name, 0, c, src, TMP)
                if more:
                    for c in range(CHUNKS):
                        dve.wait_ge(sem("x_added"), adds_before(name, c) + 1)
                        moments(name, 1, c, x_tile)
                    for c in range(CHUNKS):
                        norm(name, 1, c, x_tile, XN)

            def last_part(L, w):
                dve.wait_ge(sem(f"part1_{L}"), w + 1)
                dve.tensor_tensor(parts[4 * L + w][:, 2, :], rest[:, w % 2, :], parts[4 * L + w][:, 1, :],
                                  ALU.subtract)\
                    .then_inc(sem(f"split_done{L}"), 1)

            def rotate(w):
                step = sem("rotated")
                dve.wait_ge(sem("qk_ps0"), w + 1)
                if w >= 2:
                    dve.wait_ge(sem("split_done0"), w - 1)
                dve.tensor_tensor(full[:, w % 2, :], bank(QK_BANK[0][w], 2), rope[:, 0, :], ALU.mult)\
                    .then_inc(step, 1)
                dve.tensor_tensor(rest[:, w % 2, :], bank(QK_BANK[0][w] + 2, 2), rope[:, 1, :], ALU.mult)\
                    .then_inc(step, 1)
                dve.wait_ge(step, 2 * w + 2)
                dve.tensor_tensor(full[:, w % 2, :], full[:, w % 2, :], rest[:, w % 2, :], ALU.add)\
                    .then_inc(sem("qk_full0"), 1)

            def attend(L, plan, beside_first):
                maxed, small = sem(f"rowmax{L}"), sem(f"small_done{L}")

                def row_max(n, par, jj):
                    qt, j = plan.jobs[jj]
                    pair, e = divmod(j, 2)
                    dve.wait_ge(sem(f"first_ps{L}"), JOBS * n + jj + 1)
                    dve.tensor_reduce(nmax[:, par, qt // 4, e, 4 * pair + qt % 4:4 * pair + qt % 4 + 1],
                                      bank(plan.first_bank(jj), 1 if plan.single(jj) else 2)[:, 0:plan.keys(qt)], AX.X, ALU.max, negate=True)\
                        .then_inc(maxed, 1)

                def copy_max(turns, par, qh):
                    dve.wait_ge(sem(f"small_ps{L}"), turns + 1)
                    dve.tensor_copy(nmaxT[:, par, qh, :], bank(7).bitcast(BF16)[0:48, 0:P]).then_inc(small, 1)

                def normalise(turns, n, qh):
                    dve.wait_ge(sem(f"small_ps{L}"), turns + 1)
                    o = bank(7).rearrange("p (x v) -> p x v", v=32)
                    dve.reciprocal(rden[:, qh, :], o[:, :, DH]).then_inc(sem(f"rden{L}"), 1)
                    dve.wait_ge(sem(f"rden{L}"), 2 * n + qh + 1)
                    dve.tensor_tensor(Y[:, 4 * qh:4 * qh + 4, n, :].rearrange("p k (j d) -> p k j d", j=G),
                                      o[:, :, 0:DH].rearrange("p (k j) d -> p k j d", j=G),
                                      rden[:, qh, :].rearrange("p (k j) -> p k j", j=G).unsqueeze(3)
                                      .to_broadcast([P, 4, G, DH]), ALU.mult)\
                        .then_inc(small, 1)

                for jj in range(JOBS):
                    beside_first(jj)
                    row_max(0, 0, jj)
                copy_max(0, 0, 0)

                def period(n, par, rounds, first, last):
                    for s in range(plan.n):
                        if not last:
                            for jj in plan.beside[s]:
                                row_max(n + 1, 1 - par, jj)
                        kind = plan.small.get(s)
                        if kind == "max1":
                            copy_max(turn(kind, n, first), par, 1)
                        if kind == "max0" and not last:
                            copy_max(turn(kind, n, first), 1 - par, 0)
                        if kind == "out0":
                            normalise(turn(kind, n, first), n, 0)
                        if kind == "out1" and not first:
                            normalise(turn(kind, n, first), n - 1, 1)

                periods(dve, period)
                normalise(turn("max0", NG - 1), NG - 1, 1)

            dve.wait_ge(sem("w0_in"), 64)
            for q in (0, 2):
                plain = ups[:, q, 4:8].rearrange("p (i k) -> p i k", k=2)
                turned = ups[:, q + 1, 4:8].rearrange("p (i k) -> p i k", k=2)
                dve.memset(ups[:, q + 1, 0:4], 0.0).then_inc(sem("ups_rot"), 1)
                dve.tensor_scalar(turned[:, :, 0], plain[:, :, 1], -1.0, None, ALU.mult).then_inc(sem("ups_rot"), 1)
                dve.tensor_copy(turned[:, :, 1], plain[:, :, 0]).then_inc(sem("ups_rot"), 1)
            dve.wait_ge(sem("folded_ps"), 1)
            for side in range(2):
                dve.tensor_copy(wqk[0][:, side].rearrange("p r (h d) -> p r h d", h=H),
                                bank(side)[:, 0:256].rearrange("p (h r d) -> p r h d", h=H, r=2))\
                    .then_inc(sem("folded"), 1)
            dve.tensor_copy(wv[0][:, :], bank(2)[:, 0:P]).then_inc(sem("folded"), 1)
            dve.wait_ge(sem("x_in"), 16)
            dve.wait_ge(sem("pool_const"), POOL_CONSTS)
            for c in range(CHUNKS):
                moments("ln0", 1, c, x_tile)
            for c in range(CHUNKS):
                norm("ln0", 1, c, x_tile, XN)
            dve.wait_ge(sem("rope_in"), 16)
            rotate(0)
            rotate(1)
            last_part(0, 0)
            rotate(2)
            last_part(0, 1)
            rotate(3)
            last_part(0, 2)
            last_part(0, 3)
            attend(0, PLANS[0], lambda jj: None)
            post("post0", "branch_ps0", ps_tile, True)
            def route_step(c, j):
                step, k, t = sem("route"), 9 * c, slice(TC * c, TC * c + TC)
                sc, bi = esc[:, t], ebi[:, t]
                mine = bi.unsqueeze(3).to_broadcast([P, TC, E, E])
                theirs = bi.unsqueeze(2).to_broadcast([P, TC, E, E])
                x0, x1 = cmp[:, 0, t], cmp[:, 1, t]
                bias = ebias[:, :].unsqueeze(1).to_broadcast([P, TC, E])
                before = before8[:, :, :].unsqueeze(1).to_broadcast([P, TC, E, E])
                if j == 0:
                    dve.wait_ge(sem("gate_exp"), c + 1)
                    dve.tensor_scalar(sc, sc, 1.0, None, ALU.add).then_inc(step, 1)
                elif j == 1:
                    dve.wait_ge(step, k + 1)
                    dve.reciprocal(sc, sc).then_inc(step, 1)
                elif j == 2:
                    dve.wait_ge(step, k + 2)
                    dve.tensor_tensor(bi, sc, bias, ALU.add).then_inc(step, 1)
                elif j == 3:
                    dve.wait_ge(step, k + 3)
                    dve.tensor_tensor(x1, theirs, mine, ALU.is_equal).then_inc(step, 1)
                    dve.tensor_tensor(x0, theirs, mine, ALU.is_gt).then_inc(step, 1)
                elif j == 4:
                    dve.wait_ge(step, k + 4)
                    dve.tensor_tensor(x1, x1, before, ALU.mult).then_inc(step, 1)
                elif j == 5:
                    dve.wait_ge(step, k + 6)
                    dve.tensor_tensor(x0, x0, x1, ALU.add).then_inc(step, 1)
                elif j == 6:
                    dve.wait_ge(step, k + 7)
                    dve.tensor_reduce(erank[:, t], x0, AX.X, ALU.add).then_inc(step, 1)
                elif j == 7:
                    dve.wait_ge(step, k + 8)
                    dve.tensor_scalar(chosen[:, t], erank[:, t], 1.5, None, ALU.is_lt).then_inc(step, 1)
                elif j == 8:
                    dve.wait_ge(step, k + 9)
                    dve.tensor_tensor(sc, sc, chosen[:, t], ALU.mult).then_inc(sem("chosen"), 1)

            for j in range(ROUTE_STEPS):
                route_step(0, j)

            def route_beside(i, place):
                for c, at in ROUTE_AT.items():
                    j = 2 * (i - at) + place
                    if 0 <= j < ROUTE_STEPS:
                        route_step(c, j)

            def scale_in(u):
                c, e = divmod(u, E)
                dve.wait_ge(sem("score_ps"), u + 1)
                if u >= 2:
                    dve.wait_ge(sem("unit_ps"), through("expert", u - 2))
                dve.tensor_tensor(xsT[:, u % 2, :], XNT[:, CW * c:CW * c + CW], bank(SPREAD_BANK[u % 2]), ALU.mult)\
                    .then_inc(sem("xsT"), 1)

            def square(u):
                dve.wait_ge(sem("unit_read"), through("expert", u))
                if u >= 2:
                    dve.wait_ge(sem("down_ps"), u - 1)
                dve.tensor_tensor(hsq[:, u % 2], hrelu[:, u % 2], hrelu[:, u % 2], ALU.mult)\
                    .then_inc(sem("hsq"), 1)

            def round_out(u):
                dve.wait_ge(sem("down_ps"), u + 1)
                if u >= 2:
                    dve.wait_ge(sem("eacc"), u - 1)
                dve.tensor_copy(eout[:, u % 2, :], bank(5 + u % 2)).then_inc(sem("eout_dve"), 1)

            def post1(what, half, c):
                src = x_tile if half else (lambda c, t: ps[:, 7, P * t:P * t + P]) if c == 3 else yb_tile
                if what == "moments":
                    if half:
                        dve.wait_ge(sem("x_added"), adds_before("post1", c) + 1)
                    elif c == 3:
                        dve.wait_ge(sem("back_ps3"), 1)
                    else:
                        dve.wait_ge(sem("unit_read"), through("back", c))
                    moments("post1", half, c, src)
                elif what == "norm":
                    norm("post1", half, c, src, XN if half else TMP)
                else:
                    last_part(1, c)

            for i in range(-2, len(UNITS) + 4):
                if expert(i + 2) is not None:
                    scale_in(expert(i + 2))
                route_beside(i, 0)
                if expert(i - 1) is not None:
                    square(expert(i - 1))
                route_beside(i, 1)
                u = expert(i - 3)
                if u is not None and rounded_by_dve(u):
                    round_out(u)
                if i in BESIDE_EXPERTS:
                    post1(*BESIDE_EXPERTS[i])

            def beside_first(jj):
                if jj == BESIDE_FIRST["moments0"]:
                    post1("moments", 0, 3)
                if jj == BESIDE_FIRST["norm0"]:
                    post1("norm", 0, 3)
                if jj == BESIDE_FIRST["moments1"]:
                    post1("moments", 1, 2)
                    post1("moments", 1, 3)
                if jj == BESIDE_FIRST["norm1"]:
                    post1("norm", 1, 2)
                    post1("norm", 1, 3)
                for w in (2, 3):
                    if jj == BESIDE_FIRST[f"part{w}"]:
                        last_part(1, w)

            attend(1, PLANS[1], beside_first)
            post("post2", "branch_ps1", ps_tile, True)
            for c in range(CHUNKS):
                router_scores(dve, sem, FF, XN, c)
            dve_ffn(dve, sem, bank, ps, FF, XN, YB)
            post("post3", "ffn_out", yb_tile, False)

        @block.tensor
        def _(pe):
            def turn_xn(at, c):
                for t in range(TC):
                    ins = pe.transpose(ps[:, at, P * t:P * t + P], XN[:, TC * c + t, :], ident[:, :])
                return ins

            def transpose_xn(name, banks, chunks=range(CHUNKS)):
                for c in chunks:
                    pe.wait_ge(sem("normed"), TC * (norms_before(name, 1, c) + 1))
                    turn_xn(banks[c], c).then_inc(sem("xnT_ps"), 1)

            def q_or_k(L, w, at):
                b, side = divmod(w, 2)
                for r in range(2 - L):
                    for c in range(2):
                        ins = pe.matmul(ps[:, at + 2 * r + c, :], wqk[L][:, side, r, :],
                                        XNT[:, T * b + CW * c:T * b + CW * c + CW], start=True, stop=True)
                return ins

            def values(L, b, at, tiles=range(KT)):
                for k in tiles:
                    o = bank(at, 1 if len(tiles) < KT else 2)[:, P * (k - tiles[0]):P * (k - tiles[0]) + P]
                    ins = pe.matmul(o, XNT[:, T * b + P * k:T * b + P * k + P], wv[L][:, :],
                                    start=True, stop=not L)
                    if L:
                        ins = pe.matmul(o, ones_row[:, :], bvo[:, 0, :], start=False, stop=True)
                return ins

            def attend(L, plan, beside_first):
                first, second, pv, small = (sem(f"{k}{L}") for k in ("first_ps", "second_ps", "pv", "small_ps"))
                exps, maxed, small_done = sem(f"exp{L}"), sem(f"rowmax{L}"), sem(f"small_done{L}")

                def first_job(n, par, rounds, jj, prologue=False):
                    qt, j = plan.jobs[jj]
                    pair, e = divmod(j, 2)
                    if jj == 0:
                        pe.wait_ge(sem(f"first_in{L}{par}"), 64 * (rounds + 1))
                    before, at = plan.maxima_before(jj), plan.first_bank(jj)
                    if not (prologue and before <= 0):
                        pe.wait_ge(maxed, JOBS * n + before)
                    keys = plan.keys(qt)
                    for k0 in range(0, keys, 512):
                        k1 = min(keys, k0 + 512)
                        masked = plan.causal and k1 == keys
                        ins = pe.matmul(ps[:, at + k0 // 512, 0:k1 - k0],
                                        SQ[:, par, j, P * qt:P * qt + P], SK[:, par, pair, k0:k1],
                                        start=True, stop=not masked)
                        if masked:
                            ins = pe.matmul(ps[:, at + k0 // 512, k1 - k0 - P:k1 - k0],
                                            ident_bf[:, :], mask_bf[:, 0, :], start=False, stop=True)
                    ins.then_inc(first, 1)

                def scores(n, par, rounds, s, j, begin, last):
                    qh, kt = plan.steps[s]
                    pair, e = divmod(j, 2)
                    c0 = plan.skipped(qh, kt)
                    if s == 0 and j == 0:
                        pe.wait_ge(sem(f"second_in{L}{par}"), 80 * (rounds + 1))
                    if kt == 0 and j == 0:
                        pe.wait_ge(sem(f"max_in{L}{qh}"), 32 * (n + 1))
                    if last and s == 0:
                        if j == 0:
                            pe.wait_ge(maxed, JOBS * NG)
                    elif last:
                        pe.wait_ge(exps, (plan.n * n + s - 1) * G + j + 1)
                    elif not (begin and s == 0 and j < 2):
                        pe.wait_ge(exps, (plan.n * n + s) * G + j - 1)
                    o = second_bank(j, last)
                    diagonal = plan.diagonal(qh, kt)
                    ins = pe.matmul(ps[:, o, c0:512], TK[:, par, pair, P * kt:P * kt + P],
                                    TQ[:, par, j, 512 * qh + c0:512 * qh + 512],
                                    start=True, stop=not diagonal)
                    if diagonal:
                        ins = pe.matmul(ps[:, o, c0:c0 + P], ident_bf[:, :], mask_bf[:, 1, :],
                                        start=False, stop=True)
                    ins.then_inc(second, 1)

                def times_values(n, par, s, begin):
                    qh, kt = plan.steps[s]
                    c0 = plan.skipped(qh, kt)
                    pe.wait_ge(exps, (plan.n * n + s + 1) * G)
                    if kt == 0 and not (begin and qh == 0):
                        pe.wait_ge(sem(f"out_copied{L}"), 2 * n + qh)
                    end = s == plan.n - 1 or plan.steps[s + 1][0] != qh
                    for j in range(G):
                        ins = pe.matmul(ps[32 * j:32 * j + VW, 6, c0:512], VS[:, par, kt, j, :],
                                        probs[:, s % 2, j, c0:512], start=(kt == 0), stop=end)
                    ins.then_inc(pv, 1)

                def max_rows(turns, n, par, qh, begin=False):
                    if not begin:
                        pe.wait_ge(small_done, turns)
                    pe.wait_ge(sem(f"max3_{L}"), 8 * n + 4 * qh + 4)
                    pe.transpose(bank(7).bitcast(BF16)[:, 0:P], nmax3_cols[:, par, qh, :], ident_bf[:, :])\
                        .then_inc(small, 1)

                def out_rows(turns, n, qh):
                    pe.wait_ge(small_done, turns)
                    pe.wait_ge(sem(f"out_copied{L}"), 2 * n + qh + 1)
                    for q in range(4):
                        ins = pe.transpose(ps[:, 7, P * q:P * q + P], OS[:, qh, P * q:P * q + P], ident[:, :])
                    ins.then_inc(small, 1)

                for jj in range(JOBS):
                    beside_first(jj)
                    first_job(0, 0, 0, jj, prologue=True)
                for name, value in (qk_full(L, 3), values_done(L, 1)):
                    pe.wait_ge(sem(name), value)
                max_rows(0, 0, 0, 0, begin=True)

                def period(n, par, rounds, begin, last):
                    for s in range(plan.n):
                        beside = [] if last else plan.beside[s]
                        at = 0
                        for i, piece in enumerate(("s0", "s1", "values", "s2", "s3")):
                            if piece != "values":
                                scores(n, par, rounds, s, int(piece[1]), begin, last)
                            elif s:
                                times_values(n, par, s - 1, begin)
                            elif not begin:
                                times_values(n - 1, 1 - par, plan.n - 1, False)
                            upto = len(beside) * plan.done_by[i] // 4
                            for jj in beside[at:upto]:
                                first_job(n + 1, 1 - par, rounds + par, jj)
                            at = upto
                        kind = plan.small.get(s)
                        if kind == "max1":
                            max_rows(turn(kind, n, begin), n, par, 1)
                        if kind == "max0" and not last:
                            max_rows(turn(kind, n, begin), n + 1, 1 - par, 0)
                        if kind == "out0":
                            out_rows(turn(kind, n, begin), n, 0)
                        if kind == "out1" and not begin:
                            out_rows(turn(kind, n, begin), n - 1, 1)

                periods(pe, period)
                times_values(NG - 1, 1, plan.n - 1, False)
                out_rows(turn("max0", NG - 1), NG - 1, 1)

            def project_out(L):
                pe.wait_ge(sem(f"small_done{L}"), 4 * NG)
                for c in range(CHUNKS):
                    for t in range(TC):
                        b, k = divmod(TC * c + t, KT)
                        ins = pe.transpose(ps[:, c, P * t:P * t + P],
                                           Y[:, k, G * b:G * b + G, :].rearrange("p g d -> p (g d)"), ident[:, :])
                    ins.then_inc(sem(f"yT_ps{L}"), 1)
                for c in range(CHUNKS):
                    pe.wait_ge(sem(f"yT{L}"), c + 1)
                    for t in range(TC):
                        o = ps[:, 4 + c, P * t:P * t + P]
                        ins = pe.matmul(o, YT[:, CW * c + P * t:CW * c + P * t + P], wo[L][:, :],
                                        start=True, stop=not L)
                        if L:
                            ins = pe.matmul(o, ones_row[:, :], bvo[:, 1, :], start=False, stop=True)
                    ins.then_inc(sem(f"branch_ps{L}"), 1)

            pe.wait_ge(sem("w0_in"), 64)
            pe.wait_ge(sem("ups_rot"), 6)
            for side in range(2):
                for h in range(H):
                    pe.matmul(ps[:, side, 16 * h:16 * h + 16], down[:, side, h, :],
                              ups[:, 2 * side:2 * side + 2, :].rearrange("p r d -> p (r d)"), start=True, stop=True)
            for h in range(H):
                ins = pe.matmul(ps[:, 2, DH * h:DH * h + DH], down[:, 2, h, :], ups[:, 4, :],
                                start=True, stop=True)
            ins.then_inc(sem("folded_ps"), 1)
            pe.wait_ge(sem("const_in"), 32)
            transpose_xn("ln0", LN0_BANK, range(2))
            pe.wait_ge(sem("folded"), 3)
            pe.wait_ge(sem("xnT"), 2)
            q_or_k(0, 0, QK_BANK[0][0]).then_inc(sem("qk_ps0"), 1)
            q_or_k(0, 1, QK_BANK[0][1]).then_inc(sem("qk_ps0"), 1)
            pe.wait_ge(sem("qk_full0"), 1)
            values(0, 0, V_BANK[0][0]).then_inc(sem("v_ps0"), 1)
            transpose_xn("ln0", LN0_BANK, range(2, CHUNKS))
            pe.wait_ge(sem("xnT"), CHUNKS)
            pe.wait_ge(sem("qk_full0"), 2)
            q_or_k(0, 2, QK_BANK[0][2]).then_inc(sem("qk_ps0"), 1)
            pe.wait_ge(sem("v_done0"), 4)
            q_or_k(0, 3, QK_BANK[0][3]).then_inc(sem("qk_ps0"), 1)
            pe.wait_ge(sem("qk_full0"), 3)
            values(0, 1, V_BANK[0][1]).then_inc(sem("v_ps0"), 1)
            pe.wait_ge(sem("act_const"), 2)
            pe.wait_ge(sem("qk_full0"), 4)
            pe.wait_ge(sem("v_done0"), 8)
            attend(0, PLANS[0], lambda jj: None)
            pe.wait_ge(sem("later_in"), 16 * LATER)
            project_out(0)
            def gate(c):
                pe.wait_ge(sem("xnT"), turned_before("post0", c + 1))
                for t in range(TC):
                    i = TC * c + t
                    ins = pe.matmul(ps[:, 4 + c, E * t:E * t + E], XNT[:, P * i:P * i + P], gateT[:, :],
                                    start=True, stop=True)
                ins.then_inc(sem("gate_ps"), 1)

            for c in range(CHUNKS):
                transpose_xn("post0", range(CHUNKS), [c])
                if c:
                    gate(c - 1)
            gate(CHUNKS - 1)
            pe.wait_ge(sem("moe_bf"), 3)

            def turn_parts(at, c):
                pe.wait_ge(sem("score3"), 5 * c + 5)
                for t in range(TC):
                    ins = pe.transpose(bank(at).bitcast(BF16)[:, P * t:P * t + P], esc3_cols[:, TC * c + t, :],
                                       ident_bf[:, :])
                return ins

            turn_parts(0, 0).then_inc(sem("esc3T_ps"), 1)
            pe.wait_ge(sem("gate_exp"), CHUNKS)

            def spread_score(u):
                c, e = divmod(u, E)
                if u == 0:
                    pe.wait_ge(sem("esc3T"), 1)
                if c and e == 0:
                    pe.wait_ge(sem("unit_read"), through("parts", c))
                if u >= 2:
                    pe.wait_ge(sem("xsT"), u - 1)
                pe.matmul(bank(SPREAD_BANK[u % 2]), pick_bf[:, e:e + 1].to_broadcast([P, P]), esc3T[:, CW * c:CW * c + CW],
                          start=True, stop=True).then_inc(sem("score_ps"), 1)

            def turn_back(at, c):
                for t in range(TC):
                    ins = pe.transpose(ps[:, at, P * t:P * t + P], OS[:, c % 2, P * t:P * t + P], ident[:, :])
                return ins

            def do_unit(v):
                kind, n = UNITS[v]
                if kind == "expert":
                    pe.wait_ge(sem("xsT"), n + 1)
                if kind == "turn":
                    pe.wait_ge(sem("normed"), TC * (norms_before("post1", 1, n) + 1))
                if kind == "q":
                    pe.wait_ge(sem("unit_read"), through("turn", 1))
                if kind == "back":
                    pe.wait_ge(sem("moe_sum"), n + 1)
                for k in range(HALVES[v]):
                    h = halves_before(v) + k
                    at = half_bank(h)
                    if h >= 3:
                        pe.wait_ge(sem("unit_read"), h - 2)
                    if kind == "shared":
                        ins = pe.matmul(ps[0:HH, at, :], supT[:, HH * k:HH * k + HH], XNT[:, CW * n:CW * n + CW],
                                        start=True, stop=True)
                    elif kind == "expert":
                        ins = pe.matmul(ps[0:HH, at, :], wup_bf[:, n % E, HH * k:HH * k + HH], xsT[:, n % 2, :],
                                        start=True, stop=True)
                    elif kind == "parts":
                        ins = turn_parts(at, n)
                    elif kind == "turn":
                        ins = turn_xn(at, n)
                    elif kind == "back":
                        ins = turn_back(at, n)
                    elif kind == "v":
                        ins = values(1, 0, at, range(TC * k, TC * k + TC))
                    else:
                        ins = pe.matmul(bank(at), wqk[1][:, n, 0, :], XNT[:, CW * k:CW * k + CW], start=True, stop=True)
                    ins.then_inc(sem("unit_ps"), 1)

            def wait_rounded(u):
                if rounded_by_dve(u):
                    pe.wait_ge(sem("eout_dve"), (u + 1) // 4)
                else:
                    pe.wait_ge(sem("eout_act"), u + 1 - (u + 1) // 4)

            def expert_down(u):
                c, e = divmod(u, E)
                pe.wait_ge(sem("hsq"), u + 1)
                if u >= 2:
                    wait_rounded(u - 2)
                for k in range(2):
                    ins = pe.matmul(bank(5 + u % 2), wdn_bf[:, e, k, :], hsq[:, u % 2, k, :], start=(k == 0),
                                    stop=(k == 1))
                ins.then_inc(sem("down_ps"), 1)

            def add_up(u):
                c, e = divmod(u, E)
                if e == E // 2:
                    pe.wait_ge(sem("shared_sq"), c + 1)
                    for k in range(2):
                        ins = pe.matmul(bank(7), sdnT[:, k, :], hs2[:, k, :], start=False, stop=False)
                    ins.then_inc(sem("shared_ps"), 1)
                wait_rounded(u)
                if e == 0 and c:
                    pe.wait_ge(sem("moe_sum"), c)
                pe.matmul(ps[:, 7, :], ident_bf[:, :], eout[:, u % 2, :], start=(e == 0), stop=(e == E - 1))\
                    .then_inc(sem("eacc"), 1)

            for i in range(-2, len(UNITS) + 4):
                if 0 <= i < len(UNITS):
                    do_unit(i)
                if expert(i + 2) is not None:
                    spread_score(expert(i + 2))
                if expert(i - 2) is not None:
                    expert_down(expert(i - 2))
                if expert(i - 4) is not None:
                    add_up(expert(i - 4))

            def beside_first(jj):
                if jj == BESIDE_FIRST["turn"]:
                    transpose_xn("post1", TURN_BANK, range(2, CHUNKS))
                if jj == BESIDE_FIRST["q"]:
                    pe.wait_ge(sem("xnT"), turned_before("post1", CHUNKS))
                    q_or_k(1, 2, QK_BANK[1][2]).then_inc(sem("qk_ps1"), 1)
                if jj == BESIDE_FIRST["k"]:
                    q_or_k(1, 3, QK_BANK[1][3]).then_inc(sem("qk_ps1"), 1)
                if jj == BESIDE_FIRST["v"]:
                    pe.wait_ge(sem("qk_full1"), 1)
                    values(1, 1, V_BANK[1][1]).then_inc(sem("v_ps1"), 1)

            pe.wait_ge(sem("moe_sum"), CHUNKS)
            turn_back(7, CHUNKS - 1).then_inc(sem("back_ps3"), 1)
            pe.wait_ge(sem("unit_read"), halves_before(len(UNITS)))
            attend(1, PLANS[1], beside_first)
            project_out(1)
            pe_ffn(pe, sem, bank, ps, FF, XN, ident)


QK_BANK = ((0, 4, 4, 0), (None, None, 6, 4))
V_BANK = ((0, 4), (None, 6))
LN0_BANK = (4, 5, 2, 3)
TURN_BANK = (None, None, 4, 5)
POOL_CONSTS = 10
FFN_INPUTS = ("wr", "iota", "offset", "tri", "g1", "g2", "qkvT", "woutT", "w1T", "w2T", "w3T",
              "headmask", "mask2")
LATER = 15 + len(FFN_INPUTS)


def ffn_buffers(sb, full, rest, XNT, TMP, YT, arena):
    f = dict(
        wr=sb("wr", [P, C]), iota=sb("iota", [P, P]), offset=sb("offset", [P, TILES]),
        tri=sb("tri", [P, P]), g1=sb("g1", [P, C]), g2=sb("g2", [P, C]), qkvT=sb("qkvT", [C, 3 * C]),
        woutT=sb("woutT", [C, C]), w1T=sb("w1T", [C, FC * P]), w2T=sb("w2T", [C, FC * P]),
        w3T=sb("w3T", [P, FC, C]), headmask=sb("headmask", [P, H]), mask2=sb("mask2", [P, P]),
        score=sb("score", [P, TILES]), count=sb("count", [P, TILES, 3]),
        rank=sb("rank", [P, TILES]), nsel=sb("nsel", [P, TILES]), slot=sb("slot", [P, TILES]),
        ssq=sb("ssq", [P, 2]), small=sb("small", [P, 4]),
       
        smax=sb("smax", [P, H]), sden=sb("sden", [P, H]),
       
    )
    f = {k: v[:] if len(v.shape) == 1 else v[(slice(None),) * len(v.shape)] for k, v in f.items()}
    for k, name in enumerate(("xs", "h", "hT", "qT", "kT", "v", "o", "oT", "x2", "xp")):
        f[name] = arena[:, P * (8 + k):P * (9 + k)]
    f["ga"], f["gb"] = arena[:, 0:FC * P], arena[:, FC * P:2 * FC * P]
    f["junk"] = full[:, :, :]
    f["sel"] = YT[:, :].rearrange("p (t s) -> p t s", t=TILES)
    f["selT"] = XNT[:, :]
    f["s"] = TMP[:, :, :]
    f["qm"] = YT[:, :].rearrange("p (h q) -> p h q", h=H)
    f["pT"] = rest[:, :, :].rearrange("p a t -> p (a t)").rearrange("p (h q) -> p h q", h=H)
    return f


def router_scores(dve, sem, f, XN, c):
    for t in range(TC * c, TC * c + TC):
        dve.wait_ge(sem("normed"), TC * norms_before("post2", 1, c) + t % TC + 1)
        if t:
            dve.wait_ge(sem("score"), t)
        dve.tensor_tensor_reduce(out=f["h"], in0=XN[:, t, :], in1=f["wr"], scale=1.0, scalar=0.0,
                                 op0=ALU.mult, op1=ALU.add, accum_out=f["score"][:, t:t + 1])\
            .then_inc(sem("score"), 1)


def dve_ffn(dve, sem, bank, ps, f, XN, YB):
    step = sem("ffn_dve")
    n, n_counted = [0], [0]

    def counted(ins):
        n_counted[0] += 1
        ins.then_inc(sem("counted"), 1)

    def junk():
        if n_counted[0] >= 2:
            dve.wait_ge(sem("counted"), n_counted[0] - 1)
        return f["junk"][:, n_counted[0] % 2, :]

    def link(ins):
        n[0] += 1
        ins.then_inc(step, 1)
        dve.wait_ge(step, n[0])

    for b in range(B):
        dve.wait_ge(sem("row_ps"), b + 1)
        row = bank(2 * b, 2)
        for k in range(KT):
            t = KT * b + k
            mine, cnt, own = f["score"][:, t:t + 1], f["count"], slice(P * k, P * k + P)
            if k:
                counted(dve.tensor_scalar(junk()[:, 0:P * k], row[:, 0:P * k], mine, None, ALU.is_ge, ALU.add,
                                          accum_out=cnt[:, t, 0:1]))
            counted(dve.tensor_scalar(junk()[:, P * k:T], row[:, P * k:T], mine, None, ALU.is_gt, ALU.add,
                                      accum_out=cnt[:, t, 1:2]))
            counted(dve.scalar_tensor_tensor(out=junk()[:, own], in0=row[:, own], scalar=mine, in1=f["tri"],
                                             op0=ALU.is_equal, op1=ALU.mult, accum_out=cnt[:, t, 2:3]))
        ts = slice(KT * b, KT * b + KT)
        dve.wait_ge(sem("counted"), n_counted[0])
        link(dve.tensor_reduce(f["rank"][:, ts], f["count"][:, ts], AX.X, ALU.add))
        link(dve.tensor_scalar(f["nsel"][:, ts], f["rank"][:, ts], TOP - 0.5, None, ALU.is_gt))
        link(dve.scalar_tensor_tensor(out=f["slot"][:, ts], in0=f["nsel"][:, ts], scalar=4096.0,
                                      in1=f["rank"][:, ts], op0=ALU.mult, op1=ALU.add))
        link(dve.tensor_tensor(f["slot"][:, ts], f["slot"][:, ts], f["offset"][:, ts], ALU.add))
        dve.tensor_tensor(f["sel"][:, ts], f["iota"].unsqueeze(1).to_broadcast([P, KT, P]),
                          f["slot"][:, ts].unsqueeze(2).to_broadcast([P, KT, P]), ALU.is_equal)\
            .then_inc(sem("sel"), 1)

    def rms(i, src, gain):
        dve.tensor_tensor_reduce(out=f["h"], in0=src, in1=src, scale=1.0, scalar=0.0, op0=ALU.mult,
                                 op1=ALU.add, accum_out=f["ssq"][:, i:i + 1]).then_inc(sem(f"ssq{i}"), 1)
        dve.wait_ge(sem(f"rms{i}"), 2)
        dve.scalar_tensor_tensor(out=f["h"], in0=src, scalar=f["small"][:, 2 * i + 1:2 * i + 2], in1=gain,
                                 op0=ALU.mult, op1=ALU.mult).then_inc(sem(f"rows{i}"), 1)

    dve.wait_ge(sem("gathered"), TILES)
    link(dve.tensor_copy(f["xs"], ps[:, 7, 0:C]))
    rms(0, f["xs"], f["g1"])
    dve.wait_ge(sem("qT"), 1)
    dve.tensor_tensor(f["qm"], f["qT"].unsqueeze(1).to_broadcast([P, H, P]),
                      f["headmask"].unsqueeze(2).to_broadcast([P, H, P]), ALU.mult).then_inc(sem("qm"), 1)
    dve.wait_ge(sem("s_ps"), 1)
    link(dve.tensor_tensor(f["s"], bank(0, 4).rearrange("p (h k) -> p h k", h=H),
                           f["mask2"].unsqueeze(1).to_broadcast([P, H, P]), ALU.add))
    link(dve.tensor_reduce(f["smax"], f["s"], AX.X, ALU.max, negate=True))
    dve.tensor_tensor(f["s"], f["s"], f["smax"].unsqueeze(2).to_broadcast([P, H, P]), ALU.add)\
        .then_inc(sem("s_shifted"), 1)
    dve.wait_ge(sem("s_exp"), 1)
    link(dve.tensor_reduce(f["sden"], f["s"], AX.X, ALU.add))
    link(dve.reciprocal(f["sden"], f["sden"]))
    dve.wait_ge(sem("o_ps"), 1)
    dve.tensor_tensor(f["o"].rearrange("p (h d) -> p h d", h=H), ps[:, 0, 0:C].rearrange("p (h d) -> p h d", h=H),
                      f["sden"].unsqueeze(2).to_broadcast([P, H, DH]), ALU.mult).then_inc(sem("o"), 1)
    dve.wait_ge(sem("attn_ps"), 1)
    link(dve.tensor_tensor(f["x2"], f["xs"], ps[:, 2, 0:C], ALU.add))
    rms(1, f["x2"], f["g2"])
    dve.wait_ge(sem("ga_exp"), 1)
    link(dve.tensor_scalar(f["ga"], f["ga"], 1.0, None, ALU.add))
    link(dve.reciprocal(f["ga"], f["ga"]))
    link(dve.tensor_tensor(f["ga"], f["ga"], bank(4)[:, 0:FC * P], ALU.mult))
    dve.tensor_tensor(f["gb"], f["ga"], bank(5)[:, 0:FC * P], ALU.mult).then_inc(sem("gb"), 1)
    dve.wait_ge(sem("ff_ps"), 1)
    dve.tensor_tensor(f["xp"], f["x2"], ps[:, 6, 0:C], ALU.add).then_inc(sem("xp"), 1)
    for c in range(CHUNKS):
        dve.wait_ge(sem("back_ps"), c + 1)
        for t in range(TC):
            ins = dve.scalar_tensor_tensor(out=YB[:, TC * c + t, :], in0=XN[:, TC * c + t, :],
                                           scalar=f["nsel"][:, TC * c + t:TC * c + t + 1],
                                           in1=ps[:, c, P * t:P * t + P], op0=ALU.mult, op1=ALU.add)
        ins.then_inc(sem("ffn_out"), 1)


def act_ffn(act, sem, bank, ps, f):
    def copy(dst, src, wait, done, func=ACT.Copy, scale=1.0):
        act.wait_ge(sem(wait), 1)
        act.activation(dst, src, func, scale=scale).then_inc(sem(done), 1)

    for c in range(CHUNKS):
        act.wait_ge(sem("selT_ps"), c + 1)
        act.activation(f["selT"][:, CW * c:CW * c + CW], bank(4 + c % 3), ACT.Copy).then_inc(sem("selT"), 1)
    copy(f["hT"], ps[:, 1, 0:P], "hT_ps0", "hT0")
    copy(f["qT"], ps[:, 2, 0:P], "qkv_ps", "qT")
    copy(f["kT"], ps[:, 2, P:2 * P], "qkv_ps", "kT")
    copy(f["v"], ps[:, 2, 2 * P:3 * P], "qkv_ps", "v")
    act.wait_ge(sem("s_shifted"), 1)
    act.activation(f["s"], f["s"], ACT.Exp, scale=SCALE).then_inc(sem("s_exp"), 1)
    for c in range(4):
        act.wait_ge(sem("pT_ps"), c + 1)
        act.activation(f["pT"][:, 4 * c:4 * c + 4, :], bank(4 + c).rearrange("p (h q) -> p h q", h=4), ACT.Copy)\
            .then_inc(sem("pT"), 1)
    copy(f["oT"], ps[:, 1, 0:P], "oT_ps", "oT")
    copy(f["hT"], ps[:, 1, 0:P], "hT_ps1", "hT1")
    copy(f["ga"], bank(4)[:, 0:FC * P], "ga_ps", "ga_exp", ACT.Exp, -1.0)


def pe_ffn(pe, sem, bank, ps, f, XN, ident):
    def turn_sel(b):
        for c in (2 * b, 2 * b + 1):
            if c == 3:
                pe.wait_ge(sem("selT"), 1)
            for t in range(TC):
                ins = pe.transpose(ps[:, 4 + c % 3, P * t:P * t + P], f["sel"][:, TC * c + t, :], ident[:, :])
            ins.then_inc(sem("selT_ps"), 1)

    for b in range(B):
        pe.wait_ge(sem("score"), KT * (b + 1))
        for k in range(KT):
            ins = pe.transpose(bank(2 * b, 2)[:, P * k:P * k + P],
                               f["score"][:, KT * b + k:KT * b + k + 1].to_broadcast([P, P]), ident[:, :])
        ins.then_inc(sem("row_ps"), 1)
    for t in range(TILES):
        pe.wait_ge(sem("sel"), t // KT + 1)
        pe.matmul(ps[:, 7, 0:C], f["sel"][:, t, :], XN[:, t, :], start=(t == 0), stop=(t == TILES - 1))\
            .then_inc(sem("gathered"), 1)
        if t % KT == KT - 1 and t < TILES - 1:
            turn_sel(t // KT)
    turn_sel(1)
    pe.wait_ge(sem("rows0"), 1)
    pe.transpose(ps[:, 1, 0:P], f["h"], ident[:, :]).then_inc(sem("hT_ps0"), 1)
    pe.wait_ge(sem("hT0"), 1)
    pe.matmul(ps[:, 2, 0:P], f["qkvT"][:, 0:C], f["hT"], start=True, stop=True)
    pe.matmul(ps[:, 2, P:2 * P], f["qkvT"][:, C:2 * C], f["hT"], start=True, stop=True)
    pe.matmul(ps[:, 2, 2 * P:3 * P], f["hT"], f["qkvT"][:, 2 * C:3 * C], start=True, stop=True)\
        .then_inc(sem("qkv_ps"), 1)
    pe.wait_ge(sem("qm"), 1)
    pe.wait_ge(sem("v"), 1)
    for h in range(H):
        ins = pe.matmul(bank(0, 4)[:, P * h:P * h + P], f["qm"][:, h, :], f["kT"], start=True, stop=True)
    ins.then_inc(sem("s_ps"), 1)
    pe.wait_ge(sem("s_exp"), 1)
    pe.wait_ge(sem("selT"), CHUNKS)
    for c in range(4):
        for h in range(4 * c, 4 * c + 4):
            ins = pe.transpose(ps[:, 4 + c, P * (h % 4):P * (h % 4) + P], f["s"][:, h, :], ident[:, :])
        ins.then_inc(sem("pT_ps"), 1)
    for h in range(H):
        pe.wait_ge(sem("pT"), h // 4 + 1)
        ins = pe.matmul(ps[:, 0, DH * h:DH * h + DH], f["pT"][:, h, :], f["v"][:, DH * h:DH * h + DH],
                        start=True, stop=True)
    ins.then_inc(sem("o_ps"), 1)
    pe.wait_ge(sem("o"), 1)
    pe.transpose(ps[:, 1, 0:P], f["o"], ident[:, :]).then_inc(sem("oT_ps"), 1)
    pe.wait_ge(sem("oT"), 1)
    pe.matmul(ps[:, 2, 0:C], f["oT"], f["woutT"], start=True, stop=True).then_inc(sem("attn_ps"), 1)
    pe.wait_ge(sem("rows1"), 1)
    pe.transpose(ps[:, 1, 0:P], f["h"], ident[:, :]).then_inc(sem("hT_ps1"), 1)
    pe.wait_ge(sem("hT1"), 1)
    for k in range(FC):
        pe.matmul(ps[:, 4, P * k:P * k + P], f["w1T"][:, P * k:P * k + P], f["hT"], start=True, stop=True)
    for k in range(FC):
        ins = pe.matmul(ps[:, 5, P * k:P * k + P], f["w2T"][:, P * k:P * k + P], f["hT"], start=True, stop=True)
    ins.then_inc(sem("ga_ps"), 1)
    pe.wait_ge(sem("gb"), 1)
    for k in range(FC):
        ins = pe.matmul(ps[:, 6, 0:C], f["gb"][:, P * k:P * k + P], f["w3T"][:, k, :], start=(k == 0),
                        stop=(k == FC - 1))
    ins.then_inc(sem("ff_ps"), 1)
    pe.wait_ge(sem("xp"), 1)
    for c in range(CHUNKS):
        for t in range(TC):
            ins = pe.matmul(ps[:, c, P * t:P * t + P], f["selT"][:, P * (TC * c + t):P * (TC * c + t) + P],
                            f["xp"], start=True, stop=True)
        ins.then_inc(sem("back_ps"), 1)


def layouts(i):
    def c(x):
        return np.ascontiguousarray(x)

    def rows(x):
        return c(np.broadcast_to(x, (P, x.shape[-1])))

    f4 = np.float32
    hd = np.arange(P) % DH
    inv = (1.0 / 10000.0 ** (np.arange(0, 4, 2, dtype=f4) / f4(4))).astype(f4)
    angle = (np.arange(T, dtype=f4)[:, None] * inv[None, :]).astype(f4)
    angle = np.concatenate((angle, angle), -1).astype(np.float64)
    cos, sin = np.ones((P, T), f4), np.zeros((P, T), f4)
    for p in range(P):
        if hd[p] >= 4:
            cos[p], sin[p] = np.cos(angle[:, hd[p] - 4]), np.sin(angle[:, hd[p] - 4])
    k = np.arange(P)
    after = k[None, :] > k[:, None]
    return {
        "x": c(i["L0_attn_x"].reshape(B * T, C)),
        "ident": np.eye(P, dtype=f4),
        "masks": c(np.stack([np.where(after, f4(NEG), f4(0)), np.where(after.T, f4(NEG), f4(0))], 1)),
        "upq": c(np.concatenate([i["L0_attn_Wq_up_c"], i["L0_attn_Wq_up_e"]], 1)),
        "upk": c(np.concatenate([i["L0_attn_Wk_up_c"], i["L0_attn_Wk_up_e"]], 1)),
        "upv": c(i["L0_attn_Wv_up"]),
        "down": c(np.stack([i[f"L0_attn_W{s}_down"].T.reshape(H, LAT, C).transpose(1, 0, 2) for s in "qkv"], 1)),
        "rope": c(np.stack([cos, sin], 1)),
        "wo0": c(i["L0_attn_Wc"]),
        "gateT": c(i["L0_ffn_gate_w"].T),
        "pick": c((np.arange(P)[:, None] // 3 == np.arange(E)[None, :]).astype(f4)),
        "ebias": rows(i["L0_ffn_expert_bias"]),
        "before8": c(np.broadcast_to((np.arange(E)[None, :] < np.arange(E)[:, None]).astype(f4), (P, E, E))),
        "wupT": c(i["L0_ffn_w_up"].transpose(2, 0, 1).reshape(C, E * HID)),
        "wdnT": c(i["L0_ffn_w_down"].reshape(E, C, 2, HH).transpose(3, 0, 2, 1).reshape(HH, E * 2 * C)),
        "supT": c(i["L0_ffn_shared_w_up"].T),
        "sdnT": c(i["L0_ffn_shared_w_down"].reshape(C, 2, HH).transpose(2, 1, 0)),
        "wq1": c(i["L1_attn_Wq"].T), "wk1": c(i["L1_attn_Wk"].T), "wv1": c(i["L1_attn_Wv"].T),
        "wo1": c(i["L1_attn_Wo"].T),
        "bqk": c(np.stack([i["L1_attn_bq"], i["L1_attn_bk"]], 1)),
        "bvo": c(np.stack([i["L1_attn_bv"], i["L1_attn_bo"]], 0)[None]),
        "wr": rows(i["L1_ffn_w_router"]),
        "iota": c(np.broadcast_to(k.astype(f4), (P, P))),
        "offset": c(np.broadcast_to((np.arange(TILES) // KT * TOP).astype(f4), (P, TILES))),
        "tri": c((~after & (k[None, :] != k[:, None])).astype(f4)),
        "g1": rows(i["L1_ffn_g1"]), "g2": rows(i["L1_ffn_g2"]),
        "qkvT": c(i["L1_ffn_W_qkv"].T), "woutT": c(i["L1_ffn_W_out"].T),
        "w1T": c(np.pad(i["L1_ffn_W1"].T, ((0, 0), (0, FC * P - DFF)))),
        "w2T": c(np.pad(i["L1_ffn_W2"].T, ((0, 0), (0, FC * P - DFF)))),
        "w3T": c(np.pad(i["L1_ffn_W3"].T, ((0, FC * P - DFF), (0, 0))).reshape(FC, P, C).transpose(1, 0, 2)),
        "headmask": c((k[:, None] // DH == np.arange(H)[None, :]).astype(f4)),
        "mask2": c(np.where(after | (k[None, :] // TOP != k[:, None] // TOP), f4(NEG), f4(0))),
    }


def kernel(**inputs):
    import concourse.bacc as bacc
    from concourse.bass_utils import run_bass_kernel_spmd

    arrays = layouts({name: np.asarray(v) for name, v in inputs.items()})
    nc = bacc.Bacc("TRN2", target_bir_lowering=False, num_devices=1)
    a = {name: nc.dram_tensor(name + "_in", v.shape, mybir.dt.from_np(v.dtype), kind="ExternalInput").ap()
         for name, v in arrays.items()}
    out = nc.dram_tensor("out", (B * T, C), F32, kind="ExternalOutput").ap()
    build(nc, a, out)
    got = run_bass_kernel_spmd(nc, [{name + "_in": v for name, v in arrays.items()}], core_ids=[0])
    return got.results[0]["out"].reshape(B, T, C)
```

```python
from contextlib import ExitStack

import numpy as np

from concourse import mybir

F32 = mybir.dt.float32
BF16 = mybir.dt.bfloat16
ACT = mybir.ActivationFunctionType
ALU = mybir.AluOpType
AX = mybir.AxisListType

P = 128
B, T, C = 2, 1024, 128
H, DH, LAT = 16, 8, 64
TILES = B * T // P
CHUNKS = 4
TC = TILES // CHUNKS
CW = TC * P
G = 4
NG = B * H // G
KT = T // P
E, HID, HH = 8, 176, 88
TOP = 64
DFF, FC = 341, 3
SCALE = 1.0 / float(np.sqrt(DH))
LN_EPS, RMS_EPS = 1e-5, 1e-6
NEG = -1e30
Q_PARTS = (0, 0, 1, 1, 0, 2)
K_PARTS = (0, 1, 0, 1, 2, 0)
NPROD = len(Q_PARTS)
STACK = DH * NPROD
STACK_M = STACK + 3
VW = DH + 1
JOBS = KT * G


TURN_AT, BRANCH_AT = 3, 5
LAST_PARTS_AT = (8, 16)
EARLY_MAX = JOBS // 2 + 3
JOB_COST = 0.5


class Plan:

    def __init__(self, causal):
        self.causal = causal
        self.done_by = (2, 2, 2, 3, 4) if causal else (0, 0, 0, 0, 4)
        self.steps = [(qh, kt) for qh in range(2) for kt in range(4 * qh + 4 if causal else KT)]
        self.n = len(self.steps)
        self.jobs = [(qt, j) for qt in range(KT) for j in range(G)]
        job_cost = [self.keys(qt) // P + JOB_COST for qt, _ in self.jobs]
        step_cost = [4 - self.skipped(qh, kt) // P for qh, kt in self.steps]
        self.beside, at, done = [], 0, 0.0
        for i in range(self.n):
            done += step_cost[i] * sum(job_cost) / sum(step_cost)
            upto = at
            while upto < JOBS and (sum(job_cost[:upto + 1]) <= done + 1e-6 or i == self.n - 1):
                upto += 1
            self.beside.append(list(range(at, upto)))
            at = upto
        self.half = next(i for i, (qh, _) in enumerate(self.steps) if qh == 1)
        first_max = next(i for i, b in enumerate(self.beside) if JOBS // 2 - 1 in b)
        self.small = {0: "max1", 2: "out1", self.half + 1: "out0",
                      max(self.half + 2, first_max + 2): "max0"}
        assert len(self.small) == 4 and max(self.small) < self.n

    def keys(self, qt):
        return (qt + 1) * P if self.causal else T

    def single(self, jj):
        return self.causal and self.jobs[jj][0] < 4

    def first_bank(self, jj):
        return jj % 4 if self.single(jj) else 2 * (jj % 2)

    def maxima_before(self, jj):
        if self.single(jj):
            return (-1, -1, 0, 0)[jj] if jj < 4 else jj - 3
        return jj - 2 if jj and self.single(jj - 1) else jj - 1

    def skipped(self, qh, kt):
        return max(0, kt * P - qh * 512) if self.causal else 0

    def diagonal(self, qh, kt):
        return self.causal and kt * P >= qh * 512


PLANS = (Plan(True), Plan(False))
NORMS = {("ln0", 1): 0, ("post0", 0): 1, ("post0", 1): 2, ("post1", 0): 3, ("post1", 1): 4,
         ("post2", 0): 5, ("post2", 1): 6, ("post3", 0): 7}
ADDS = {"post0": 0, "post1": 1, "post2": 2, "post3": 3}
TURNED = {"ln0": 0, "post0": 1, "post1": 2}


def norms_before(name, half, c):
    if name == "post1":
        return CHUNKS * NORMS[name, 0] + (2 * c + half if c < 2 else 2 * half + c + 2)
    if name in ("post0", "post2"):
        return CHUNKS * NORMS[name, 0] + CHUNKS * (c // 2) + 2 * half + c % 2
    return CHUNKS * NORMS[name, half] + c


def adds_before(name, c):
    return CHUNKS * ADDS[name] + c


def turned_before(name, c):
    return CHUNKS * TURNED[name] + c - (2 if name == "post1" else 0)


UNITS = [(kind, c * E + e if kind == "expert" else c) for c in range(CHUNKS)
         for kind, e in [("shared", 0)] + [("expert", e) for e in range(E)]]
for _at, _unit in ((8, ("parts", 1)), (15, ("back", 0)), (16, ("parts", 2)), (19, ("parts", 3)), (24, ("turn", 0)),
                   (27, ("back", 1)), (36, ("turn", 1)), (38, ("back", 2)), (39, ("q", 0)), (41, ("k", 1)),
                   (45, ("v", 0))):
    UNITS.insert(_at, _unit)
HALVES = [1 if _kind in ("parts", "back", "turn") else 2 for _kind, _ in UNITS]
SPREAD_BANK = (0, 4)
SLOTS = 3
AHEAD, DOWN, ROUND, ADD, SUM = 3, 2, 2, 3, 4


def unit(kind, n):
    return UNITS.index((kind, n))


def halves_before(v):
    return sum(HALVES[:v])


def through(kind, n):
    return halves_before(unit(kind, n) + 1)


def half_bank(h):
    return 1 + h % 3


def expert(v):
    return UNITS[v][1] if 0 <= v < len(UNITS) and UNITS[v][0] == "expert" else None


BESIDE_EXPERTS = {17: ("moments", 0, 0), 19: ("norm", 0, 0), 21: ("moments", 1, 0), 23: ("norm", 1, 0),
                  29: ("moments", 0, 1), 31: ("norm", 0, 1), 33: ("moments", 1, 1), 35: ("norm", 1, 1),
                  40: ("rest", 0, 0), 42: ("rest", 0, 1), 43: ("part", 0, 0), 44: ("part", 0, 1),
                  45: ("moments", 0, 2), 47: ("norm", 0, 2)}
ROUTE_AT = {1: 1, 2: 6, 3: 11}
ROUTE_STEPS = 9
BESIDE_FIRST = {"moments0": 0, "norm0": 0, "moments1": 0, "norm1": 0, "turn": 0, "q": 2, "k": 5, "v": 8,
                "part2": 6, "part3": 10}


def qk_full(L, w):
    if L == 0:
        return "qk_full0", w + 1
    return ("unit_read", through("qk"[w], w)) if w < 2 else ("qk_full1", w - 1)


def values_done(L, b):
    if L == 0:
        return "v_done0", 4 * b + 4
    return ("unit_read", through("v", 0)) if b == 0 else ("v_done1", 4)


def rounded_by_dve(u):
    return u % 4 == 3


TURN = {"max1": 0, "out1": 1, "out0": 2, "max0": 3}


def turn(kind, n, first=False):
    if first:
        return {"max1": 1, "out0": 2, "max0": 3}[kind]
    return 4 * n + TURN[kind]


def second_bank(j, last):
    return j if last else 4 + j % 2


def periods(eng, emit, last=NG - 1):
    emit(0, 0, 0, True, False)
    with eng.Fori(0, (NG - 2) // 2) as i:
        emit(2 * i + 1, 1, i, False, False)
        emit(2 * i + 2, 0, i + 1, False, False)
    emit(NG - 1, 1, NG // 2 - 1, False, True)


def build(nc, a, out):
    ctx = ExitStack()
    with ctx:
        sems = {}

        def sb(name, shape, dt=F32):
            return ctx.enter_context(nc.sbuf_tensor(name, shape, dt))

        def sem(name):
            if name not in sems:
                sems[name] = ctx.enter_context(nc.semaphore(name))
            return sems[name]

        def dram(name, shape, dt):
            return nc.dram_tensor(name, shape, dt, kind="Internal").ap()

        X = sb("X", [P, TILES, C])
        XN = sb("XN", [P, TILES, C])
        XNT = sb("XNT", [P, TILES * P])
        TMP = sb("TMP", [P, TILES, C])
        Y = sb("Y", [P, KT, NG, G * DH])
        YB = Y[:, :, :, :].rearrange("p k n d -> p (k n d)").rearrange("p (t c) -> p t c", t=TILES)
        YT = sb("YT", [P, TILES * P])
        bn = sb("bn", [P, TILES, 6])
        mv = sb("mv", [P, TILES, 2])
        veps = sb("veps", [P, TILES])
        rstd = sb("rstd", [P, TILES])
        neg_mean = sb("neg_mean", [P, TILES])
        shift = sb("shift", [P, TILES])
        neg_half = sb("neg_half", [P, TILES])
        ident = sb("ident", [P, P])
        masks = sb("masks", [P, 2, P])
        ident_bf = sb("ident_bf", [P, P], BF16)
        mask_bf = sb("mask_bf", [P, 2, P], BF16)
        ones_row = sb("ones_row", [1, P])
        ones_bf = sb("ones_bf", [P, 2], BF16)
        rope = TMP[:, :, :].rearrange("p t c -> p (t c)").rearrange("p (a t) -> p a t", a=2)
        arena = sb("arena", [P, 6144])
        down = arena[:, 0:3 * (H // 2) * C].rearrange("p (s h c) -> p s h c", s=3, h=H // 2)
        parts = [arena[:, :].bitcast(BF16).rearrange("p (u k t) -> p u k t", u=4, k=3)[:, w ^ 2 * L]
                 for L in range(2) for w in range(4)]
        ups = sb("ups", [P, 5, DH])
        ups2 = sb("ups2", [P, 2, 5, DH])
        wqk = [sb(f"wqk{i}", [C, 2, 2, H * DH]) for i in range(2)]
        wv = [sb(f"wv{i}", [C, H * DH]) for i in range(2)]
        wo = [sb(f"wo{i}", [C, C]) for i in range(2)]
        bqk = sb("bqk", [P, 2])
        bvo = sb("bvo", [1, 2, C])
        full = sb("full", [P, 2, T])
        rest = sb("rest", [P, 2, T])
        Vx = sb("Vx", [P, NG, KT, G, VW])
        SQ, TQ = (sb(n, [P, 2, G, T], BF16) for n in ("SQ", "TQ"))
        SK, TK = (sb(n, [P, 2, G // 2, T], BF16) for n in ("SK", "TK"))
        VS = sb("VS", [P, 2, KT, G, VW])
        probs = sb("probs", [P, 2, G, 512])
        nmax = sb("nmax", [P, 2, 2, 2, 8])
        nmax_rest = sb("nmax_rest", [P, 2, 2, 2, 8])
        nmax3_cols = sb("nmax3", [P, 2, 2, P], BF16)
        nmax3 = nmax3_cols[:, :, :, 0:48].rearrange("p g h (e i x) -> p g h e i x", e=2, i=3)
        zeros = sb("zeros", [P, 16])
        nmaxT = sb("nmaxT", [48, 2, 2, P], BF16)
        OS = sb("OS", [P, 2, 512])
        rden = sb("rden", [P, 2, 16])
        gateT = sb("gateT", [C, E])
        ebias = sb("ebias", [P, E])
        before8 = sb("before8", [P, E, E])
        moe_f = probs[:, :, :, :].rearrange("p a j q -> p (a j q)")[:, 0:E * (HID + 2 * C)]
        moe_b = sb("moe_b", [P, E * (HID + 2 * C)], BF16)
        wup_bf = moe_b[:, 0:E * HID].rearrange("p (e h) -> p e h", e=E)
        wdn_bf = moe_b[0:HH, E * HID:].rearrange("p (e k c) -> p e k c", e=E, k=2)
        supT = sb("supT", [C, HID])
        sdnT = sb("sdnT", [HH, 2, C])
        esc = sb("esc", [P, TILES, E])
        ebi = sb("ebi", [P, TILES, E])
        erank = sb("erank", [P, TILES, E])
        chosen = sb("chosen", [P, TILES, E])
        pick = sb("pick", [P, E])
        pick_bf = sb("pick_bf", [P, E], BF16)
        arena_bf = arena[:, :].bitcast(BF16)
        probs_bf = [probs[:, a, b, :].bitcast(BF16) for a, b in ((0, 3), (1, 2), (1, 3))]
        xsT = [arena_bf[:, CW * i:CW * i + CW] for i in range(2)] + [probs_bf[0][:, 0:CW]]
        eout = [arena_bf[:, CW * i:CW * i + CW] for i in range(2, 4)] + [probs_bf[0][:, CW:]]
        hrelu = [t[0:HH, :].rearrange("p (k q) -> p k q", k=2)
                 for t in (arena_bf[:, 4 * CW:6 * CW], arena_bf[:, 6 * CW:8 * CW], probs_bf[1])]
        hsq = [t[0:HH, :].rearrange("p (k q) -> p k q", k=2)
               for t in (arena_bf[:, 8 * CW:10 * CW], arena_bf[:, 10 * CW:12 * CW], probs_bf[2])]
        cmp = arena[:, 3072:3072 + 2 * TILES * E * E].rearrange("p (x t e j) -> p x t e j", x=2, t=TILES, e=E)
        esc3_cols = arena_bf[:, 20 * CW:24 * CW].rearrange("p (t x) -> p t x", t=TILES)
        esc3 = esc3_cols[:, :, 0:3 * E].rearrange("p t (e i) -> p t e i", e=E)
        esc_rest = probs[:, 0, 2, 0:TILES * E].rearrange("p (t e) -> p t e", t=TILES)
        esc3T = YT[:, :].bitcast(BF16)[:, 0:B * T]
        hs = probs[0:HH, 0, 0:2, :]
        hs2 = probs[0:HH, 1, 0:2, :]

        ps = ctx.enter_context(nc.psum_tensor("ps", [P, 8, 512], F32))

        def bank(i, n=1):
            return ps[:, i:i + n, :].rearrange("p a b -> p (a b)")

        split_d = [dram(f"split{i}", [2, B, 3, P, T], BF16) for i in range(2)]
        stack_d = [dram(f"stack{i}", [2, NG, 2, P, T], BF16) for i in range(2)]
        nmax_d = [dram(f"nmaxd{i}", [2, 2, 48, P], BF16) for i in range(2)]

        FF = ffn_buffers(sb, full, rest, XNT, TMP, YT, arena)

        block = ctx.enter_context(nc.Block())

        @block.sync
        def _(sp):
            for b in range(B):
                sp.dma_start(X[:, KT * b:KT * b + KT, :],
                             a["x"].rearrange("(t p) c -> p t c", p=P)[:, KT * b:KT * b + KT, :])\
                    .then_inc(sem(f"x_in{b}"), 16)
            sp.dma_start(ident[:, :], a["ident"]).then_inc(sem("const_in"), 16)
            for q, name in ((0, "upq"), (2, "upk"), (4, "upv")):
                sp.dma_start(ups[:, q, :], a[name]).then_inc(sem("ups_in"), 16)
            sp.dma_start(down, a["down"]).then_inc(sem("down_in"), 16)
            sp.dma_start(masks[:, :, :], a["masks"]).then_inc(sem("const_in"), 16)
            sp.dma_start(rope, a["rope"]).then_inc(sem("rope_in"), 16)
            later = [(wo[0][:, :], "wo0"), (gateT[:, :], "gateT"), (pick[:, :], "pick"), (ebias[:, :], "ebias"),
                     (before8[:, :, :], "before8"),
                     (moe_f[:, 0:E * HID], "wupT"), (moe_f[0:HH, E * HID:], "wdnT"),
                     (supT[:, :], "supT"), (sdnT[:, :, :], "sdnT"),
                     (wqk[1][:, 0, 0, :], "wq1"), (wqk[1][:, 1, 0, :], "wk1"), (wv[1][:, :], "wv1"),
                     (wo[1][:, :], "wo1"), (bqk[:, :], "bqk"), (bvo[:, :, :], "bvo")]
            later += [(FF[k], k) for k in FFN_INPUTS]
            for dst, key in later:
                sp.dma_start(dst, a[key]).then_inc(sem("later_in"), 16)
            assert len(later) == LATER

            def part_out(L, w, k):
                b, side = w // 2, w % 2
                sp.wait_ge(sem((f"part0_{L}", f"part1_{L}", f"split_done{L}")[k]), w + 1)
                sp.dma_start(split_d[L][side, b, k], parts[4 * L + w][:, k, :]).then_inc(sem(f"part_out{w}{k}"), 16)

            def stack(L, w, k):
                b, side = w // 2, w % 2
                sp.wait_ge(sem(f"part_out{w}{k}"), 16 * (L + 1))
                rows = stack_d[L][side, NG // 2 * b:NG // 2 * (b + 1)]\
                    .rearrange("g r (e s) t -> (g r e) s t", e=2)
                for i, part in enumerate((Q_PARTS, K_PARTS)[side]):
                    if part == k:
                        sp.dma_start(rows[:, DH * i:DH * (i + 1), :],
                                     split_d[L][side, b, k].rearrange("(h d) t -> h d t", d=DH))\
                            .then_inc(sem(f"stacked{L}{b}"), 16)

            def restack(L, b):
                q, k = 2 * b, 2 * b + 1
                part_out(L, q, 0)
                part_out(L, k, 0)
                part_out(L, q, 1)
                stack(L, q, 0)
                part_out(L, k, 1)
                stack(L, k, 0)
                part_out(L, q, 2)
                stack(L, q, 1)
                part_out(L, k, 2)
                stack(L, k, 1)
                stack(L, q, 2)
                stack(L, k, 2)

            def load_first(L, n, par):
                for side, dst in ((0, SQ), (1, SK)):
                    for e in range(2):
                        heads = slice(e, G, 2) if side == 0 else slice(0, G // 2)
                        sp.dma_start(dst[64 * e:64 * e + STACK, par, heads, :],
                                     stack_d[L][side, n, :, 64 * e:64 * e + STACK, :]
                                     .rearrange("r s t -> s r t")).then_inc(sem(f"first_in{L}{par}"), 16)

            def load_second(L, n, par):
                for side, dst in ((0, TQ), (1, TK)):
                    for e in range(2):
                        heads = slice(e, G, 2) if side == 0 else slice(0, G // 2)
                        sp.dma_start(dst[64 * e:64 * e + STACK, par, heads, :],
                                     stack_d[L][side, n, :, 64 * e:64 * e + STACK, :]
                                     .rearrange("r s t -> s r t")).then_inc(sem(f"second_in{L}{par}"), 16)
                sp.dma_start(VS[:, par].rearrange("p k j v -> p (k j v)"),
                             Vx[:, n].rearrange("p k j v -> p (k j v)")).then_inc(sem(f"second_in{L}{par}"), 16)

            def place_max(L, turns, n, par, qh):
                sp.wait_ge(sem(f"small_done{L}"), turns + 1)
                sp.dma_start(nmax_d[L][par, qh], nmaxT[:, par, qh, :]).then_inc(sem(f"max_out{L}{qh}"), 16)
                sp.wait_ge(sem(f"max_out{L}{qh}"), 16 * (n + 1))
                for e in range(2):
                    sp.dma_start(TQ[64 * e + STACK:64 * e + STACK_M, par, e:G:2, 512 * qh:512 * qh + 512],
                                 nmax_d[L][par, qh, 24 * e:24 * e + 24, :]
                                 .rearrange("(i r q) t -> i r (q t)", i=3, r=2))\
                        .then_inc(sem(f"max_in{L}{qh}"), 16)

            for L, plan in enumerate(PLANS):
                if L == 0:
                    sp.wait_ge(sem("pool_const"), POOL_CONSTS)
                restack(L, 0)
                sp.wait_ge(sem(f"stacked{L}0"), 32 * NPROD)
                load_first(L, 0, 0)
                name, value = values_done(L, 0)
                sp.wait_ge(sem(name), value)
                load_second(L, 0, 0)
                load_first(L, 1, 1)
                load_second(L, 1, 1)
                restack(L, 1)
                place_max(L, 0, 0, 0, 0)

                def period(n, par, first=False, more_first=True, more_second=True, last=False):
                    if more_first and par == 0:
                        if not first:
                            sp.wait_ge(sem(f"stacked{L}1"), 32 * NPROD)
                            name, value = values_done(L, 1)
                            sp.wait_ge(sem(name), value)
                    if more_first:
                        sp.wait_ge(sem(f"rowmax{L}"), JOBS * (n + 1))
                        load_first(L, n + 2, par)
                    if not first and more_second:
                        sp.wait_ge(sem(f"pv{L}"), plan.n * n)
                        load_second(L, n + 1, 1 - par)
                    place_max(L, turn("max1", n, first), n, par, 1)
                    if not last:
                        place_max(L, turn("max0", n, first), n + 1, 1 - par, 0)

                period(0, 0, first=True)
                with sp.Fori(0, 2) as i:
                    period(2 * i + 1, 1)
                    period(2 * i + 2, 0)
                period(5, 1)
                period(6, 0, more_first=False)
                period(7, 1, more_first=False, more_second=False, last=True)

            for c in range(CHUNKS):
                sp.wait_ge(sem("x_added"), adds_before("post3", c) + 1)
                sp.dma_start(out.rearrange("(t p) c -> p t c", p=P)[:, TC * c:TC * c + TC, :],
                             X[:, TC * c:TC * c + TC, :]).then_inc(sem("stored"), 16)
            sp.wait_ge(sem("stored"), 16 * CHUNKS)

        @block.gpsimd
        def _(pool):
            pool.memset(neg_half[:, :], -0.5).then_inc(sem("pool_const"), 1)
            pool.wait_ge(sem("pool_const"), 1)

            def inv_std(name, c, half):
                done, k = sem("norm_rstd"), norms_before(name, half, c)
                t = slice(TC * c, TC * c + TC)
                pool.wait_ge(sem("norm_stats"), k + 1)
                pool.tensor_scalar(veps[:, t], mv[:, t, 1], LN_EPS, None, ALU.add).then_inc(done, 1)
                if by_act(name, c):
                    pool.tensor_scalar(neg_mean[:, t], mv[:, t, 0], -1.0, None, ALU.mult)\
                        .then_inc(sem("neg_mean"), 1)
                pool.wait_ge(done, 2 * k + 1)
                pool.tensor_tensor(rstd[:, t], veps[:, t], neg_half[:, t], ALU.pow).then_inc(done, 1)
                if by_act(name, c):
                    pool.wait_ge(sem("neg_mean"), act_norms(name, half, c))
                    pool.wait_ge(done, 2 * k + 2)
                    pool.tensor_tensor(shift[:, t], neg_mean[:, t], rstd[:, t], ALU.mult).then_inc(sem("shift"), 1)

            def residual(name, c):
                pool.wait_ge(sem("normed"), TC * (norms_before(name, 0, c) + 1))
                t = slice(TC * c, TC * c + TC)
                pool.tensor_tensor(X[:, t, :], X[:, t, :], TMP[:, t, :], ALU.add)\
                    .then_inc(sem("x_added"), 1)

            def post(name, more):
                for chunks in (range(2), range(2, CHUNKS)):
                    for half in range(1 + more):
                        for c in chunks:
                            inv_std(name, c, half)

            def split(L, w):
                pool.wait_ge(sem(f"part0_{L}"), w + 1)
                pool.tensor_tensor(rest[:, w % 2, :], full[:, w % 2, :], parts[4 * L + w][:, 0, :],
                                   ALU.subtract).then_inc(sem(f"rest_{L}"), 1)

            def split_max(L):
                step = sem(f"max3_{L}")
                zero = zeros[:, :].rearrange("p (e x) -> p e x", e=2)

                def one(n, par):
                    for qh in range(2):
                        at = 8 * n + 4 * qh
                        src, left = nmax[:, par, qh], nmax_rest[:, par, qh]
                        dst = nmax3[:, par, qh]
                        pool.wait_ge(sem(f"rowmax{L}"), JOBS * n + JOBS // 2 * (qh + 1))
                        pool.tensor_tensor(dst[:, :, 0, :], src, zero, ALU.add).then_inc(step, 1)
                        pool.wait_ge(step, at + 1)
                        pool.tensor_tensor(left, src, dst[:, :, 0, :], ALU.subtract).then_inc(step, 1)
                        pool.wait_ge(step, at + 2)
                        pool.tensor_tensor(dst[:, :, 1, :], left, zero, ALU.add).then_inc(step, 1)
                        pool.wait_ge(step, at + 3)
                        pool.tensor_tensor(dst[:, :, 2, :], left, dst[:, :, 1, :], ALU.subtract)\
                            .then_inc(step, 1)

                with pool.Fori(0, NG // 2) as i:
                    one(2 * i, 0)
                    one(2 * i + 1, 1)

            inv_std("ln0", 0, 1)
            inv_std("ln0", 1, 1)
            inv_std("ln0", 2, 1)
            inv_std("ln0", 3, 1)
            constants = ((zeros[:, :], 0.0), (TK[:, :, :, :], 1.0), (Vx[:, :, :, :, :], 1.0),
                         (ones_row[:, :], 1.0), (ones_bf[:, :], 1.0), (nmax3_cols[:, :, :, :], 0.0),
                         (SK[:, :, :, :].bitcast(F32), 0.0), (SQ[:, :, :, :].bitcast(F32), 0.0),
                         (TQ[:, :, :, :].bitcast(F32), 0.0))
            assert len(constants) + 1 == POOL_CONSTS
            for dst, value in constants:
                pool.memset(dst, value).then_inc(sem("pool_const"), 1)
            pool.wait_ge(sem("pool_const"), POOL_CONSTS)
            for w in range(4):
                split(0, w)
            split_max(0)
            post("post0", True)
            pool.memset(esc3_cols.bitcast(F32), 0.0).then_inc(sem("score3_zero"), 1)
            pool.wait_ge(sem("score3_zero"), 1)
            def score_parts(c):
                t, n = slice(TC * c, TC * c + TC), 5 * c
                src, left = esc[:, t], esc_rest[:, t]
                no_score = zeros[:, 0:E].unsqueeze(1).to_broadcast([P, TC, E])
                step = sem("score3")
                pool.wait_ge(sem("chosen"), c + 1)
                pool.tensor_tensor(esc3[:, t, :, 0], src, no_score, ALU.add).then_inc(step, 1)
                pool.wait_ge(step, n + 1)
                pool.tensor_tensor(left, src, esc3[:, t, :, 0], ALU.subtract).then_inc(step, 1)
                pool.wait_ge(step, n + 2)
                pool.tensor_tensor(esc3[:, t, :, 1], left, no_score, ALU.add).then_inc(step, 1)
                pool.wait_ge(step, n + 3)
                pool.tensor_tensor(left, left, esc3[:, t, :, 1], ALU.subtract).then_inc(step, 1)
                pool.wait_ge(step, n + 4)
                pool.tensor_tensor(esc3[:, t, :, 2], left, no_score, ALU.add).then_inc(step, 1)

            def shared_square(c):
                pool.wait_ge(sem("unit_read"), through("shared", c))
                if c:
                    pool.wait_ge(sem("shared_ps"), c)
                pool.tensor_tensor(hs2, hs, hs, ALU.mult).then_inc(sem("shared_sq"), 1)

            score_parts(0)
            shared_square(0)
            score_parts(1)
            shared_square(1)
            score_parts(2)
            score_parts(3)
            inv_std("post1", 0, 0)
            residual("post1", 0)
            inv_std("post1", 0, 1)
            shared_square(2)
            inv_std("post1", 1, 0)
            residual("post1", 1)
            inv_std("post1", 1, 1)
            shared_square(3)
            inv_std("post1", 2, 0)
            residual("post1", 2)
            inv_std("post1", 3, 0)
            residual("post1", 3)
            inv_std("post1", 2, 1)
            inv_std("post1", 3, 1)
            split(1, 2)
            split(1, 3)
            split_max(1)
            post("post2", True)
            for i in range(2):
                pool.wait_ge(sem("ssq"), i + 1)
                pool.tensor_scalar(FF["small"][:, 2 * i:2 * i + 1], FF["ssq"][:, i:i + 1], 1.0 / C, RMS_EPS,
                                   ALU.mult, ALU.add).then_inc(sem("rms"), 1)
                pool.wait_ge(sem("rms"), 2 * i + 1)
                pool.tensor_tensor(FF["small"][:, 2 * i + 1:2 * i + 2], FF["small"][:, 2 * i:2 * i + 1],
                                   neg_half[:, 0:1], ALU.pow).then_inc(sem("rms"), 1)
            post("post3", False)

        @block.scalar
        def _(act):
            act.wait_ge(sem("const_in"), 32)
            act.activation(ident_bf[:, :], ident[:, :], ACT.Copy).then_inc(sem("act_const"), 1)
            act.activation(mask_bf[:, :, :], masks[:, :, :], ACT.Copy).then_inc(sem("act_const"), 1)

            def norm(name, half, c, src, dst):
                act.wait_ge(sem("shift"), act_norms(name, half, c))
                for t in range(TC):
                    i = TC * c + t
                    act.activation(dst[:, i, :], src(c, t), ACT.Identity, bias=shift[:, i:i + 1],
                                   scale=rstd[:, i:i + 1]).then_inc(sem("normed"), 1)

            def x_tile(c, t):
                return X[:, TC * c + t, :]

            def ps_tile(c, t):
                return ps[:, 4 + c, P * t:P * t + P]

            def yb_tile(c, t):
                return YB[:, TC * c + t, :]

            def post(name, src, more, chunks):
                for c in chunks:
                    norm(name, 0, c, src, TMP)
                if more:
                    for c in chunks:
                        norm(name, 1, c, x_tile, XN)

            def to_xnT(name, banks, chunks=range(CHUNKS)):
                for c in chunks:
                    act.wait_ge(sem("xnT_ps"), turned_before(name, c) + 1)
                    act.activation(XNT[:, CW * c:CW * c + CW], bank(banks[c]), ACT.Copy)\
                        .then_inc(sem("xnT"), 1)

            def q_or_k(w, at, ready, count, done):
                act.wait_ge(sem(ready), count)
                if w >= 2:
                    act.wait_ge(sem("split_done1"), w - 1)
                act.activation(full[:, w % 2, :], bank(at, 2), ACT.Identity,
                               bias=bqk[:, w % 2:w % 2 + 1]).then_inc(sem(done), 1)

            def part(L, w, k):
                name, value = qk_full(L, w) if k == 0 else (f"rest_{L}", w + 1)
                act.wait_ge(sem(name), value)
                act.activation(parts[4 * L + w][:, k, :], (full, rest)[k][:, w % 2, :], ACT.Copy)\
                    .then_inc(sem(f"part{k}_{L}"), 1)

            def values(L, b, at):
                v = bank(at, 2).rearrange("p (k g j d) -> p k g j d", k=KT, g=G, j=G)
                return [act.activation(Vx[:, G * b + g, :, :, 0:DH], v[:, :, g], ACT.Copy) for g in range(G)]

            def attend(L, plan):
                exps, pv, ev = sem(f"exp{L}"), sem(f"pv{L}"), sem(f"out_copied{L}")

                def copy_out(qh, turns, n_pv):
                    act.wait_ge(pv, n_pv)
                    act.activation(OS[:, qh, :], bank(6), ACT.Copy).then_inc(ev, 1)

                def period(n, par, rounds, first, last):
                    for s, (qh, kt) in enumerate(plan.steps):
                        c0 = plan.skipped(qh, kt)
                        for j in range(G):
                            act.wait_ge(sem(f"second_ps{L}"), (plan.n * n + s) * G + j + 1)
                            if j == 0 and not (first and s < 2):
                                act.wait_ge(pv, plan.n * n + s - 1)
                            act.activation(probs[:, s % 2, j, c0:512], ps[:, second_bank(j, last), c0:512],
                                           ACT.Exp, scale=SCALE).then_inc(exps, 1)
                        if s == 0 and not first:
                            copy_out(1, None, plan.n * n)
                        if s == plan.half:
                            copy_out(0, None, plan.n * n + plan.half)

                periods(act, period)
                copy_out(1, None, plan.n * NG)

            def copy_yT(L):
                for c in (2, 3):
                    act.wait_ge(sem(f"yT_ps{L}"), c + 1)
                    act.activation(YT[:, CW * c:CW * c + CW], bank(c), ACT.Copy).then_inc(sem(f"yT{L}"), 1)

            to_xnT("ln0", LN0_BANK, range(2))
            part(0, 0, 0)
            part(0, 1, 0)
            part(0, 0, 1)
            part(0, 1, 1)
            act.wait_ge(sem("v_ps0"), 1)
            for ins in values(0, 0, V_BANK[0][0]):
                ins.then_inc(sem("v_done0"), 1)
            to_xnT("ln0", LN0_BANK, range(2, CHUNKS))
            part(0, 2, 0)
            part(0, 3, 0)
            part(0, 2, 1)
            part(0, 3, 1)
            act.wait_ge(sem("v_ps0"), 2)
            for ins in values(0, 1, V_BANK[0][1]):
                ins.then_inc(sem("v_done0"), 1)
            act.wait_ge(sem("later_in"), 16 * LATER)
            act.activation(moe_b[:, 0:E * HID], moe_f[:, 0:E * HID], ACT.Copy).then_inc(sem("moe_bf"), 1)
            act.activation(moe_b[0:HH, E * HID:], moe_f[0:HH, E * HID:], ACT.Copy).then_inc(sem("moe_bf"), 1)
            act.wait_ge(sem("moe_bf"), 2)
            act.activation(pick_bf[:, :], pick[:, :], ACT.Copy).then_inc(sem("moe_bf"), 1)
            act.activation(FF["count"][:, :, 0], FF["earlier"], ACT.Copy).then_inc(sem("moe_bf"), 1)
            attend(0, PLANS[0])
            copy_yT(0)
            post("post0", ps_tile, True, (2, 3))
            def gate_exp(c):
                act.wait_ge(sem("gate_ps"), c + 1)
                act.activation(esc[:, TC * c:TC * c + TC, :].rearrange("p t e -> p (t e)"),
                               bank(4 + c)[:, 0:TC * E], ACT.Exp, scale=-1.0).then_inc(sem("gate_exp"), 1)

            for c in range(CHUNKS):
                to_xnT("post0", range(CHUNKS), [c])
                if c:
                    gate_exp(c - 1)
            gate_exp(CHUNKS - 1)

            def copy_parts(at, c):
                return act.activation(esc3T[:, CW * c:CW * c + CW], bank(at).bitcast(BF16)[:, 0:CW], ACT.Copy)

            act.wait_ge(sem("esc3T_ps"), 1)
            copy_parts(0, 0).then_inc(sem("esc3T"), 1)

            def read_unit(v):
                kind, n = UNITS[v]
                for k in range(HALVES[v]):
                    h = halves_before(v) + k
                    src = bank(half_bank(h))
                    act.wait_ge(sem("unit_ps"), h + 1)
                    if kind == "shared":
                        if n and k == 0:
                            act.wait_ge(sem("shared_sq"), n)
                        ins = act.activation(hs[:, k, :], src[0:HH, :], ACT.Relu)
                    elif kind == "expert":
                        if n >= SLOTS and k == 0:
                            act.wait_ge(sem("hsq"), n - SLOTS + 1)
                        ins = act.activation(hrelu[n % SLOTS][:, k, :], src[0:HH, :], ACT.Relu)
                    elif kind == "parts":
                        ins = copy_parts(half_bank(h), n)
                    elif kind == "turn":
                        ins = act.activation(XNT[:, CW * n:CW * n + CW], src, ACT.Copy)
                    elif kind == "back":
                        ins = act.activation(YB[:, TC * n:TC * n + TC, :], src.rearrange("p (t c) -> p t c", t=TC),
                                             ACT.Copy)
                    elif kind == "v":
                        for g in range(G):
                            ins = act.activation(Vx[:, G * n + g, TC * k:TC * k + TC, :, 0:DH],
                                                 src.rearrange("p (k g j d) -> p k g j d", k=TC, g=G, j=G)[:, :, g],
                                                 ACT.Copy)
                    else:
                        ins = act.activation(full[:, n, CW * k:CW * k + CW], src, ACT.Identity,
                                             bias=bqk[:, n:n + 1])
                    ins.then_inc(sem("unit_read"), 1)

            def round_out(u):
                act.wait_ge(sem("down_ps"), u + 1)
                if u >= SLOTS:
                    act.wait_ge(sem("eacc"), u - SLOTS + 1)
                act.activation(eout[u % SLOTS], bank(5 + u % 2), ACT.Copy).then_inc(sem("eout_act"), 1)

            for i in range(len(UNITS) + SUM + 1):
                if i < len(UNITS):
                    read_unit(i)
                if i in (unit("q", 0), unit("k", 1)):
                    part(1, UNITS[i][1], 0)
                if i == unit("q", 0) + 2:
                    part(1, 0, 1)
                if i == unit("k", 1) + 2:
                    part(1, 1, 1)
                u = expert(i - ROUND)
                if u is not None and not rounded_by_dve(u):
                    round_out(u)
                u = expert(i - SUM)
                if u is not None and u % E == E - 1:
                    c = u // E
                    act.wait_ge(sem("eacc"), u + 1)
                    act.activation(OS[:, c % 2, :], bank(7), ACT.Copy).then_inc(sem("moe_sum"), 1)
            to_xnT("post1", TURN_BANK, range(2, CHUNKS))
            q_or_k(2, QK_BANK[1][2], "qk_ps1", 1, "qk_full1")
            part(1, 2, 0)
            q_or_k(3, QK_BANK[1][3], "qk_ps1", 2, "qk_full1")
            part(1, 3, 0)
            part(1, 2, 1)
            act.wait_ge(sem("v_ps1"), 1)
            for ins in values(1, 1, V_BANK[1][1]):
                ins.then_inc(sem("v_done1"), 1)
            part(1, 3, 1)
            attend(1, PLANS[1])
            copy_yT(1)
            post("post2", ps_tile, True, (2, 3))
            act_ffn(act, sem, bank, ps, FF)
            post("post3", yb_tile, False, range(CHUNKS))

        @block.vector
        def _(dve):
            def moments(name, half, c, src):
                st, k = sem("norm_bn"), norms_before(name, half, c)
                for t in range(TC):
                    dve.bn_stats(bn[:, TC * c + t, :], src(c, t)).then_inc(st, 1)
                for t in range(TC):
                    dve.wait_ge(st, TC * k + t + 1)
                    ins = dve.bn_aggr(mv[:, TC * c + t, :], bn[:, TC * c + t, :])
                ins.then_inc(sem("norm_stats"), 1)

            def norm(name, half, c, src, dst):
                dve.wait_ge(sem("norm_rstd"), 2 * norms_before(name, half, c) + 2)
                for t in range(TC):
                    i = TC * c + t
                    dve.tensor_scalar(dst[:, i, :], src(c, t), mv[:, i, 0:1], rstd[:, i:i + 1],
                                      ALU.subtract, ALU.mult).then_inc(sem("normed"), 1)

            def x_tile(c, t):
                return X[:, TC * c + t, :]

            def ps_tile(c, t):
                return ps[:, 4 + c, P * t:P * t + P]

            def yb_tile(c, t):
                return YB[:, TC * c + t, :]

            def residual(name, c):
                dve.wait_ge(sem("normed"), TC * (norms_before(name, 0, c) + 1))
                t = slice(TC * c, TC * c + TC)
                dve.tensor_tensor(X[:, t, :], X[:, t, :], TMP[:, t, :], ALU.add).then_inc(sem("x_added"), 1)

            def post(name, ready, src, more):
                for c in range(CHUNKS):
                    dve.wait_ge(sem(ready), c + 1)
                    moments(name, 0, c, src)
                for c in range(CHUNKS + 1):
                    if c < CHUNKS:
                        residual(name, c)
                    if more and c:
                        second_moments(name, c - 1)

            def second_moments(name, c):
                dve.wait_ge(sem("x_added"), adds_before(name, c) + 1)
                moments(name, 1, c, x_tile)

            def branch_moments(L, c):
                dve.wait_ge(sem(f"branch_ps{L}"), c + 1)
                moments(f"post{2 * L}", 0, c, ps_tile)

            def beside_last(L, s):
                name = f"post{2 * L}"
                if s == TURN_AT:
                    for c in range(2):
                        dve.wait_ge(sem(f"yT_ps{L}"), c + 1)
                        dve.tensor_copy(YT[:, CW * c:CW * c + CW], bank(4 + c)).then_inc(sem(f"yT{L}"), 1)
                if s == BRANCH_AT:
                    for c in range(2):
                        branch_moments(L, c)
                    for c in range(2):
                        norm(name, 0, c, ps_tile, TMP)
                    for c in range(2):
                        residual(name, c)
                    for c in range(2):
                        second_moments(name, c)
                    for c in range(2):
                        norm(name, 1, c, x_tile, XN)
                    if L:
                        router_scores(dve, sem, FF, XN, 0)
                        router_scores(dve, sem, FF, XN, 1)

            def last_part(L, w):
                dve.wait_ge(sem(f"part1_{L}"), w + 1)
                dve.tensor_tensor(parts[4 * L + w][:, 2, :], rest[:, w % 2, :], parts[4 * L + w][:, 1, :],
                                  ALU.subtract)\
                    .then_inc(sem(f"split_done{L}"), 1)

            def rotate(w):
                step = sem("rotated")
                dve.wait_ge(sem("qk_ps0"), w + 1)
                if w >= 2:
                    dve.wait_ge(sem("split_done0"), w - 1)
                dve.tensor_tensor(full[:, w % 2, :], bank(QK_BANK[0][w], 2), rope[:, 0, :], ALU.mult)\
                    .then_inc(step, 1)
                dve.tensor_tensor(rest[:, w % 2, :], bank(QK_BANK[0][w] + 2, 2), rope[:, 1, :], ALU.mult)\
                    .then_inc(step, 1)
                dve.wait_ge(step, 2 * w + 2)
                dve.tensor_tensor(full[:, w % 2, :], full[:, w % 2, :], rest[:, w % 2, :], ALU.add)\
                    .then_inc(sem("qk_full0"), 1)

            def attend(L, plan, beside_first):
                maxed, small = sem(f"rowmax{L}"), sem(f"small_done{L}")

                def row_max(n, par, jj):
                    qt, j = plan.jobs[jj]
                    pair, e = divmod(j, 2)
                    dve.wait_ge(sem(f"first_ps{L}"), JOBS * n + jj + 1)
                    dve.tensor_reduce(nmax[:, par, qt // 4, e, 4 * pair + qt % 4:4 * pair + qt % 4 + 1],
                                      bank(plan.first_bank(jj), 1 if plan.single(jj) else 2)[:, 0:plan.keys(qt)], AX.X, ALU.max, negate=True)\
                        .then_inc(maxed, 1)

                def copy_max(turns, par, qh):
                    dve.wait_ge(sem(f"small_ps{L}"), turns + 1)
                    dve.tensor_copy(nmaxT[:, par, qh, :], bank(7).bitcast(BF16)[0:48, 0:P]).then_inc(small, 1)

                def normalise(turns, n, qh):
                    dve.wait_ge(sem(f"small_ps{L}"), turns + 1)
                    o = bank(7).rearrange("p (x v) -> p x v", v=32)
                    dve.reciprocal(rden[:, qh, :], o[:, :, DH]).then_inc(sem(f"rden{L}"), 1)
                    dve.wait_ge(sem(f"rden{L}"), 2 * n + qh + 1)
                    dve.tensor_tensor(Y[:, 4 * qh:4 * qh + 4, n, :].rearrange("p k (j d) -> p k j d", j=G),
                                      o[:, :, 0:DH].rearrange("p (k j) d -> p k j d", j=G),
                                      rden[:, qh, :].rearrange("p (k j) -> p k j", j=G).unsqueeze(3)
                                      .to_broadcast([P, 4, G, DH]), ALU.mult)\
                        .then_inc(small, 1)

                for jj in range(JOBS):
                    beside_first(jj)
                    row_max(0, 0, jj)
                    if jj == EARLY_MAX:
                        copy_max(0, 0, 0)

                def period(n, par, rounds, first, last):
                    for s in range(plan.n):
                        if last:
                            beside_last(L, s)
                        if not last:
                            for jj in plan.beside[s]:
                                row_max(n + 1, 1 - par, jj)
                        kind = plan.small.get(s)
                        if kind == "max1":
                            copy_max(turn(kind, n, first), par, 1)
                        if kind == "max0" and not last:
                            copy_max(turn(kind, n, first), 1 - par, 0)
                        if kind == "out0":
                            normalise(turn(kind, n, first), n, 0)
                        if kind == "out1" and not first:
                            normalise(turn(kind, n, first), n - 1, 1)

                periods(dve, period)
                normalise(turn("max0", NG - 1), NG - 1, 1)

            dve.wait_ge(sem("x_in0"), 16)
            moments("ln0", 1, 0, x_tile)
            moments("ln0", 1, 1, x_tile)
            dve.wait_ge(sem("ups_in"), 48)
            for q in (0, 2):
                plain = ups[:, q, 4:8].rearrange("p (i k) -> p i k", k=2)
                turned = ups[:, q + 1, 4:8].rearrange("p (i k) -> p i k", k=2)
                dve.memset(ups[:, q + 1, 0:4], 0.0).then_inc(sem("ups_rot"), 1)
                dve.tensor_scalar(turned[:, :, 0], plain[:, :, 1], -1.0, None, ALU.mult).then_inc(sem("ups_rot"), 1)
                dve.tensor_copy(turned[:, :, 1], plain[:, :, 0]).then_inc(sem("ups_rot"), 1)
            dve.memset(ups2[:, :, :, :], 0.0).then_inc(sem("ups_rot"), 1)
            dve.wait_ge(sem("ups_rot"), 7)
            for e in range(2):
                half = slice(LAT * e, LAT * e + LAT)
                dve.tensor_copy(ups2[half, e, :, :], ups[half, :, :]).then_inc(sem("ups_rot"), 1)
            norm("ln0", 1, 0, x_tile, XN)
            norm("ln0", 1, 1, x_tile, XN)
            dve.wait_ge(sem("x_in1"), 16)
            moments("ln0", 1, 2, x_tile)
            moments("ln0", 1, 3, x_tile)
            norm("ln0", 1, 2, x_tile, XN)
            norm("ln0", 1, 3, x_tile, XN)
            dve.wait_ge(sem("folded_ps"), 1)
            for side in range(2):
                dve.tensor_copy(wqk[0][:, side].rearrange("p r (h d) -> p r h d", h=H),
                                bank(side)[:, 0:256].rearrange("p (h r d) -> p r h d", h=H, r=2))\
                    .then_inc(sem("folded"), 1)
            dve.tensor_copy(wv[0][:, :], bank(2)[:, 0:P]).then_inc(sem("folded"), 1)
            dve.wait_ge(sem("rope_in"), 16)
            rotate(0)
            rotate(1)
            last_part(0, 0)
            last_part(0, 1)
            rotate(2)
            rotate(3)

            def beside_first0(jj):
                for w, at in ((2, LAST_PARTS_AT[0]), (3, LAST_PARTS_AT[1])):
                    if jj == at:
                        last_part(0, w)

            attend(0, PLANS[0], beside_first0)
            for c in (2, 3):
                branch_moments(0, c)
            residual("post0", 2)
            residual("post0", 3)
            second_moments("post0", 2)
            second_moments("post0", 3)
            def route_step(c, j):
                step, k, t = sem("route"), 9 * c, slice(TC * c, TC * c + TC)
                sc, bi = esc[:, t], ebi[:, t]
                mine = bi.unsqueeze(3).to_broadcast([P, TC, E, E])
                theirs = bi.unsqueeze(2).to_broadcast([P, TC, E, E])
                x0, x1 = cmp[:, 0, t], cmp[:, 1, t]
                bias = ebias[:, :].unsqueeze(1).to_broadcast([P, TC, E])
                before = before8[:, :, :].unsqueeze(1).to_broadcast([P, TC, E, E])
                if j == 0:
                    dve.wait_ge(sem("gate_exp"), c + 1)
                    dve.tensor_scalar(sc, sc, 1.0, None, ALU.add).then_inc(step, 1)
                elif j == 1:
                    dve.wait_ge(step, k + 1)
                    dve.reciprocal(sc, sc).then_inc(step, 1)
                elif j == 2:
                    dve.wait_ge(step, k + 2)
                    dve.tensor_tensor(bi, sc, bias, ALU.add).then_inc(step, 1)
                elif j == 3:
                    dve.wait_ge(step, k + 3)
                    dve.tensor_tensor(x1, theirs, mine, ALU.is_equal).then_inc(step, 1)
                    dve.tensor_tensor(x0, theirs, mine, ALU.is_gt).then_inc(step, 1)
                elif j == 4:
                    dve.wait_ge(step, k + 4)
                    dve.tensor_tensor(x1, x1, before, ALU.mult).then_inc(step, 1)
                elif j == 5:
                    dve.wait_ge(step, k + 6)
                    dve.tensor_tensor(x0, x0, x1, ALU.add).then_inc(step, 1)
                elif j == 6:
                    dve.wait_ge(step, k + 7)
                    dve.tensor_reduce(erank[:, t], x0, AX.X, ALU.add).then_inc(step, 1)
                elif j == 7:
                    dve.wait_ge(step, k + 8)
                    dve.tensor_scalar(chosen[:, t], erank[:, t], 1.5, None, ALU.is_lt).then_inc(step, 1)
                elif j == 8:
                    dve.wait_ge(step, k + 9)
                    dve.tensor_tensor(sc, sc, chosen[:, t], ALU.mult).then_inc(sem("chosen"), 1)

            for j in range(ROUTE_STEPS):
                route_step(0, j)

            def route_beside(i, place):
                for c, at in ROUTE_AT.items():
                    j = 2 * (i - at) + place
                    if 0 <= j < ROUTE_STEPS:
                        route_step(c, j)

            def scale_in(u):
                c, e = divmod(u, E)
                dve.wait_ge(sem("score_ps"), u + 1)
                if u >= SLOTS:
                    dve.wait_ge(sem("unit_ps"), through("expert", u - SLOTS))
                dve.tensor_tensor(xsT[u % SLOTS], XNT[:, CW * c:CW * c + CW], bank(SPREAD_BANK[u % 2]), ALU.mult)\
                    .then_inc(sem("xsT"), 1)

            def square(u):
                dve.wait_ge(sem("unit_read"), through("expert", u))
                if u >= SLOTS:
                    dve.wait_ge(sem("down_ps"), u - SLOTS + 1)
                dve.tensor_tensor(hsq[u % SLOTS], hrelu[u % SLOTS], hrelu[u % SLOTS], ALU.mult)\
                    .then_inc(sem("hsq"), 1)

            def round_out(u):
                dve.wait_ge(sem("down_ps"), u + 1)
                if u >= SLOTS:
                    dve.wait_ge(sem("eacc"), u - SLOTS + 1)
                dve.tensor_copy(eout[u % SLOTS], bank(5 + u % 2)).then_inc(sem("eout_dve"), 1)

            def post1(what, half, c):
                src = x_tile if half else (lambda c, t: ps[:, 7, P * t:P * t + P]) if c == 3 else yb_tile
                if what == "moments":
                    if half:
                        dve.wait_ge(sem("x_added"), adds_before("post1", c) + 1)
                    elif c == 3:
                        dve.wait_ge(sem("back_ps3"), 1)
                    else:
                        dve.wait_ge(sem("unit_read"), through("back", c))
                    moments("post1", half, c, src)
                elif what == "norm":
                    norm("post1", half, c, src, XN if half else TMP)
                elif what == "rest":
                    dve.wait_ge(sem("part0_1"), c + 1)
                    dve.tensor_tensor(rest[:, c, :], full[:, c, :], parts[4 + c][:, 0, :], ALU.subtract)\
                        .then_inc(sem("rest_1"), 1)
                else:
                    last_part(1, c)

            for i in range(-AHEAD, len(UNITS) + ADD):
                if expert(i + AHEAD) is not None:
                    scale_in(expert(i + AHEAD))
                route_beside(i, 0)
                if expert(i - 1) is not None:
                    square(expert(i - 1))
                route_beside(i, 1)
                u = expert(i - ROUND)
                if u is not None and rounded_by_dve(u):
                    round_out(u)
                if i in BESIDE_EXPERTS:
                    post1(*BESIDE_EXPERTS[i])

            def beside_first(jj):
                if jj == BESIDE_FIRST["moments0"]:
                    post1("moments", 0, 3)
                if jj == BESIDE_FIRST["norm0"]:
                    post1("norm", 0, 3)
                if jj == BESIDE_FIRST["moments1"]:
                    post1("moments", 1, 2)
                    post1("moments", 1, 3)
                if jj == BESIDE_FIRST["norm1"]:
                    post1("norm", 1, 2)
                    post1("norm", 1, 3)
                for w in (2, 3):
                    if jj == BESIDE_FIRST[f"part{w}"]:
                        last_part(1, w)

            attend(1, PLANS[1], beside_first)
            def post2(step):
                if step == "moments":
                    branch_moments(1, 2)
                    branch_moments(1, 3)
                elif step == "residual":
                    residual("post2", 2)
                    residual("post2", 3)
                    second_moments("post2", 2)
                    second_moments("post2", 3)
                else:
                    router_scores(dve, sem, FF, XN, 2)
                    router_scores(dve, sem, FF, XN, 3)

            dve_ffn(dve, sem, bank, ps, FF, XN, YB, post2)
            post("post3", "ffn_out", yb_tile, False)

        @block.tensor
        def _(pe):
            def turn_xn(at, c):
                for t in range(TC):
                    ins = pe.transpose(ps[:, at, P * t:P * t + P], XN[:, TC * c + t, :], ident[:, :])
                return ins

            def transpose_xn(name, banks, chunks=range(CHUNKS)):
                for c in chunks:
                    pe.wait_ge(sem("normed"), TC * (norms_before(name, 1, c) + 1))
                    turn_xn(banks[c], c).then_inc(sem("xnT_ps"), 1)

            def q_or_k(L, w, at):
                b, side = divmod(w, 2)
                for r in range(2 - L):
                    for c in range(2):
                        ins = pe.matmul(ps[:, at + 2 * r + c, :], wqk[L][:, side, r, :],
                                        XNT[:, T * b + CW * c:T * b + CW * c + CW], start=True, stop=True)
                return ins

            def values(L, b, at, tiles=range(KT)):
                for k in tiles:
                    o = bank(at, 1 if len(tiles) < KT else 2)[:, P * (k - tiles[0]):P * (k - tiles[0]) + P]
                    ins = pe.matmul(o, XNT[:, T * b + P * k:T * b + P * k + P], wv[L][:, :],
                                    start=True, stop=not L)
                    if L:
                        ins = pe.matmul(o, ones_row[:, :], bvo[:, 0, :], start=False, stop=True)
                return ins

            def attend(L, plan, beside_first):
                first, second, pv, small = (sem(f"{k}{L}") for k in ("first_ps", "second_ps", "pv", "small_ps"))
                exps, maxed, small_done = sem(f"exp{L}"), sem(f"rowmax{L}"), sem(f"small_done{L}")

                def first_job(n, par, rounds, jj, prologue=False):
                    qt, j = plan.jobs[jj]
                    pair, e = divmod(j, 2)
                    if jj == 0:
                        pe.wait_ge(sem(f"first_in{L}{par}"), 64 * (rounds + 1))
                    before, at = plan.maxima_before(jj), plan.first_bank(jj)
                    if not (prologue and before <= 0):
                        pe.wait_ge(maxed, JOBS * n + before)
                    keys = plan.keys(qt)
                    for k0 in range(0, keys, 512):
                        k1 = min(keys, k0 + 512)
                        masked = plan.causal and k1 == keys
                        ins = pe.matmul(ps[:, at + k0 // 512, 0:k1 - k0],
                                        SQ[:, par, j, P * qt:P * qt + P], SK[:, par, pair, k0:k1],
                                        start=True, stop=not masked)
                        if masked:
                            ins = pe.matmul(ps[:, at + k0 // 512, k1 - k0 - P:k1 - k0],
                                            ident_bf[:, :], mask_bf[:, 0, :], start=False, stop=True)
                    ins.then_inc(first, 1)

                def scores(n, par, rounds, s, j, begin, last):
                    qh, kt = plan.steps[s]
                    pair, e = divmod(j, 2)
                    c0 = plan.skipped(qh, kt)
                    if s == 0 and j == 0:
                        pe.wait_ge(sem(f"second_in{L}{par}"), 80 * (rounds + 1))
                    if kt == 0 and j == 0:
                        pe.wait_ge(sem(f"max_in{L}{qh}"), 32 * (n + 1))
                    if last and s == 0:
                        if j == 0:
                            pe.wait_ge(maxed, JOBS * NG)
                    elif last:
                        pe.wait_ge(exps, (plan.n * n + s - 1) * G + j + 1)
                    elif not (begin and s == 0 and j < 2):
                        pe.wait_ge(exps, (plan.n * n + s) * G + j - 1)
                    o = second_bank(j, last)
                    diagonal = plan.diagonal(qh, kt)
                    ins = pe.matmul(ps[:, o, c0:512], TK[:, par, pair, P * kt:P * kt + P],
                                    TQ[:, par, j, 512 * qh + c0:512 * qh + 512],
                                    start=True, stop=not diagonal)
                    if diagonal:
                        ins = pe.matmul(ps[:, o, c0:c0 + P], ident_bf[:, :], mask_bf[:, 1, :],
                                        start=False, stop=True)
                    ins.then_inc(second, 1)

                def times_values(n, par, s, begin):
                    qh, kt = plan.steps[s]
                    c0 = plan.skipped(qh, kt)
                    pe.wait_ge(exps, (plan.n * n + s + 1) * G)
                    if kt == 0 and not (begin and qh == 0):
                        pe.wait_ge(sem(f"out_copied{L}"), 2 * n + qh)
                    end = s == plan.n - 1 or plan.steps[s + 1][0] != qh
                    for j in range(G):
                        ins = pe.matmul(ps[32 * j:32 * j + VW, 6, c0:512], VS[:, par, kt, j, :],
                                        probs[:, s % 2, j, c0:512], start=(kt == 0), stop=end)
                    ins.then_inc(pv, 1)

                def max_rows(turns, n, par, qh, begin=False):
                    if not begin:
                        pe.wait_ge(small_done, turns)
                    pe.wait_ge(sem(f"max3_{L}"), 8 * n + 4 * qh + 4)
                    pe.transpose(bank(7).bitcast(BF16)[:, 0:P], nmax3_cols[:, par, qh, :], ident_bf[:, :])\
                        .then_inc(small, 1)

                def out_rows(turns, n, qh):
                    pe.wait_ge(small_done, turns)
                    pe.wait_ge(sem(f"out_copied{L}"), 2 * n + qh + 1)
                    for q in range(4):
                        ins = pe.transpose(ps[:, 7, P * q:P * q + P], OS[:, qh, P * q:P * q + P], ident[:, :])
                    ins.then_inc(small, 1)

                for jj in range(JOBS):
                    beside_first(jj)
                    first_job(0, 0, 0, jj, prologue=True)
                    if jj == EARLY_MAX:
                        for name, value in (qk_full(L, 3), values_done(L, 1)):
                            pe.wait_ge(sem(name), value)
                        max_rows(0, 0, 0, 0, begin=True)

                def period(n, par, rounds, begin, last):
                    for s in range(plan.n):
                        if last:
                            beside_last(L, s)
                        beside = [] if last else plan.beside[s]
                        at = 0
                        for i, piece in enumerate(("s0", "s1", "s2", "s3", "values") if last else
                                                  ("s0", "s1", "values", "s2", "s3")):
                            if piece != "values":
                                scores(n, par, rounds, s, int(piece[1]), begin, last)
                            elif s:
                                times_values(n, par, s - 1, begin)
                            elif not begin:
                                times_values(n - 1, 1 - par, plan.n - 1, False)
                            upto = len(beside) * plan.done_by[i] // 4
                            for jj in beside[at:upto]:
                                first_job(n + 1, 1 - par, rounds + par, jj)
                            at = upto
                        kind = plan.small.get(s)
                        if kind == "max1":
                            max_rows(turn(kind, n, begin), n, par, 1)
                        if kind == "max0" and not last:
                            max_rows(turn(kind, n, begin), n + 1, 1 - par, 0)
                        if kind == "out0":
                            out_rows(turn(kind, n, begin), n, 0)
                        if kind == "out1" and not begin:
                            out_rows(turn(kind, n, begin), n - 1, 1)

                periods(pe, period)
                times_values(NG - 1, 1, plan.n - 1, False)
                out_rows(turn("max0", NG - 1), NG - 1, 1)

            def turn_y(L, c):
                at = 4 + c if c < 2 else c
                for t in range(TC):
                    b, k = divmod(TC * c + t, KT)
                    ins = pe.transpose(ps[:, at, P * t:P * t + P],
                                       Y[:, k, G * b:G * b + G, :].rearrange("p g d -> p (g d)"), ident[:, :])
                ins.then_inc(sem(f"yT_ps{L}"), 1)

            def project_out(L, c):
                pe.wait_ge(sem(f"yT{L}"), c + 1)
                for t in range(TC):
                    o = ps[:, 4 + c, P * t:P * t + P]
                    ins = pe.matmul(o, YT[:, CW * c + P * t:CW * c + P * t + P], wo[L][:, :],
                                    start=True, stop=not L)
                    if L:
                        ins = pe.matmul(o, ones_row[:, :], bvo[:, 1, :], start=False, stop=True)
                ins.then_inc(sem(f"branch_ps{L}"), 1)

            def beside_last(L, s):
                if s == TURN_AT:
                    turn_y(L, 0)
                    turn_y(L, 1)
                if s == BRANCH_AT:
                    pe.wait_ge(sem("later_in"), 16 * LATER)
                    project_out(L, 0)
                    project_out(L, 1)

            pe.wait_ge(sem("const_in"), 32)
            transpose_xn("ln0", LN0_BANK, range(2))
            pe.wait_ge(sem("ups_in"), 48)
            pe.wait_ge(sem("down_in"), 16)
            pe.wait_ge(sem("ups_rot"), 9)
            for side in range(2):
                for h in range(H // 2):
                    pe.matmul(ps[:, side, 32 * h:32 * h + 32], down[:, side, h, :],
                              ups2[:, :, 2 * side:2 * side + 2, :], start=True, stop=True)
            for h in range(H // 2):
                ins = pe.matmul(ps[:, 2, 2 * DH * h:2 * DH * h + 2 * DH], down[:, 2, h, :], ups2[:, :, 4, :],
                                start=True, stop=True)
            ins.then_inc(sem("folded_ps"), 1)
            pe.wait_ge(sem("folded"), 3)
            pe.wait_ge(sem("xnT"), 2)
            q_or_k(0, 0, QK_BANK[0][0]).then_inc(sem("qk_ps0"), 1)
            q_or_k(0, 1, QK_BANK[0][1]).then_inc(sem("qk_ps0"), 1)
            pe.wait_ge(sem("qk_full0"), 1)
            values(0, 0, V_BANK[0][0]).then_inc(sem("v_ps0"), 1)
            transpose_xn("ln0", LN0_BANK, range(2, CHUNKS))
            pe.wait_ge(sem("xnT"), CHUNKS)
            pe.wait_ge(sem("qk_full0"), 2)
            q_or_k(0, 2, QK_BANK[0][2]).then_inc(sem("qk_ps0"), 1)
            pe.wait_ge(sem("v_done0"), 4)
            q_or_k(0, 3, QK_BANK[0][3]).then_inc(sem("qk_ps0"), 1)
            pe.wait_ge(sem("qk_full0"), 3)
            values(0, 1, V_BANK[0][1]).then_inc(sem("v_ps0"), 1)
            pe.wait_ge(sem("act_const"), 2)
            pe.wait_ge(sem("qk_full0"), 4)
            attend(0, PLANS[0], lambda jj: None)
            pe.wait_ge(sem("small_done0"), 4 * NG)
            turn_y(0, 2)
            turn_y(0, 3)
            project_out(0, 2)
            project_out(0, 3)
            def gate(c):
                pe.wait_ge(sem("xnT"), turned_before("post0", c + 1))
                for t in range(TC):
                    i = TC * c + t
                    ins = pe.matmul(ps[:, 4 + c, E * t:E * t + E], XNT[:, P * i:P * i + P], gateT[:, :],
                                    start=True, stop=True)
                ins.then_inc(sem("gate_ps"), 1)

            for c in range(CHUNKS):
                transpose_xn("post0", range(CHUNKS), [c])
                if c:
                    gate(c - 1)
            gate(CHUNKS - 1)
            pe.wait_ge(sem("moe_bf"), 4)

            def turn_parts(at, c):
                pe.wait_ge(sem("score3"), 5 * c + 5)
                for t in range(TC):
                    ins = pe.transpose(bank(at).bitcast(BF16)[:, P * t:P * t + P], esc3_cols[:, TC * c + t, :],
                                       ident_bf[:, :])
                return ins

            turn_parts(0, 0).then_inc(sem("esc3T_ps"), 1)
            pe.wait_ge(sem("gate_exp"), CHUNKS)

            def spread_score(u):
                c, e = divmod(u, E)
                if u == 0:
                    pe.wait_ge(sem("esc3T"), 1)
                if c and e == 0:
                    pe.wait_ge(sem("unit_read"), through("parts", c))
                if u >= 2:
                    pe.wait_ge(sem("xsT"), u - 1)
                pe.matmul(bank(SPREAD_BANK[u % 2]), pick_bf[:, e:e + 1].to_broadcast([P, P]), esc3T[:, CW * c:CW * c + CW],
                          start=True, stop=True).then_inc(sem("score_ps"), 1)

            def turn_back(at, c):
                for t in range(TC):
                    ins = pe.transpose(ps[:, at, P * t:P * t + P], OS[:, c % 2, P * t:P * t + P], ident[:, :])
                return ins

            def do_unit(v):
                kind, n = UNITS[v]
                if kind == "expert":
                    pe.wait_ge(sem("xsT"), n + 1)
                if kind == "turn":
                    pe.wait_ge(sem("normed"), TC * (norms_before("post1", 1, n) + 1))
                if kind == "q":
                    pe.wait_ge(sem("unit_read"), through("turn", 1))
                if kind == "back":
                    pe.wait_ge(sem("moe_sum"), n + 1)
                for k in range(HALVES[v]):
                    h = halves_before(v) + k
                    at = half_bank(h)
                    if h >= 3:
                        pe.wait_ge(sem("unit_read"), h - 2)
                    if kind == "shared":
                        ins = pe.matmul(ps[0:HH, at, :], supT[:, HH * k:HH * k + HH], XNT[:, CW * n:CW * n + CW],
                                        start=True, stop=True)
                    elif kind == "expert":
                        ins = pe.matmul(ps[0:HH, at, :], wup_bf[:, n % E, HH * k:HH * k + HH], xsT[n % SLOTS],
                                        start=True, stop=True)
                    elif kind == "parts":
                        ins = turn_parts(at, n)
                    elif kind == "turn":
                        ins = turn_xn(at, n)
                    elif kind == "back":
                        ins = turn_back(at, n)
                    elif kind == "v":
                        ins = values(1, 0, at, range(TC * k, TC * k + TC))
                    else:
                        ins = pe.matmul(bank(at), wqk[1][:, n, 0, :], XNT[:, CW * k:CW * k + CW], start=True, stop=True)
                    ins.then_inc(sem("unit_ps"), 1)

            def wait_rounded(u):
                if rounded_by_dve(u):
                    pe.wait_ge(sem("eout_dve"), (u + 1) // 4)
                else:
                    pe.wait_ge(sem("eout_act"), u + 1 - (u + 1) // 4)

            def expert_down(u):
                c, e = divmod(u, E)
                pe.wait_ge(sem("hsq"), u + 1)
                if u >= 2:
                    wait_rounded(u - 2)
                for k in range(2):
                    ins = pe.matmul(bank(5 + u % 2), wdn_bf[:, e, k, :], hsq[u % SLOTS][:, k, :], start=(k == 0),
                                    stop=(k == 1))
                ins.then_inc(sem("down_ps"), 1)

            def add_up(u):
                c, e = divmod(u, E)
                if e == E // 2:
                    pe.wait_ge(sem("shared_sq"), c + 1)
                    for k in range(2):
                        ins = pe.matmul(bank(7), sdnT[:, k, :], hs2[:, k, :], start=False, stop=False)
                    ins.then_inc(sem("shared_ps"), 1)
                wait_rounded(u)
                if e == 0 and c:
                    pe.wait_ge(sem("moe_sum"), c)
                pe.matmul(ps[:, 7, :], ident_bf[:, :], eout[u % SLOTS], start=(e == 0), stop=(e == E - 1))\
                    .then_inc(sem("eacc"), 1)

            for i in range(-AHEAD, len(UNITS) + ADD):
                if 0 <= i < len(UNITS):
                    do_unit(i)
                if expert(i + AHEAD) is not None:
                    spread_score(expert(i + AHEAD))
                if expert(i - DOWN) is not None:
                    expert_down(expert(i - DOWN))
                if expert(i - ADD) is not None:
                    add_up(expert(i - ADD))

            def beside_first(jj):
                if jj == BESIDE_FIRST["turn"]:
                    transpose_xn("post1", TURN_BANK, range(2, CHUNKS))
                if jj == BESIDE_FIRST["q"]:
                    pe.wait_ge(sem("xnT"), turned_before("post1", CHUNKS))
                    q_or_k(1, 2, QK_BANK[1][2]).then_inc(sem("qk_ps1"), 1)
                if jj == BESIDE_FIRST["k"]:
                    q_or_k(1, 3, QK_BANK[1][3]).then_inc(sem("qk_ps1"), 1)
                if jj == BESIDE_FIRST["v"]:
                    pe.wait_ge(sem("qk_full1"), 1)
                    values(1, 1, V_BANK[1][1]).then_inc(sem("v_ps1"), 1)

            pe.wait_ge(sem("moe_sum"), CHUNKS)
            turn_back(7, CHUNKS - 1).then_inc(sem("back_ps3"), 1)
            pe.wait_ge(sem("unit_read"), halves_before(len(UNITS)))
            attend(1, PLANS[1], beside_first)
            pe.wait_ge(sem("small_done1"), 4 * NG)
            turn_y(1, 2)
            turn_y(1, 3)
            spread_row(pe, sem, bank, FF, ident, 0)
            project_out(1, 2)
            project_out(1, 3)
            pe_ffn(pe, sem, bank, ps, FF, XN, ident, ones_bf)


NORMED_BY_ACT = {"post0": 0, "post2": 4, "post3": 8}


def by_act(name, c):
    return name == "post3" or (name in NORMED_BY_ACT and c >= 2)


def act_norms(name, half, c):
    return NORMED_BY_ACT[name] + (c if name == "post3" else 2 * half + c - 2) + 1


QK_BANK = ((0, 4, 4, 0), (None, None, 6, 4))
V_BANK = ((0, 4), (None, 6))
LN0_BANK = (4, 5, 2, 3)
TURN_BANK = (None, None, 4, 5)
POOL_CONSTS = 10
FFN_INPUTS = ("wr", "iota", "offset", "earlier", "tri", "g1", "g2", "qkvT", "woutT", "w1T", "w2T", "w3T",
              "headmask", "mask2")
LATER = 15 + len(FFN_INPUTS)


def ffn_buffers(sb, full, rest, XNT, TMP, YT, arena):
    f = dict(
        wr=sb("wr", [P, C]), iota=sb("iota", [P, P]), offset=sb("offset", [P, TILES]),
        earlier=sb("earlier", [P, TILES]),
        tri=sb("tri", [P, P]), g1=sb("g1", [P, C]), g2=sb("g2", [P, C]), qkvT=sb("qkvT", [C, 3 * C]),
        woutT=sb("woutT", [C, C]), w1T=sb("w1T", [C, FC * P]), w2T=sb("w2T", [C, FC * P]),
        w3T=sb("w3T", [P, FC, C]), headmask=sb("headmask", [P, H]), mask2=sb("mask2", [P, P]),
        score=sb("score", [P, TILES]), count=sb("count", [P, TILES, 3]),
        rank=sb("rank", [P, TILES]), nsel=sb("nsel", [P, TILES]), slot=sb("slot", [P, TILES]),
        ssq=sb("ssq", [P, 2]), small=sb("small", [P, 4]),
        smax=sb("smax", [P, H]), sbias=sb("sbias", [P, H]), sden=sb("sden", [P, H]),
    )
    f = {k: v[:] if len(v.shape) == 1 else v[(slice(None),) * len(v.shape)] for k, v in f.items()}
    for k, name in enumerate(("xs", "h", "hT", "qT", "kT", "v", "o", "oT", "x2", "xp")):
        f[name] = arena[:, P * (8 + k):P * (9 + k)]
    f["pv"] = arena[:, P * 18:P * 22]
    f["ga"], f["gb"] = arena[:, 0:FC * P], arena[:, FC * P:2 * FC * P]
    first = full[:, :, :].rearrange("p a t -> p (a t)").bitcast(BF16).rearrange("p (x t) -> p x t", x=4)
    last = rest[:, 1, :].bitcast(BF16).rearrange("p (x t) -> p x t", x=4)
    f["ahead"] = [first[:, k, P * k:T] if k < 4 else last[:, k - 4, 0:T - P * k] for k in range(KT)]
    f["junk"] = rest[:, 0, :].rearrange("p (x q) -> p x q", q=P)
    f["sel"] = YT[:, :].rearrange("p (t s) -> p t s", t=TILES)
    f["selT"] = XNT[:, :]
    f["s"] = TMP[:, :, :]
    f["qm"] = YT[:, :].rearrange("p (h q) -> p h q", h=H)
    f["pT"] = rest[:, :, :].rearrange("p a t -> p (a t)").rearrange("p (h q) -> p h q", h=H)
    return f


def router_scores(dve, sem, f, XN, c):
    for t in range(TC * c, TC * c + TC):
        dve.wait_ge(sem("normed"), TC * norms_before("post2", 1, c) + t % TC + 1)
        if t >= 2:
            dve.wait_ge(sem("score"), t - 1)
        dve.tensor_tensor_reduce(out=f["junk"][:, t % 2, :], in0=XN[:, t, :], in1=f["wr"], scale=1.0, scalar=0.0,
                                 op0=ALU.mult, op1=ALU.add, accum_out=f["score"][:, t:t + 1])\
            .then_inc(sem("score"), 1)


def dve_ffn(dve, sem, bank, ps, f, XN, YB, post2):
    step = sem("ffn_dve")
    n = [0]

    def link(ins):
        n[0] += 1
        ins.then_inc(step, 1)
        dve.wait_ge(step, n[0])

    post2("moments")
    for b in range(B):
        dve.wait_ge(sem("row_ps"), b + 1)
        row = bank(2 * b, 2)
        for k in range(KT):
            if b == 0 and k == 4:
                post2("residual")
            t = KT * b + k
            mine, cnt, own = f["score"][:, t:t + 1], f["count"], slice(P * k, P * k + P)
            if b:
                dve.wait_ge(sem("summed"), KT - 1)
            dve.tensor_scalar(f["ahead"][k], row[:, P * k:T], mine, None, ALU.is_gt, ALU.add,
                              accum_out=cnt[:, t, 1:2]).then_inc(sem("compared"), 1)
            if t >= 2:
                dve.wait_ge(sem("tied"), t - 1)
            dve.scalar_tensor_tensor(out=f["junk"][:, 2 + t % 2, :], in0=row[:, own], scalar=mine, in1=f["tri"],
                                     op0=ALU.is_equal, op1=ALU.mult, accum_out=cnt[:, t, 2:3])\
                .then_inc(sem("tied"), 1)
        if b == 0:
            post2("scores")
        ts = slice(KT * b, KT * b + KT)
        dve.wait_ge(sem("compared"), KT * (b + 1))
        dve.wait_ge(sem("tied"), KT * (b + 1))
        link(dve.tensor_reduce(f["rank"][:, ts], f["count"][:, ts], AX.X, ALU.add))
        later = slice(KT * b + 1, KT * b + KT)
        dve.wait_ge(sem("summed"), (KT - 1) * (b + 1))
        link(dve.scalar_tensor_tensor(out=f["rank"][:, later], in0=ps[:, 4 + b, 1:KT], scalar=-1.0,
                                      in1=f["rank"][:, later], op0=ALU.mult, op1=ALU.add))
        link(dve.tensor_scalar(f["nsel"][:, ts], f["rank"][:, ts], TOP - 0.5, None, ALU.is_gt))
        link(dve.scalar_tensor_tensor(out=f["slot"][:, ts], in0=f["nsel"][:, ts], scalar=4096.0,
                                      in1=f["rank"][:, ts], op0=ALU.mult, op1=ALU.add))
        link(dve.tensor_tensor(f["slot"][:, ts], f["slot"][:, ts], f["offset"][:, ts], ALU.add))
        dve.tensor_tensor(f["sel"][:, ts], f["iota"].unsqueeze(1).to_broadcast([P, KT, P]),
                          f["slot"][:, ts].unsqueeze(2).to_broadcast([P, KT, P]), ALU.is_equal)\
            .then_inc(sem("sel"), 1)

    def rms(i, src, gain):
        dve.tensor_tensor_reduce(out=f["h"], in0=src, in1=src, scale=1.0, scalar=0.0, op0=ALU.mult,
                                 op1=ALU.add, accum_out=f["ssq"][:, i:i + 1]).then_inc(sem("ssq"), 1)
        dve.wait_ge(sem("rms"), 2 * i + 2)
        dve.scalar_tensor_tensor(out=f["h"], in0=src, scalar=f["small"][:, 2 * i + 1:2 * i + 2], in1=gain,
                                 op0=ALU.mult, op1=ALU.mult).then_inc(sem("rows"), 1)

    dve.wait_ge(sem("gathered"), CHUNKS)
    link(dve.tensor_copy(f["xs"], ps[:, 6, 0:C]))
    rms(0, f["xs"], f["g1"])
    dve.wait_ge(sem("qT"), 1)
    for c in range(4):
        hs = slice(4 * c, 4 * c + 4)
        dve.tensor_tensor(f["qm"][:, hs], f["qT"].unsqueeze(1).to_broadcast([P, 4, P]),
                          f["headmask"][:, hs].unsqueeze(2).to_broadcast([P, 4, P]), ALU.mult)\
            .then_inc(sem("qm"), 1)
    for c in range(4):
        hs = slice(4 * c, 4 * c + 4)
        dve.wait_ge(sem("s_ps"), c + 1)
        link(dve.tensor_tensor(f["s"][:, hs], bank(c).rearrange("p (h k) -> p h k", h=4),
                               f["mask2"].unsqueeze(1).to_broadcast([P, 4, P]), ALU.add))
        link(dve.tensor_reduce(f["smax"][:, hs], f["s"][:, hs], AX.X, ALU.max, negate=True))
        dve.tensor_scalar(f["sbias"][:, hs], f["smax"][:, hs], SCALE, None, ALU.mult).then_inc(sem("s_max"), 1)
    for c in range(4):
        hs = slice(4 * c, 4 * c + 4)
        dve.wait_ge(sem("s_exp"), c + 1)
        link(dve.tensor_reduce(f["sden"][:, hs], f["s"][:, hs], AX.X, ALU.add))
    link(dve.reciprocal(f["sden"], f["sden"]))
    dve.wait_ge(sem("o_ps"), 1)
    dve.tensor_tensor(f["o"].rearrange("p (h d) -> p h d", h=H),
                      ps[:, 0, :].rearrange("p (h v) -> p h v", v=32)[:, :, 0:DH],
                      f["sden"].unsqueeze(2).to_broadcast([P, H, DH]), ALU.mult).then_inc(sem("o"), 1)
    dve.wait_ge(sem("attn_ps"), 1)
    link(dve.tensor_tensor(f["x2"], f["xs"], ps[:, 2, 0:C], ALU.add))
    rms(1, f["x2"], f["g2"])
    dve.wait_ge(sem("ga_exp"), 1)
    link(dve.tensor_scalar(f["ga"], f["ga"], 1.0, None, ALU.add))
    for k in range(FC):
        cols = slice(P * k, P * k + P)
        link(dve.reciprocal(f["ga"][:, cols], f["ga"][:, cols]))
        link(dve.tensor_tensor(f["ga"][:, cols], f["ga"][:, cols], bank(4)[:, cols], ALU.mult))
        dve.tensor_tensor(f["gb"][:, cols], f["ga"][:, cols], bank(5)[:, cols], ALU.mult).then_inc(sem("gb"), 1)
    dve.wait_ge(sem("ff_ps"), 1)
    dve.tensor_tensor(f["xp"], f["x2"], ps[:, 6, 0:C], ALU.add).then_inc(sem("xp"), 1)
    for c in range(CHUNKS):
        dve.wait_ge(sem("back_ps"), c + 1)
        for t in range(TC):
            ins = dve.scalar_tensor_tensor(out=YB[:, TC * c + t, :], in0=XN[:, TC * c + t, :],
                                           scalar=f["nsel"][:, TC * c + t:TC * c + t + 1],
                                           in1=ps[:, c, P * t:P * t + P], op0=ALU.mult, op1=ALU.add)
        ins.then_inc(sem("ffn_out"), 1)


def act_ffn(act, sem, bank, ps, f):
    def copy(dst, src, wait, done, func=ACT.Copy, scale=1.0, count=1):
        act.wait_ge(sem(wait), count)
        act.activation(dst, src, func, scale=scale).then_inc(sem(done), 1)

    for c in range(CHUNKS):
        act.wait_ge(sem("selT_ps"), c + 1)
        act.activation(f["selT"][:, CW * c:CW * c + CW], bank(c), ACT.Copy).then_inc(sem("selT"), 1)
    copy(f["hT"], ps[:, 7, 0:P], "hT_ps", "hT")
    copy(f["qT"], ps[:, 5, 0:P], "qkv_ps", "qT")
    copy(f["kT"], ps[:, 5, P:2 * P], "qkv_ps", "kT")
    copy(f["v"], ps[:, 5, 2 * P:3 * P], "qkv_ps", "v")

    def exponentials(c):
        act.wait_ge(sem("s_max"), c + 1)
        for h in range(4 * c, 4 * c + 4):
            ins = act.activation(f["s"][:, h, :], f["s"][:, h, :], ACT.Exp, bias=f["sbias"][:, h:h + 1], scale=SCALE)
        ins.then_inc(sem("s_exp"), 1)

    def copy_pT(c):
        act.wait_ge(sem("pT_ps"), c + 1)
        act.activation(f["pT"][:, 4 * c:4 * c + 4, :], bank(4 + c).rearrange("p (h q) -> p h q", h=4), ACT.Copy)\
            .then_inc(sem("pT"), 1)

    for c in range(4):
        exponentials(c)
        if c:
            copy_pT(c - 1)
    copy_pT(3)
    copy(f["pv"], bank(1), "oT_ps", "oT")
    copy(f["oT"], ps[:, 1, 0:P], "oT_ps", "oT", count=2)
    copy(f["hT"], ps[:, 1, 0:P], "hT_ps", "hT", count=2)
    copy(f["ga"], bank(4)[:, 0:FC * P], "ga_ps", "ga_exp", ACT.Exp, -1.0)


def spread_row(pe, sem, bank, f, ident, b):
    pe.wait_ge(sem("score"), KT * (b + 1))
    for k in range(KT):
        ins = pe.transpose(bank(2 * b, 2)[:, P * k:P * k + P],
                           f["score"][:, KT * b + k:KT * b + k + 1].to_broadcast([P, P]), ident[:, :])
    ins.then_inc(sem("row_ps"), 1)


def pe_ffn(pe, sem, bank, ps, f, XN, ident, ones_bf):
    def gather(c):
        pe.wait_ge(sem("sel"), c // 2 + 1)
        for t in range(TC * c, TC * c + TC):
            ins = pe.matmul(ps[:, 6, 0:C], f["sel"][:, t, :], XN[:, t, :], start=(t == 0), stop=(t == TILES - 1))
        ins.then_inc(sem("gathered"), 1)

    def turn_sel(b):
        for c in (2 * b, 2 * b + 1):
            for t in range(TC):
                ins = pe.transpose(ps[:, c, P * t:P * t + P], f["sel"][:, TC * c + t, :], ident[:, :])
            ins.then_inc(sem("selT_ps"), 1)

    for b in range(B):
        if b:
            spread_row(pe, sem, bank, f, ident, b)
        for j in range(1, KT):
            pe.wait_ge(sem("compared"), KT * b + j)
            for k in range(j):
                ins = pe.matmul(ps[:, 4 + b, j:j + 1], f["ahead"][k][:, P * (j - k):P * (j - k) + P], ones_bf[:, 0:1],
                                start=(k == 0), stop=(k == j - 1))
            ins.then_inc(sem("summed"), 1)
            if b and j in (2, 4):
                gather(j // 2 - 1)
        if b:
            turn_sel(0)
    gather(2)
    gather(3)
    turn_sel(1)
    pe.wait_ge(sem("rows"), 1)
    pe.transpose(ps[:, 7, 0:P], f["h"], ident[:, :]).then_inc(sem("hT_ps"), 1)
    pe.wait_ge(sem("hT"), 1)
    pe.matmul(ps[:, 5, 0:P], f["qkvT"][:, 0:C], f["hT"], start=True, stop=True)
    pe.matmul(ps[:, 5, P:2 * P], f["qkvT"][:, C:2 * C], f["hT"], start=True, stop=True)
    pe.matmul(ps[:, 5, 2 * P:3 * P], f["hT"], f["qkvT"][:, 2 * C:3 * C], start=True, stop=True)\
        .then_inc(sem("qkv_ps"), 1)
    pe.wait_ge(sem("v"), 1)
    pe.wait_ge(sem("selT"), CHUNKS)
    for c in range(4):
        pe.wait_ge(sem("qm"), c + 1)
        for h in range(4 * c, 4 * c + 4):
            ins = pe.matmul(ps[:, c, P * (h % 4):P * (h % 4) + P], f["qm"][:, h, :], f["kT"], start=True, stop=True)
        ins.then_inc(sem("s_ps"), 1)
    for c in range(4):
        pe.wait_ge(sem("s_exp"), c + 1)
        for h in range(4 * c, 4 * c + 4):
            ins = pe.transpose(ps[:, 4 + c, P * (h % 4):P * (h % 4) + P], f["s"][:, h, :], ident[:, :])
        ins.then_inc(sem("pT_ps"), 1)
    for c in range(4):
        pe.wait_ge(sem("pT"), c + 1)
        for j in range(4):
            h = 4 * c + j
            ins = pe.matmul(ps[32 * j:32 * j + DH, 1, P * c:P * c + P], f["v"][:, DH * h:DH * h + DH],
                            f["pT"][:, h, :], start=True, stop=True)
    ins.then_inc(sem("oT_ps"), 1)
    pe.wait_ge(sem("oT"), 1)
    for c in range(4):
        ins = pe.transpose(ps[:, 0, P * c:P * c + P], f["pv"][:, P * c:P * c + P], ident[:, :])
    ins.then_inc(sem("o_ps"), 1)
    pe.wait_ge(sem("o"), 1)
    pe.transpose(ps[:, 1, 0:P], f["o"], ident[:, :]).then_inc(sem("oT_ps"), 1)
    pe.wait_ge(sem("oT"), 2)
    pe.matmul(ps[:, 2, 0:C], f["oT"], f["woutT"], start=True, stop=True).then_inc(sem("attn_ps"), 1)
    pe.wait_ge(sem("rows"), 2)
    pe.transpose(ps[:, 1, 0:P], f["h"], ident[:, :]).then_inc(sem("hT_ps"), 1)
    pe.wait_ge(sem("hT"), 2)
    for k in range(FC):
        pe.matmul(ps[:, 4, P * k:P * k + P], f["w1T"][:, P * k:P * k + P], f["hT"], start=True, stop=True)
    for k in range(FC):
        ins = pe.matmul(ps[:, 5, P * k:P * k + P], f["w2T"][:, P * k:P * k + P], f["hT"], start=True, stop=True)
    ins.then_inc(sem("ga_ps"), 1)
    for k in range(FC):
        pe.wait_ge(sem("gb"), k + 1)
        ins = pe.matmul(ps[:, 6, 0:C], f["gb"][:, P * k:P * k + P], f["w3T"][:, k, :], start=(k == 0),
                        stop=(k == FC - 1))
    ins.then_inc(sem("ff_ps"), 1)
    pe.wait_ge(sem("xp"), 1)
    for c in range(CHUNKS):
        for t in range(TC):
            ins = pe.matmul(ps[:, c, P * t:P * t + P], f["selT"][:, P * (TC * c + t):P * (TC * c + t) + P],
                            f["xp"], start=True, stop=True)
        ins.then_inc(sem("back_ps"), 1)


def layouts(i):
    def c(x):
        return np.ascontiguousarray(x)

    def rows(x):
        return c(np.broadcast_to(x, (P, x.shape[-1])))

    def twice(x):
        return c(np.concatenate([x, x], 0))

    f4 = np.float32
    hd = np.arange(P) % DH
    inv = (1.0 / 10000.0 ** (np.arange(0, 4, 2, dtype=f4) / f4(4))).astype(f4)
    angle = (np.arange(T, dtype=f4)[:, None] * inv[None, :]).astype(f4)
    angle = np.concatenate((angle, angle), -1).astype(np.float64)
    cos, sin = np.ones((P, T), f4), np.zeros((P, T), f4)
    for p in range(P):
        if hd[p] >= 4:
            cos[p], sin[p] = np.cos(angle[:, hd[p] - 4]), np.sin(angle[:, hd[p] - 4])
    k = np.arange(P)
    after = k[None, :] > k[:, None]
    return {
        "x": c(i["L0_attn_x"].reshape(B * T, C)),
        "ident": np.eye(P, dtype=f4),
        "masks": c(np.stack([np.where(after, f4(NEG), f4(0)), np.where(after.T, f4(NEG), f4(0))], 1)),
        "upq": twice(np.concatenate([i["L0_attn_Wq_up_c"], i["L0_attn_Wq_up_e"]], 1)),
        "upk": twice(np.concatenate([i["L0_attn_Wk_up_c"], i["L0_attn_Wk_up_e"]], 1)),
        "upv": twice(i["L0_attn_Wv_up"]),
        "down": c(np.stack([i[f"L0_attn_W{s}_down"].T.reshape(H // 2, P, C).transpose(1, 0, 2) for s in "qkv"], 1)),
        "rope": c(np.stack([cos, sin], 1)),
        "wo0": c(i["L0_attn_Wc"]),
        "gateT": c(i["L0_ffn_gate_w"].T),
        "pick": c((np.arange(P)[:, None] // 3 == np.arange(E)[None, :]).astype(f4)),
        "ebias": rows(i["L0_ffn_expert_bias"]),
        "before8": c(np.broadcast_to((np.arange(E)[None, :] < np.arange(E)[:, None]).astype(f4), (P, E, E))),
        "wupT": c(i["L0_ffn_w_up"].transpose(2, 0, 1).reshape(C, E * HID)),
        "wdnT": c(i["L0_ffn_w_down"].reshape(E, C, 2, HH).transpose(3, 0, 2, 1).reshape(HH, E * 2 * C)),
        "supT": c(i["L0_ffn_shared_w_up"].T),
        "sdnT": c(i["L0_ffn_shared_w_down"].reshape(C, 2, HH).transpose(2, 1, 0)),
        "wq1": c(i["L1_attn_Wq"].T), "wk1": c(i["L1_attn_Wk"].T), "wv1": c(i["L1_attn_Wv"].T),
        "wo1": c(i["L1_attn_Wo"].T),
        "bqk": c(np.stack([i["L1_attn_bq"], i["L1_attn_bk"]], 1)),
        "bvo": c(np.stack([i["L1_attn_bv"], i["L1_attn_bo"]], 0)[None]),
        "wr": rows(i["L1_ffn_w_router"]),
        "iota": c(np.broadcast_to(k.astype(f4), (P, P))),
        "offset": c(np.broadcast_to((np.arange(TILES) // KT * TOP).astype(f4), (P, TILES))),
        "earlier": c(np.broadcast_to((np.arange(TILES) % KT * P).astype(f4), (P, TILES))),
        "tri": c((~after & (k[None, :] != k[:, None])).astype(f4)),
        "g1": rows(i["L1_ffn_g1"]), "g2": rows(i["L1_ffn_g2"]),
        "qkvT": c(i["L1_ffn_W_qkv"].T), "woutT": c(i["L1_ffn_W_out"].T),
        "w1T": c(np.pad(i["L1_ffn_W1"].T, ((0, 0), (0, FC * P - DFF)))),
        "w2T": c(np.pad(i["L1_ffn_W2"].T, ((0, 0), (0, FC * P - DFF)))),
        "w3T": c(np.pad(i["L1_ffn_W3"].T, ((0, FC * P - DFF), (0, 0))).reshape(FC, P, C).transpose(1, 0, 2)),
        "headmask": c((k[:, None] // DH == np.arange(H)[None, :]).astype(f4)),
        "mask2": c(np.where(after | (k[None, :] // TOP != k[:, None] // TOP), f4(NEG), f4(0))),
    }


def kernel(**inputs):
    import concourse.bacc as bacc
    from concourse.bass_utils import run_bass_kernel_spmd

    arrays = layouts({name: np.asarray(v) for name, v in inputs.items()})
    nc = bacc.Bacc("TRN2", target_bir_lowering=False, num_devices=1)
    a = {name: nc.dram_tensor(name + "_in", v.shape, mybir.dt.from_np(v.dtype), kind="ExternalInput").ap()
         for name, v in arrays.items()}
    out = nc.dram_tensor("out", (B * T, C), F32, kind="ExternalOutput").ap()
    build(nc, a, out)
    got = run_bass_kernel_spmd(nc, [{name + "_in": v for name, v in arrays.items()}], core_ids=[0])
    return got.results[0]["out"].reshape(B, T, C)
```
